# Optimizing a Trainium2 kernel written in Bass

```python
import numpy as np
import jax
import jax.numpy as jnp

def _softmax(x, axis=-1):
    return jax.nn.softmax(x, axis=axis)

def _gelu(x):
    return jax.nn.gelu(x, approximate=True)

def _silu(x):
    return jax.nn.silu(x)

def _sigmoid(x):
    return jax.nn.sigmoid(x)

def _layernorm(x, axis=-1, eps=1e-05):
    m = jnp.mean(x, axis=axis, keepdims=True)
    v = jnp.var(x, axis=axis, keepdims=True)
    return (x - m) / jnp.sqrt(v + eps)

def _scatter_add(tgt, idx, src, axis=0):
    return tgt.at[idx].add(src)

def _segment_sum(src, seg, n):
    return jax.ops.segment_sum(src, seg, n)
kernel_name = 'mk_flamingo_gated_d2_seqx_r4_71dd19'

def setup_inputs(seed: int=0):
    np.random.seed(seed)
    _w = jnp.asarray

    def _rec_inputs():
        import jax
        import jax.numpy as jnp
        _rk = jax.random.key(seed)
        x = -0.0002928 + 1 * jax.random.normal(jax.random.fold_in(_rk, 1), (32, 256, 256), jnp.float32)
        _lenS = 256 - jax.random.randint(jax.random.fold_in(_rk, 7), (32,), 0, max(1, 256 // 4) + 1, jnp.int32)
        _lenS2 = 256 - jax.random.randint(jax.random.fold_in(_rk, 8), (32,), 0, max(1, 256 // 4) + 1, jnp.int32)
        _ctx_1024P = jax.random.normal(jax.random.fold_in(_rk, 11), (32, 16, 256), jnp.float32)
        _ctx_1024c = jax.random.dirichlet(jax.random.fold_in(_rk, 511), 0.3 * jnp.ones((16,), jnp.float32), (32, 256))
        _ctx_1024t = jnp.einsum('bsk,bkd->bsd', _ctx_1024c, _ctx_1024P)
        _ctx_1024t = _ctx_1024t * jax.lax.rsqrt(jnp.mean(jnp.square(_ctx_1024t)) + 1e-12) * 0.953939
        ctx_1024 = -1.39393e-06 + 0.999914 * (_ctx_1024t + 0.3 * jax.random.normal(jax.random.fold_in(_rk, 611), (32, 256, 256), jnp.float32))
        _g = jax.random.normal(jax.random.fold_in(_rk, 9001), (2, 2), jnp.float32)
        _g = jnp.sign(_g) * jnp.maximum(jnp.abs(_g), 1.0) + (_g == 0) * 1.0
        g_xattn = _g[0]
        g_ffn = _g[1]
        return (x, ctx_1024, g_xattn, g_ffn)
    x, ctx_1024, g_xattn, g_ffn = _rec_inputs()

    def _L0_xattn_setup():
        import jax, jax.numpy as jnp
        import numpy as np
        D_KEY = 256
        D_VALUE = 256
        N_HEADS = 16
        key = jax.random.key(seed)
        ks = jax.random.split(key, 7)
        B, S = (2, 512)
        scale_q = 1.0 / np.sqrt(D_KEY)
        return {'query': jax.random.normal(ks[0], (B, S, D_KEY), dtype=jnp.float32), 'key': jax.random.normal(ks[1], (B, S, D_KEY), dtype=jnp.float32), 'value': jax.random.normal(ks[2], (B, S, D_VALUE), dtype=jnp.float32), 'wq': jax.random.normal(ks[3], (D_KEY, D_KEY), dtype=jnp.float32) * scale_q, 'wk': jax.random.normal(ks[4], (D_KEY, D_KEY), dtype=jnp.float32) * scale_q, 'wv': jax.random.normal(ks[5], (D_VALUE, D_VALUE), dtype=jnp.float32) * scale_q, 'wo': jax.random.normal(ks[6], (D_KEY, D_VALUE), dtype=jnp.float32) * scale_q}
    _L0_xattn_all = _L0_xattn_setup()
    _L0_xattn_in = {k: v for k, v in _L0_xattn_all.items() if k in ('wq', 'wk', 'wv', 'wo')}
    del _L0_xattn_all

    def _L0_ffn_setup():
        import jax, jax.numpy as jnp
        import numpy as np

        def _bitlinear(x, w_latent):
            scale = jax.lax.stop_gradient(jnp.clip(jnp.mean(jnp.abs(w_latent), axis=1, keepdims=True), 1e-05, None))
            tern = jnp.clip(jnp.round(w_latent / scale), -1.0, 1.0)
            w = w_latent + jax.lax.stop_gradient(tern - w_latent)
            return x @ (w * scale).T
        key = jax.random.key(seed)
        ks = jax.random.split(key, 6)
        dim, hidden, rank = (256, 1024, 16)
        B, S = (4, 1024)
        x = jax.random.normal(ks[0], (B, S, dim), dtype=jnp.float32)
        w_fc = 0.02 * jax.random.normal(ks[1], (hidden, dim), dtype=jnp.float32)
        w_proj = 0.02 * jax.random.normal(ks[2], (dim, hidden), dtype=jnp.float32)
        u = 0.02 * jax.random.normal(ks[3], (hidden, rank), dtype=jnp.float32)
        v = 0.02 * jax.random.normal(ks[4], (rank, dim), dtype=jnp.float32)
        fast_b = jax.random.normal(ks[5], (rank, rank), dtype=jnp.float32)
        gate = jnp.float32(0.05)
        return {'x': x, 'fast_b': fast_b, 'w_fc': w_fc, 'w_proj': w_proj, 'u': u, 'v': v, 'gate': gate}
    _L0_ffn_all = _L0_ffn_setup()
    _L0_ffn_in = {k: v for k, v in _L0_ffn_all.items() if k in ('fast_b', 'w_fc', 'w_proj', 'u', 'v', 'gate')}
    del _L0_ffn_all

    def _L1_xattn_setup():
        import jax, jax.numpy as jnp
        import numpy as np
        from jax import lax
        BIG = jnp.float32(1e+30)

        def _pairwise_euclidean(a, b):
            aa = jnp.sum(a * a, axis=-1)[:, None]
            bb = jnp.sum(b * b, axis=-1)[None, :]
            ab = a @ b.T
            return jnp.sqrt(jnp.maximum(aa + bb - 2.0 * ab, 0.0))

        def _dtw_cost(D):
            row0 = jnp.cumsum(D[0])

            def row_step(prev_row, d_row):
                first = d_row[0] + prev_row[0]

                def col_step(left, inp):
                    d_ij, up, diag = inp
                    r = d_ij + jnp.minimum(jnp.minimum(up, left), diag)
                    return (r, r)
                _, rest = lax.scan(col_step, first, (d_row[1:], prev_row[1:], prev_row[:-1]))
                row = jnp.concatenate([first[None], rest])
                return (row, row)
            _, rows = lax.scan(row_step, row0, D[1:])
            return jnp.concatenate([row0[None], rows], axis=0)

        def _backtrack(R, T1, T2):
            L = T1 + T2 - 1

            def step(carry, _):
                i, j, done = carry
                valid = jnp.logical_not(done)
                cd = jnp.where((i > 0) & (j > 0), R[jnp.maximum(i - 1, 0), jnp.maximum(j - 1, 0)], BIG)
                cu = jnp.where(i > 0, R[jnp.maximum(i - 1, 0), j], BIG)
                cl = jnp.where(j > 0, R[i, jnp.maximum(j - 1, 0)], BIG)
                choice = jnp.argmin(jnp.stack([cd, cu, cl]))
                ni = jnp.where(choice <= 1, i - 1, i)
                nj = jnp.where((choice == 0) | (choice == 2), j - 1, j)
                at_origin = (i == 0) & (j == 0)
                ni = jnp.where(at_origin, 0, ni)
                nj = jnp.where(at_origin, 0, nj)
                return ((ni, nj, done | at_origin), (i, j, valid))
            init = (jnp.int32(T1 - 1), jnp.int32(T2 - 1), jnp.bool_(False))
            _, (i_idx, j_idx, valid) = lax.scan(step, init, None, length=L)
            return (i_idx, j_idx, valid)

        def _align_one(small, large):
            T_small, d = small.shape
            T_large = large.shape[0]
            D = _pairwise_euclidean(small, large)
            R = _dtw_cost(D)
            i_idx, j_idx, valid = _backtrack(R, T_small, T_large)
            contrib = small[i_idx] * valid[:, None].astype(small.dtype)
            expanded = jnp.zeros((T_large, d), dtype=small.dtype).at[j_idx].add(contrib)
            return expanded
        key = jax.random.key(seed)
        k1, k2 = jax.random.split(key)
        teacher = jax.random.normal(k1, (16, 100, 256), dtype=jnp.float32)
        student = jax.random.normal(k2, (16, 150, 256), dtype=jnp.float32)
        return {'teacher_features': teacher, 'student_features': student}
    _L1_xattn_all = _L1_xattn_setup()
    _L1_xattn_in = {k: v for k, v in _L1_xattn_all.items() if k in ()}
    del _L1_xattn_all

    def _L1_ffn_setup():
        import jax, jax.numpy as jnp
        import numpy as np
        EPS = 1e-05

        def rmsnorm(x):
            return x * jax.lax.rsqrt(jnp.mean(x * x, axis=-1, keepdims=True) + EPS)

        def act_quant(x):
            scale = 127.0 / jnp.clip(jnp.max(jnp.abs(x), axis=-1, keepdims=True), 1e-05)
            q = jnp.clip(jnp.round(x * scale), -128.0, 127.0) / scale
            return x + jax.lax.stop_gradient(q - x)

        def weight_quant(w):
            scale = 1.0 / jnp.clip(jnp.mean(jnp.abs(w)), 1e-05)
            q = jnp.clip(jnp.round(w * scale), -1.0, 1.0) / scale
            return w + jax.lax.stop_gradient(q - w)

        def bitlinear(x, w, b):
            xq = act_quant(rmsnorm(x))
            wq = weight_quant(w)
            return jnp.einsum('bsd,fd->bsf', xq, wq) + b
        key = jax.random.key(seed)
        k0, k1, k2 = jax.random.split(key, 3)
        B, S, D, F = (2, 2048, 256, 1024)
        x = jax.random.normal(k0, (B, S, D), dtype=jnp.float32)
        w1 = jax.random.normal(k1, (F, D), dtype=jnp.float32) * (1.0 / np.sqrt(D))
        b1 = jnp.zeros((F,), dtype=jnp.float32)
        w2 = jax.random.normal(k2, (D, F), dtype=jnp.float32) * (1.0 / np.sqrt(F))
        b2 = jnp.zeros((D,), dtype=jnp.float32)
        return {'x': x, 'w1': w1, 'b1': b1, 'w2': w2, 'b2': b2}
    _L1_ffn_all = _L1_ffn_setup()
    _L1_ffn_in = {k: v for k, v in _L1_ffn_all.items() if k in ('w1', 'b1', 'w2', 'b2')}
    del _L1_ffn_all
    return {'x': x, 'ctx_1024': ctx_1024, 'g_xattn': g_xattn, 'g_ffn': g_ffn, 'L0_xattn_wq': _L0_xattn_in['wq'], 'L0_xattn_wk': _L0_xattn_in['wk'], 'L0_xattn_wv': _L0_xattn_in['wv'], 'L0_xattn_wo': _L0_xattn_in['wo'], 'L0_ffn_fast_b': _L0_ffn_in['fast_b'], 'L0_ffn_w_fc': _L0_ffn_in['w_fc'], 'L0_ffn_w_proj': _L0_ffn_in['w_proj'], 'L0_ffn_u': _L0_ffn_in['u'], 'L0_ffn_v': _L0_ffn_in['v'], 'L0_ffn_gate': _L0_ffn_in['gate'], 'L1_ffn_w1': _L1_ffn_in['w1'], 'L1_ffn_b1': _L1_ffn_in['b1'], 'L1_ffn_w2': _L1_ffn_in['w2'], 'L1_ffn_b2': _L1_ffn_in['b2']}

def reference(x, ctx_1024, g_xattn, g_ffn, L0_xattn_wq, L0_xattn_wk, L0_xattn_wv, L0_xattn_wo, L0_ffn_fast_b, L0_ffn_w_fc, L0_ffn_w_proj, L0_ffn_u, L0_ffn_v, L0_ffn_gate, L1_ffn_w1, L1_ffn_b1, L1_ffn_w2, L1_ffn_b2):
    import jax
    import jax.numpy as jnp

    def _L0_xattn_ref(query, key, value, wq, wk, wv, wo):
        import jax, jax.numpy as jnp
        import numpy as np
        D_KEY = 256
        D_VALUE = 256
        N_HEADS = 16
        B, S, d_key = query.shape
        d_value = value.shape[-1]
        H = N_HEADS
        dk_h = d_key // H
        dv_h = d_value // H
        scale = jnp.sqrt(jnp.asarray(d_key, query.dtype))
        q = (query @ wq.T).reshape(B, S, H, dk_h).transpose(0, 2, 1, 3)
        k = (key @ wk.T).reshape(B, S, H, dk_h).transpose(0, 2, 1, 3)
        v = (value @ wv.T).reshape(B, S, H, dv_h).transpose(0, 2, 1, 3)
        scores = jnp.einsum('bhqd,bhkd->bhqk', q, k) / scale
        attn = jax.nn.softmax(scores, axis=-1)
        out = jnp.einsum('bhqk,bhkd->bhqd', attn, v)
        out = out.transpose(0, 2, 1, 3).reshape(B, S, d_value)
        return out @ wo.T

    def _L0_ffn_ref(x, fast_b, w_fc, w_proj, u, v, gate):
        import jax, jax.numpy as jnp
        import numpy as np

        def _bitlinear(x, w_latent):
            scale = jax.lax.stop_gradient(jnp.clip(jnp.mean(jnp.abs(w_latent), axis=1, keepdims=True), 1e-05, None))
            tern = jnp.clip(jnp.round(w_latent / scale), -1.0, 1.0)
            w = w_latent + jax.lax.stop_gradient(tern - w_latent)
            return x @ (w * scale).T
        h = _bitlinear(x, w_fc) + gate * (x @ v.T @ fast_b.T @ u.T)
        r = jnp.maximum(h, 0.0)
        return _bitlinear(r * r, w_proj)

    def _L1_xattn_ref(teacher_features, student_features):
        import jax, jax.numpy as jnp
        import numpy as np
        from jax import lax
        BIG = jnp.float32(1e+30)

        def _pairwise_euclidean(a, b):
            aa = jnp.sum(a * a, axis=-1)[:, None]
            bb = jnp.sum(b * b, axis=-1)[None, :]
            ab = a @ b.T
            return jnp.sqrt(jnp.maximum(aa + bb - 2.0 * ab, 0.0))

        def _dtw_cost(D):
            row0 = jnp.cumsum(D[0])

            def row_step(prev_row, d_row):
                first = d_row[0] + prev_row[0]

                def col_step(left, inp):
                    d_ij, up, diag = inp
                    r = d_ij + jnp.minimum(jnp.minimum(up, left), diag)
                    return (r, r)
                _, rest = lax.scan(col_step, first, (d_row[1:], prev_row[1:], prev_row[:-1]))
                row = jnp.concatenate([first[None], rest])
                return (row, row)
            _, rows = lax.scan(row_step, row0, D[1:])
            return jnp.concatenate([row0[None], rows], axis=0)

        def _backtrack(R, T1, T2):
            L = T1 + T2 - 1

            def step(carry, _):
                i, j, done = carry
                valid = jnp.logical_not(done)
                cd = jnp.where((i > 0) & (j > 0), R[jnp.maximum(i - 1, 0), jnp.maximum(j - 1, 0)], BIG)
                cu = jnp.where(i > 0, R[jnp.maximum(i - 1, 0), j], BIG)
                cl = jnp.where(j > 0, R[i, jnp.maximum(j - 1, 0)], BIG)
                choice = jnp.argmin(jnp.stack([cd, cu, cl]))
                ni = jnp.where(choice <= 1, i - 1, i)
                nj = jnp.where((choice == 0) | (choice == 2), j - 1, j)
                at_origin = (i == 0) & (j == 0)
                ni = jnp.where(at_origin, 0, ni)
                nj = jnp.where(at_origin, 0, nj)
                return ((ni, nj, done | at_origin), (i, j, valid))
            init = (jnp.int32(T1 - 1), jnp.int32(T2 - 1), jnp.bool_(False))
            _, (i_idx, j_idx, valid) = lax.scan(step, init, None, length=L)
            return (i_idx, j_idx, valid)

        def _align_one(small, large):
            T_small, d = small.shape
            T_large = large.shape[0]
            D = _pairwise_euclidean(small, large)
            R = _dtw_cost(D)
            i_idx, j_idx, valid = _backtrack(R, T_small, T_large)
            contrib = small[i_idx] * valid[:, None].astype(small.dtype)
            expanded = jnp.zeros((T_large, d), dtype=small.dtype).at[j_idx].add(contrib)
            return expanded
        return jax.vmap(_align_one)(teacher_features, student_features)

    def _L1_ffn_ref(x, w1, b1, w2, b2):
        import jax, jax.numpy as jnp
        import numpy as np
        EPS = 1e-05

        def rmsnorm(x):
            return x * jax.lax.rsqrt(jnp.mean(x * x, axis=-1, keepdims=True) + EPS)

        def act_quant(x):
            scale = 127.0 / jnp.clip(jnp.max(jnp.abs(x), axis=-1, keepdims=True), 1e-05)
            q = jnp.clip(jnp.round(x * scale), -128.0, 127.0) / scale
            return x + jax.lax.stop_gradient(q - x)

        def weight_quant(w):
            scale = 1.0 / jnp.clip(jnp.mean(jnp.abs(w)), 1e-05)
            q = jnp.clip(jnp.round(w * scale), -1.0, 1.0) / scale
            return w + jax.lax.stop_gradient(q - w)

        def bitlinear(x, w, b):
            xq = act_quant(rmsnorm(x))
            wq = weight_quant(w)
            return jnp.einsum('bsd,fd->bsf', xq, wq) + b
        h = bitlinear(x, w1, b1)
        h = jax.nn.gelu(h, approximate=False)
        return bitlinear(h, w2, b2)
    x = x + jnp.tanh(g_xattn[0]) * _L0_xattn_ref(_layernorm(x, axis=-1), ctx_1024, ctx_1024, L0_xattn_wq, L0_xattn_wk, L0_xattn_wv, L0_xattn_wo)
    x = x + jnp.tanh(g_ffn[0]) * _L0_ffn_ref(_layernorm(x, axis=-1), L0_ffn_fast_b, L0_ffn_w_fc, L0_ffn_w_proj, L0_ffn_u, L0_ffn_v, L0_ffn_gate)
    x = x + jnp.tanh(g_xattn[1]) * _L1_xattn_ref(ctx_1024, _layernorm(x, axis=-1))
    x = x + jnp.tanh(g_ffn[1]) * _L1_ffn_ref(_layernorm(x, axis=-1), L1_ffn_w1, L1_ffn_b1, L1_ffn_w2, L1_ffn_b2)
    return x

_drawn_inputs = setup_inputs


def setup_inputs(seed=0):
    import zlib

    import numpy as np

    out = dict(_drawn_inputs(seed))
    spreads = {'g_ffn': (-1.0, 0.6), 'L1_ffn_b1': (0.0, 0.353), 'L1_ffn_b2': (0.0, 0.337)}
    factors = {'L0_ffn_fast_b': 8.0, 'L0_ffn_w_fc': 2.94, 'L0_ffn_u': 8.0, 'L0_ffn_v': 8.0}
    for name, (base, spread) in spreads.items():
        noise = np.random.default_rng([zlib.crc32(name.encode()), seed]).standard_normal(out[name].shape)
        drawn = base * np.exp(spread * noise) if base else spread * noise
        out[name] = jnp.asarray(drawn.astype(out[name].dtype))
    for name, factor in factors.items():
        out[name] = (out[name] * factor).astype(out[name].dtype)
    return out
```

```python
from contextlib import ExitStack

import numpy as np
import concourse.bass as bass
from concourse import mybir

F32 = mybir.dt.float32
BF16 = mybir.dt.bfloat16
I32 = mybir.dt.int32
ALU = mybir.AluOpType
ACT = mybir.ActivationFunctionType
AX = mybir.AxisListType

P = 128
NB, S, D = 32, 256, 256
NH, DH = 16, 16
F = 1024
RANK = 16
T = S // P
C = D // P
FT = F // P
EPS = 1e-5
BIG = 3.0e38
MAGIC = 12582912.0
RSQRT_SEED = float(0x5F3759DF)

GROUPS = [(0, 6), (6, 6), (12, 4)]
SUMROW = 96
NPAIR = 8

Q_PARTS = [0, 1, 0, 1, 2, 0]
K_PARTS = [0, 0, 1, 1, 0, 2]
MAXROW = DH * len(Q_PARTS)

ROWS = 16
NCH = S // ROWS


class Batch:

    def __init__(self, half, p):
        self.half, self.p = half, p
        self.n = 2 * half + p

    def off(self, k):
        k += self.p
        return Batch(self.half + k // 2, k % 2)


def done(eng, sem, count, most, tick=None):
    if isinstance(count, int):
        if count <= 0:
            return
        count = min(count, most)
        eng.wait_ge(sem, count)
        return
    eng.wait_ge(sem, count)
    if tick is not None:
        eng.sem_inc(tick, 1)


class Chain:

    def __init__(self, eng, sem):
        self.eng, self.sem, self.base, self.n = eng, sem, 0, 0

    def tick(self, ins):
        self.n += 1
        ins.then_inc(self.sem, 1)

    def link(self, ins):
        self.tick(ins)
        self.hold()

    def hold(self):
        self.eng.wait_ge(self.sem, self.base + self.n)

    def tick_event(self):
        self.n += 1
        self.eng.sem_inc(self.sem, 1)


def layer_stats(v, ch, src, w, n=T):
    for t in range(n):
        ch.tick(v.bn_stats(w["st"][:, t, :], src[:, t, :]))
    ch.hold()
    ch.tick_event()
    for t in range(n):
        ch.tick(v.bn_aggr(w["mv"][:, t, :], w["st"][:, t, :]))
    ch.hold()
    ch.link(v.tensor_scalar(w["v"][:, 0:n], w["mv"][:, 0:n, 1], EPS, None, ALU.add))
    newton_rsqrt(v, ch, w["v"][:, 0:n], w["y"][:, 0:n], w["a"][:, 0:n])


def newton_rsqrt(v, ch, x, y, a):
    ch.link(v.tensor_scalar(y.bitcast(I32), x.bitcast(I32), -0.5, RSQRT_SEED, ALU.mult, ALU.add))
    for _ in range(3):
        ch.link(v.scalar_tensor_tensor(a, y, -0.5, y, ALU.mult, ALU.mult))
        ch.link(v.tensor_tensor(a, a, x, ALU.mult))
        ch.link(v.scalar_tensor_tensor(y, a, 1.5, y, ALU.add, ALU.mult))


def attention_phase(nc, io, scr):
    with ExitStack() as ctx:
        def sb(name, shape, dt=F32):
            return ctx.enter_context(nc.sbuf_tensor(name, shape, dt))

        def sem(name):
            return ctx.enter_context(nc.semaphore(name))

        wqT, wkT, wvT = sb("wqT", [P, C, D]), sb("wkT", [P, C, D]), sb("wvT", [P, C, D])
        woT = sb("woT", [P, len(GROUPS), D])
        wfcT = sb("wfcT", [P, C, F])
        wprT = sb("wprT", [P, FT, D])
        ident = sb("ident", [P, P])
        ones = sb("ones", [P, P])
        sel = sb("sel", [P, P])
        gates = sb("gates", [P, 4])
        xin = [sb(f"xin{p}", [P, T, D]) for p in range(2)]
        cin = [sb(f"cin{p}", [P, T, D]) for p in range(2)]
        xres = [sb(f"xres{p}", [P, T, D]) for p in range(2)]
        xhat, xT = sb("xhat", [P, T, D]), sb("xT", [P, C, S])
        cT = [sb(f"cT{p}", [P, C, S]) for p in range(2)]
        cD = sb("cD", [P, C, S])
        qp, kp = sb("qp", [P, 3, C, S], BF16), sb("kp", [P, 3, C, S], BF16)
        qr, kr = sb("qr", [P, C, S]), sb("kr", [P, C, S])
        qst = [sb(f"qst{p}", [P, NH, S], BF16) for p in range(2)]
        kst = [sb(f"kst{p}", [P, NH, S], BF16) for p in range(2)]
        vw = [sb(f"vw{p}", [P, T, NH, P]) for p in range(2)]
        nmax = sb("nmax", [P, 2 * NH])
        nsp = sb("nsp", [2 * NH, 2, P], BF16)
        pt = [sb(f"pt{r}", [P, 4, S]) for r in range(2)]
        osb, on = sb("osb", [P, len(GROUPS), S]), sb("on", [P, len(GROUPS), S])
        rc = sb("rc", [P, len(GROUPS), S])
        x1, xh2, x2T = sb("x1", [P, T, D]), sb("xh2", [P, T, D]), sb("x2T", [P, C, S])
        rl = sb("rl", [P, 2, 2, S])
        r2 = sb("r2", [P, FT, S])
        x2 = sb("x2", [P, T, D])
        yn, yT, ysq = sb("yn", [P, T, D]), sb("yT", [P, C, S]), sb("ysq", [P, C, S])
        bbs, dt_, dd = sb("bbs", [P, S]), sb("dt_", [P, T, S]), sb("dd", [P, T, S])
        aa = [sb(f"aa{p}", [P, T]) for p in range(2)]
        aaD = sb("aaD", [P, T])
        junk = sb("junk", [P, D])
        wk_ = {"st": sb("ln_st", [P, T, 6]), "mv": sb("ln_mv", [P, T, 2]), "v": sb("ln_v", [P, T]),
               "y": sb("ln_y", [P, T]), "a": sb("ln_a", [P, T])}

        setup_weights(nc, io, dict(wqT=wqT, wkT=wkT, wvT=wvT, woT=woT, wfcT=wfcT, wprT=wprT, ident=ident,
                                   ones=ones, sel=sel, gates=gates, vw=vw, qst=qst, kst=kst, rc=rc))

        sc = [ctx.enter_context(nc.psum_tensor(f"sc{r}", [P, 4, S], F32)) for r in range(2)]
        oacc = ctx.enter_context(nc.psum_tensor("oacc", [P, 2, S], F32))
        wb = [ctx.enter_context(nc.psum_tensor(f"wb{r}", [P, 2, S], F32)) for r in range(3)]

        names = ["xhat_t", "ctx_t", "q_mm", "k_mm", "v_mm", "max_t", "sum_bc01", "sum_bc2", "wo_mm", "xh2_t",
                 "fc_mm", "pr_mm", "y_t", "bb_mm", "ab_mm", "s1_mm", "s2_mm", "av_mm",
                 "xT_cp", "cT_cp", "qh_cp", "kh_cp", "vw_cp", "x2T_cp", "relu", "expd", "o_cp", "yT_cp", "bb_cp",
                 "dist", "aa_half", "aa_sum",
                 "ln1", "q_rem", "k_rem", "maxed", "max_split", "recip", "normed", "x1_res", "ln2", "x2_res", "ln3",
                 "d_part",
                 "q_parts_mid", "k_parts_mid", "q_parts", "k_parts", "squared", "y_sq", "maxrow_zero", "cD_cp",
                 "q_out", "k_out", "max_in", "x2_out", "d_out", "vchain", "sp_tick", "pool_tick"]
        e = {n: sem(n) for n in names}
        x_in = [sem(f"x_in{p}") for p in range(2)]
        c_in = [sem(f"c_in{p}") for p in range(2)]
        xr_in = [sem(f"xr_in{p}") for p in range(2)]
        q_in = [sem(f"q_in{p}") for p in range(2)]
        k_in = [sem(f"k_in{p}") for p in range(2)]
        NQ = len(Q_PARTS)

        tok = "(t p) d -> p t d"
        x_d, c_d = io["x"], io["ctx_1024"]
        block = ctx.enter_context(nc.Block())

        def run(iteration, eng, chain=None):
            iteration(Batch(-1, 1))
            iteration(Batch(0, 0))
            before = chain.n if chain else 0
            iteration(Batch(0, 1))
            step = 2 * (chain.n - before) if chain else 0
            start = chain.n if chain else 0
            with eng.Fori(1, NB // 2 - 1) as h:
                if chain:
                    chain.base = (h - 1) * step
                iteration(Batch(h, 0))
                iteration(Batch(h, 1))
            if chain:
                assert chain.n - start == step
                chain.base = (NB // 2 - 3) * step
            iteration(Batch(NB // 2 - 1, 0))
            iteration(Batch(NB // 2 - 1, 1))
            iteration(Batch(NB // 2, 0))

        def there(b):
            return not isinstance(b.n, int) or 0 <= b.n < NB

        @block.sync
        def _(sp):
            def w(s, count, most=NB):
                done(sp, s, count, most, e["sp_tick"])

            def load_x_ctx(b):
                w(e["ln1"], b.n - 1)
                sp.dma_start(xin[b.p][:], x_d[b.n].rearrange(tok, p=P)).then_inc(x_in[b.p], 16)
                w(e["ctx_t"], b.n - 1)
                w(e["aa_sum"], b.n - 1)
                sp.dma_start(cin[b.p][:], c_d[b.n].rearrange(tok, p=P)).then_inc(c_in[b.p], 16)

            def load_res(b):
                w(e["x1_res"], b.n - 1)
                sp.dma_start(xres[b.p][:], x_d[b.n].rearrange(tok, p=P)).then_inc(xr_in[b.p], 16)

            def restack(b):
                for parts, made, out, dram, st, inn, order in (
                        (qp, "q_parts", "q_out", scr["q"], qst, q_in, Q_PARTS),
                        (kp, "k_parts", "k_out", scr["k"], kst, k_in, K_PARTS)):
                    w(e[made], b.n + 1)
                    w(inn[1 - b.p], 16 * NQ * (b.off(-1).half + 1), 16 * NQ * NB)
                    sp.dma_start(dram.rearrange("a (m p) t -> p (a m) t", p=P),
                                 parts[:].rearrange("p a m t -> p (a m) t")).then_inc(e[out], 16)
                for out, dram, st, inn, order in (("q_out", scr["q"], qst, q_in, Q_PARTS),
                                                  ("k_out", scr["k"], kst, k_in, K_PARTS)):
                    w(e["s2_mm"], NPAIR * (b.n - 1), NPAIR * NB)
                    w(e[out], 16 * (b.n + 1), 16 * NB)
                    for blk, part in enumerate(order):
                        sp.dma_start(st[b.p][DH * blk:DH * blk + DH, :, :],
                                     dram[part].rearrange("(h r) t -> r h t", r=DH)).then_inc(inn[b.p], 16)

            def max_rows(b):
                w(e["max_split"], b.n + 1)
                w(e["s1_mm"], NPAIR * (b.n + 1), NPAIR * NB)
                for part in range(2):
                    sp.dma_start(qst[b.p][MAXROW + part:MAXROW + part + 1, :, :].rearrange("o h (a t) -> o (h a) t", t=P),
                                 nsp[:, part:part + 1, :].rearrange("m o t -> m o t")).then_inc(e["max_in"], 16)

            def store_x2(b):
                w(e["x2_res"], b.n + 1)
                sp.dma_start(scr["x2"][b.n].rearrange(tok, p=P), x2[:]).then_inc(e["x2_out"], 16)

            def store_d(b):
                w(e["dist"], b.n + 1)
                sp.dma_start(scr["d"].rearrange("(t p) b s -> p t b s", p=P)[:, :, b.n, :], dd[:])\
                    .then_inc(e["d_out"], 16)

            load_x_ctx(Batch(0, 0))

            def iteration(i):
                if there(i.off(2)):
                    load_x_ctx(i.off(2))
                if there(i):
                    load_res(i)
                if there(i.off(1)):
                    restack(i.off(1))
                if there(i):
                    max_rows(i)
                if there(i.off(-1)):
                    store_x2(i.off(-1))
                    store_d(i.off(-1))
            run(iteration, sp)
            sp.wait_ge(e["x2_out"], 16 * NB)
            sp.wait_ge(e["d_out"], 16 * NB)

        @block.tensor
        def _(pe):
            def w(s, count, most=NB):
                done(pe, e[s] if isinstance(s, str) else s, count, most)

            def transposes(dst, src):
                for c in range(C):
                    for t in range(T):
                        last = pe.transpose(dst[:, c, t * P:t * P + P], src[:, t, c * P:c * P + P], ident[:])
                return last

            def before(b):
                w("ln1", b.n + 1)
                w("normed", b.n - 1)
                w("kh_cp", b.n), w("k_rem", b.n)
                transposes(wb[0], xhat).then_inc(e["xhat_t"], 1)
                w(c_in[b.p], 16 * (b.half + 1), 16 * NB)
                w("vw_cp", b.n)
                transposes(wb[1], cin[b.p]).then_inc(e["ctx_t"], 1)
                w("xT_cp", b.n + 1)
                w("x1_res", b.n - 1)
                w("qh_cp", b.n), w("q_rem", b.n)
                for wt, src, bank, ready, s in ((wqT, xT, 2, "xT_cp", "q_mm"), (wkT, cT[b.p], 0, "cT_cp", "k_mm")):
                    w(ready, b.n + 1)
                    for m in range(C):
                        for c in range(C):
                            last = pe.matmul(wb[bank][:, m, :], wt[:, c, m * P:m * P + P], src[:, c, :],
                                             start=(c == 0), stop=(c == C - 1))
                    last.then_inc(e[s], 1)
                for t in range(T):
                    for c in range(C):
                        last = pe.matmul(wb[1][:, t, :], cT[b.p][:, c, t * P:t * P + P], wvT[:, c, :],
                                         start=(c == 0), stop=(c == C - 1))
                last.then_inc(e["v_mm"], 1)

            def sums(b):
                w("recip", b.n + 1)
                w("yT_cp", b.n), w("kh_cp", b.n + 2), w("k_rem", b.n + 2)
                for g in range(2):
                    last = pe.matmul(wb[0][:, g, :], sel[:], rc[:, g, :], start=True, stop=True)
                last.then_inc(e["sum_bc01"], 1)
                w("bb_cp", b.n), w("max_split", b.n + 1)
                pe.matmul(wb[1][:, 0, :], sel[:], rc[:, 2, :], start=True, stop=True).then_inc(e["sum_bc2"], 1)

            def out_proj(b):
                w("normed", b.n + 1)
                w("d_part", b.n), w("qh_cp", b.n + 2), w("q_rem", b.n + 2)
                for t in range(T):
                    for g in range(len(GROUPS)):
                        last = pe.matmul(wb[2][:, t, :], on[:, g, t * P:t * P + P], woT[:, g, :],
                                         start=(g == 0), stop=(g == len(GROUPS) - 1))
                last.then_inc(e["wo_mm"], 1)

            def scores1(b, c):
                if c < 2:
                    w("expd", NPAIR * b.n + c - 1, NPAIR * NB)
                else:
                    w("maxed", NPAIR * b.n + c - 1, NPAIR * NB)
                if c == 0:
                    w(q_in[b.p], 16 * NQ * (b.half + 1), 16 * NQ * NB)
                    w(k_in[b.p], 16 * NQ * (b.half + 1), 16 * NQ * NB)
                    w("maxrow_zero", b.n - 1)
                for u in range(4):
                    h, t = 2 * c + u // 2, u % 2
                    last = pe.matmul(sc[c % 2][:, u, :], qst[b.p][:, h, t * P:t * P + P], kst[b.p][:, h, :],
                                     start=True, stop=True)
                last.then_inc(e["s1_mm"], 1)

            def max_transpose(b):
                w("maxed", NPAIR * (b.n + 1), NPAIR * NB)
                w("relu", 4 * (b.n - 1) + 2, 4 * NB), w("vw_cp", b.n + 2)
                pe.transpose(wb[1][0:2 * NH, 0, 0:P], nmax[:], ident[:]).then_inc(e["max_t"], 1)

            def scores2(b, c):
                if c < 2:
                    w("maxed", NPAIR * b.n + NPAIR - 1 + c, NPAIR * NB)
                else:
                    w("expd", NPAIR * b.n + c - 1, NPAIR * NB)
                if c == 0:
                    w("max_in", 32 * (b.n + 1), 32 * NB)
                for u in range(4):
                    h, t = 2 * c + u // 2, u % 2
                    last = pe.matmul(sc[c % 2][:, u, :], kst[b.p][:, h, t * P:t * P + P], qst[b.p][:, h, :],
                                     start=True, stop=True)
                last.then_inc(e["s2_mm"], 1)

            def values(b, c):
                w("expd", NPAIR * b.n + c + 1, NPAIR * NB)
                if c == 0:
                    w("vw_cp", b.n + 1)
                for u in range(2):
                    h = 2 * c + u
                    g = [k for k, (h0, n) in enumerate(GROUPS) if h0 <= h < h0 + n][0]
                    h0, n = GROUPS[g]
                    if h == h0:
                        w("o_cp", 3 * b.n + g, 3 * NB)
                    for t in range(T):
                        last = pe.matmul(oacc[:, g % 2, :], vw[b.p][:, t, h, :], pt[c % 2][:, 2 * u + t, :],
                                         start=(h == h0 and t == 0), stop=(h == h0 + n - 1 and t == T - 1))
                last.then_inc(e["av_mm"], 1)

            def xh2_transposes(b):
                w("ln2", b.n + 1)
                w("qh_cp", b.n + 3), w("q_rem", b.n + 3), w("x1_res", b.n + 1)
                transposes(wb[2], xh2).then_inc(e["xh2_t"], 1)

            def fc(b, k):
                bank = (0, 1, 2, 0)[k]
                if k == 0:
                    w("x2T_cp", b.n + 1)
                    w("kh_cp", b.n + 3), w("k_rem", b.n + 3), w("normed", b.n + 1)
                elif k == 1:
                    w("vw_cp", b.n + 3), w("normed", b.n + 1)
                elif k == 3:
                    w("relu", 4 * b.n + 1, 4 * NB)
                for j in range(2):
                    f = 2 * k + j
                    for c in range(C):
                        last = pe.matmul(wb[bank][:, j, :], wfcT[:, c, f * P:f * P + P], x2T[:, c, :],
                                         start=(c == 0), stop=(c == C - 1))
                last.then_inc(e["fc_mm"], 1)

            def proj(b):
                w("relu", 4 * b.n + 3, 4 * NB)
                w("squared", 4 * (b.n + 1), 4 * NB)
                for t in range(T):
                    for f in range(FT):
                        last = pe.matmul(wb[2][:, t, :], r2[:, f, t * P:t * P + P], wprT[:, f, :],
                                         start=(f == 0), stop=(f == FT - 1))
                last.then_inc(e["pr_mm"], 1)

            def y_transposes(b):
                w("ln3", b.n + 1)
                w("relu", 4 * (b.n + 1), 4 * NB)
                transposes(wb[0], yn).then_inc(e["y_t"], 1)

            def row_norms(b):
                w("y_sq", b.n + 1)
                w("max_split", b.n + 2), w("relu", 4 * b.n + 2, 4 * NB)
                for c in range(C):
                    last = pe.matmul(wb[1][:, 0, :], ones[:], ysq[:, c, :], start=(c == 0), stop=(c == C - 1))
                last.then_inc(e["bb_mm"], 1)

            def products(b):
                w("yT_cp", b.n + 1), w("cD_cp", b.n + 1)
                w("x2_res", b.n + 1)
                for t in range(T):
                    for c in range(C):
                        last = pe.matmul(wb[2][:, t, :], cD[:, c, t * P:t * P + P], yT[:, c, :],
                                         start=(c == 0), stop=(c == C - 1))
                last.then_inc(e["ab_mm"], 1)

            def iteration(i):
                a, z = i.off(1), i.off(-1)
                if there(z):
                    sums(z)
                    out_proj(z)
                if there(a):
                    before(a)
                if there(i):
                    scores1(i, 0)
                    scores1(i, 1)
                if there(z):
                    xh2_transposes(z)
                for k in range(4):
                    if there(z):
                        fc(z, k)
                    if there(i):
                        scores1(i, k + 2)
                if there(i):
                    scores1(i, 6)
                    scores1(i, 7)
                    max_transpose(i)
                if there(z):
                    proj(z)
                for c in range(NPAIR + 1):
                    if there(i):
                        if c < NPAIR:
                            scores2(i, c)
                        if c >= 1:
                            values(i, c - 1)
                    if there(z):
                        if c == 2:
                            y_transposes(z)
                        if c == 3:
                            row_norms(z)
                        if c == 5:
                            products(z)
            run(iteration, pe)

        @block.scalar
        def _(act):
            def w(s, count, most=NB):
                done(act, e[s] if isinstance(s, str) else s, count, most)

            def copy_group(b, g):
                h0, n = GROUPS[g]
                w("av_mm", NPAIR * b.n + (h0 + n - 1) // 2 + 1, NPAIR * NB)
                if g == 0:
                    w("normed", b.n)
                act.activation(osb[:, g, :], oacc[:, g % 2, :], ACT.Copy).then_inc(e["o_cp"], 1)

            def before(b):
                w("xhat_t", b.n + 1), w("q_mm", b.n)
                act.activation(xT[:], wb[0][:], ACT.Copy).then_inc(e["xT_cp"], 1)
                w("ctx_t", b.n + 1), w("cD_cp", b.n - 1), w("v_mm", b.n - 1)
                act.activation(cT[b.p][:], wb[1][:], ACT.Copy).then_inc(e["cT_cp"], 1)
                w("q_mm", b.n + 1), w("q_out", 16 * b.n, 16 * NB)
                act.activation(qp[:, 0, :, :], wb[2][:], ACT.Copy, scale=1.0 / 16).then_inc(e["qh_cp"], 1)
                w("k_mm", b.n + 1), w("k_out", 16 * b.n, 16 * NB)
                act.activation(kp[:, 0, :, :], wb[0][:], ACT.Copy).then_inc(e["kh_cp"], 1)
                w("v_mm", b.n + 1), w("av_mm", NPAIR * (b.n - 1), NPAIR * NB)
                for g, (h0, n) in enumerate(GROUPS):
                    for t in range(T):
                        dst = vw[b.p][:, t, h0:h0 + n, :].rearrange("p h m -> p (h m)")
                        dst = diagonal(dst, n)
                        last = act.activation(dst, wb[1][:, t, DH * h0:DH * (h0 + n)].rearrange("p (h m) -> p h m", m=DH),
                                              ACT.Copy)
                last.then_inc(e["vw_cp"], 1)
                w("cD_cp", b.n - 1)
                for t in range(T):
                    if t:
                        act.wait_ge(e["aa_half"], b.n + 1)
                    ins = act.activation(junk[:], cin[b.p][:, t, :], ACT.Square, accum_out=aa[b.p][:, t:t + 1])
                    ins.then_inc(e["aa_half"] if t == 0 else e["aa_sum"], 1)

            def xh2_copy(b):
                w("xh2_t", b.n + 1), w("fc_mm", 4 * b.n, 4 * NB)
                act.activation(x2T[:], wb[2][:], ACT.Copy).then_inc(e["x2T_cp"], 1)

            def relu(b, k):
                w("fc_mm", 4 * b.n + k + 1, 4 * NB)
                w("squared", 4 * b.n + k - 1, 4 * NB)
                act.activation(rl[:, k % 2], wb[(0, 1, 2, 0)[k]][:], ACT.Relu).then_inc(e["relu"], 1)

            def exps(b, c):
                w("s2_mm", NPAIR * b.n + c + 1, NPAIR * NB)
                w("av_mm", NPAIR * b.n + c - 1, NPAIR * NB)
                act.activation(pt[c % 2][:], sc[c % 2][:], ACT.Exp).then_inc(e["expd"], 1)

            def yT_copy(b):
                w("y_t", b.n + 1), w("ab_mm", b.n), w("y_sq", b.n)
                act.activation(yT[:], wb[0][:], ACT.Copy).then_inc(e["yT_cp"], 1)

            def bb_copy(b):
                w("bb_mm", b.n + 1), w("d_part", b.n)
                act.activation(bbs[:], wb[1][:, 0, :], ACT.Copy).then_inc(e["bb_cp"], 1)

            def distance(b):
                w("d_part", b.n + 1), w("d_out", 16 * b.n, 16 * NB), w("cD_cp", b.n + 1)
                for t in range(T):
                    last = act.activation(dd[:, t, :], dt_[:, t, :], ACT.Relu, bias=aaD[:, t:t + 1])
                last.then_inc(e["dist"], 1)

            def iteration(i):
                a, z = i.off(1), i.off(-1)
                if there(z):
                    copy_group(z, 2)
                if there(a):
                    before(a)
                if there(z):
                    xh2_copy(z)
                    for k in range(4):
                        relu(z, k)
                for c in range(NPAIR):
                    if there(i):
                        exps(i, c)
                        if c == 3:
                            copy_group(i, 0)
                        if c == 6:
                            copy_group(i, 1)
                    if there(z):
                        if c == 2:
                            yT_copy(z)
                        if c == 3:
                            bb_copy(z)
                        if c == 6:
                            distance(z)
            run(iteration, act)

        @block.vector
        def _(v):
            ch = Chain(v, e["vchain"])

            def w(s, count, most=NB):
                done(v, e[s] if isinstance(s, str) else s, count, most)

            def apply_norm(dst, src, s):
                for t in range(T):
                    last = v.tensor_scalar(dst[:, t, :], src[:, t, :], wk_["mv"][:, t, 0:1], wk_["y"][:, t:t + 1],
                                           ALU.subtract, ALU.mult)
                last.then_inc(e[s], 1)

            def ln1(b):
                w(x_in[b.p], 16 * (b.half + 1), 16 * NB)
                layer_stats(v, ch, xin[b.p], wk_)
                w("xhat_t", b.n)
                apply_norm(xhat, xin[b.p], "ln1")
                w("ln1", b.n + 1)

            def recip(b):
                w("o_cp", 3 * (b.n + 1), 3 * NB), w("sum_bc2", b.n)
                for g, (_, n) in enumerate(GROUPS):
                    last = v.reciprocal(rc[SUMROW:SUMROW + n, g, :], osb[SUMROW:SUMROW + n, g, :])
                last.then_inc(e["recip"], 1)

            def normalise(b):
                w("sum_bc01", b.n + 1), w("wo_mm", b.n)
                v.tensor_tensor(on[:, 0:2, :], osb[:, 0:2, :], wb[0][:], ALU.mult)
                w("sum_bc2", b.n + 1)
                v.tensor_tensor(on[:, 2, :], osb[:, 2, :], wb[1][:, 0, :], ALU.mult).then_inc(e["normed"], 1)

            def residual1(b):
                w("wo_mm", b.n + 1), w(xr_in[b.p], 16 * (b.half + 1), 16 * NB)
                v.scalar_tensor_tensor(x1[:], wb[2][:], gates[:, 0:1], xres[b.p][:], ALU.mult, ALU.add)\
                    .then_inc(e["x1_res"], 1)
                w("x1_res", b.n + 1)
                layer_stats(v, ch, x1, wk_)
                w("xh2_t", b.n)
                apply_norm(xh2, x1, "ln2")
                w("ln2", b.n + 1)

            def remainders(b):
                w("q_mm", b.n + 1), w("qh_cp", b.n + 1), w("q_parts", b.n)
                v.scalar_tensor_tensor(qr[:], wb[2][:], 1.0 / 16, qp[:, 0, :, :], ALU.mult, ALU.subtract)\
                    .then_inc(e["q_rem"], 1)
                w("k_mm", b.n + 1), w("kh_cp", b.n + 1), w("k_parts", b.n)
                v.tensor_tensor(kr[:], wb[0][:], kp[:, 0, :, :], ALU.subtract).then_inc(e["k_rem"], 1)

            def maxima(b, c):
                w("s1_mm", NPAIR * b.n + c + 1, NPAIR * NB)
                if c == 0:
                    w("max_t", b.n)
                v.tensor_reduce(nmax[:, 4 * c:4 * c + 4], sc[c % 2][:], AX.X, ALU.max, negate=True)\
                    .then_inc(e["maxed"], 1)

            def split_max(b):
                w("max_t", b.n + 1), w("max_in", 32 * b.n, 32 * NB)
                ch.link(v.tensor_copy(nsp[:, 0, :], wb[1][0:2 * NH, 0, 0:P]))
                v.tensor_tensor(nsp[:, 1, :], wb[1][0:2 * NH, 0, 0:P], nsp[:, 0, :], ALU.subtract)\
                    .then_inc(e["max_split"], 1)

            def residual2(b):
                w("pr_mm", b.n + 1), w("x2_out", 16 * b.n, 16 * NB)
                v.scalar_tensor_tensor(x2[:], wb[2][:], gates[:, 2:3], x1[:], ALU.mult, ALU.add)\
                    .then_inc(e["x2_res"], 1)
                w("x2_res", b.n + 1)
                layer_stats(v, ch, x2, wk_)
                w("y_t", b.n)
                apply_norm(yn, x2, "ln3")
                w("ln3", b.n + 1)

            def distance_part(b):
                w("ab_mm", b.n + 1), w("bb_cp", b.n + 1), w("dist", b.n)
                for t in range(T):
                    last = v.scalar_tensor_tensor(dt_[:, t, :], wb[2][:, t, :], -2.0, bbs[:], ALU.mult, ALU.add)
                last.then_inc(e["d_part"], 1)

            ln1(Batch(0, 0))

            def iteration(i):
                a, z = i.off(1), i.off(-1)
                if there(z):
                    recip(z)
                    normalise(z)
                    residual1(z)
                if there(a):
                    remainders(a)
                if there(i):
                    for c in range(NPAIR):
                        maxima(i, c)
                    split_max(i)
                if there(z):
                    residual2(z)
                if there(i.off(2)):
                    ln1(i.off(2))
                if there(z):
                    distance_part(z)
            run(iteration, v, ch)

        @block.gpsimd
        def _(pool):
            def w(s, count, most=NB):
                done(pool, e[s], count, most, e["pool_tick"])

            def parts(b):
                for rem, made, r, pt_, out in (("q_rem", "q_parts", qr, qp, "q_out"), ("k_rem", "k_parts", kr, kp, "k_out")):
                    w(rem, b.n + 1), w(out, 16 * b.n, 16 * NB)
                    pool.tensor_copy(pt_[:, 1, :, :], r[:]).then_inc(e[made + "_mid"], 1)
                    w(made + "_mid", b.n + 1)
                    pool.tensor_tensor(pt_[:, 2, :, :], r[:], pt_[:, 1, :, :], ALU.subtract).then_inc(e[made], 1)

            def squares(b):
                for k in range(4):
                    w("relu", 4 * b.n + k + 1, 4 * NB)
                    if k == 0:
                        w("pr_mm", b.n)
                    pool.tensor_tensor(r2[:, 2 * k:2 * k + 2, :], rl[:, k % 2], rl[:, k % 2], ALU.mult)\
                        .then_inc(e["squared"], 1)

            def y_squares(b):
                w("yT_cp", b.n + 1), w("bb_mm", b.n)
                pool.tensor_tensor(ysq[:], yT[:], yT[:], ALU.mult).then_inc(e["y_sq"], 1)

            def zero_max_rows(b):
                w("s2_mm", NPAIR * (b.n + 1), NPAIR * NB)
                w("cD_cp", b.n + 1)
                pool.memset(qst[b.p][MAXROW:MAXROW + 2, :, :], 0.0).then_inc(e["maxrow_zero"], 1)
                w("maxrow_zero", b.n + 1)

            def keep_ctx(b):
                w("aa_sum", b.n + 1), w("dist", b.n)
                pool.tensor_copy(aaD[:], aa[b.p][:])
                w("cT_cp", b.n + 1), w("ab_mm", b.n)
                pool.tensor_copy(cD[:], cT[b.p][:]).then_inc(e["cD_cp"], 1)

            def iteration(i):
                a, z = i.off(1), i.off(-1)
                if there(z):
                    zero_max_rows(z)
                if there(a):
                    parts(a)
                if there(z):
                    squares(z)
                    y_squares(z)
                if there(i):
                    keep_ctx(i)
            run(iteration, pool)


def diagonal(ap, n):
    return bass.AP(ap.tensor, ap.offset, [list(ap.ap[0]), [P + DH, n], [1, DH]])


def setup_weights(nc, io, o):
    with ExitStack() as ctx:
        def sb(name, shape, dt=F32):
            return ctx.enter_context(nc.sbuf_tensor(name, shape, dt))

        def sem(name):
            return ctx.enter_context(nc.semaphore(name))

        raw = {n: sb("raw_" + n, [P, C, D]) for n in ("wq", "wk", "wv", "wo")}
        wfc, wpr = sb("wfc", [P, FT, D]), sb("wpr", [P, C, F])
        u, vv, fbT = sb("u", [P, FT, RANK]), sb("vv", [RANK, D]), sb("fbT", [RANK, RANK])
        uT, fbv = sb("uT", [RANK, F]), sb("fbv", [RANK, D])
        scl = sb("scl", [P, FT + C])
        rsc = sb("rsc", [P, FT + C])
        gin = sb("gin", [P, 5])
        ps = [ctx.enter_context(nc.psum_tensor(f"su{r}", [P, 512], F32)) for r in range(4)]
        loaded, consts, quant, turned, copied, tanhd, vch = (sem(n) for n in (
            "w_loaded", "consts", "quantised", "turned", "copied", "tanhd", "w_chain"))
        pch = sem("w_pool_chain")
        block = ctx.enter_context(nc.Block())
        NLOAD = 12

        @block.sync
        def _(sp):
            for n in ("wq", "wk", "wv", "wo"):
                sp.dma_start(raw[n][:], io["L0_xattn_" + n].rearrange("(a p) d -> p a d", p=P)).then_inc(loaded, 16)
            sp.dma_start(wfc[:], io["L0_ffn_w_fc"].rearrange("(a p) d -> p a d", p=P)).then_inc(loaded, 16)
            sp.dma_start(wpr[:], io["L0_ffn_w_proj"].rearrange("(a p) f -> p a f", p=P)).then_inc(loaded, 16)
            sp.dma_start(u[:], io["L0_ffn_u"].rearrange("(a p) r -> p a r", p=P)).then_inc(loaded, 16)
            sp.dma_start(vv[:], io["L0_ffn_v"]).then_inc(loaded, 16)
            sp.dma_start(fbT[:], io["L0_ffn_fast_b"].rearrange("a b -> b a"), allow_slow_non_contiguous=True)\
                .then_inc(loaded, 16)
            sp.dma_start(gin[:, 0:2], io["g_xattn"].partition_broadcast(P)).then_inc(loaded, 16)
            sp.dma_start(gin[:, 2:4], io["g_ffn"].partition_broadcast(P)).then_inc(loaded, 16)
            sp.dma_start(gin[:, 4:5], io["L0_ffn_gate"].partition_broadcast(P)).then_inc(loaded, 16)
            sp.wait_ge(loaded, 16 * NLOAD)

        @block.gpsimd
        def _(pool):
            pc = Chain(pool, pch)
            pc.link(pool.memset(o["ident"][:], 0.0))
            pc.link(pool.memset(o["sel"][:], 1.0))
            pc.link(pool.memset(o["ones"][:], 1.0))
            pc.link(pool.memset(o["woT"][:], 0.0))
            pc.link(pool.memset(o["rc"][:], 0.0))
            for p in range(2):
                pc.link(pool.memset(o["vw"][p][:], 0.0))
                pc.link(pool.memset(o["qst"][p][MAXROW:P, :, :], 0.0))
                pc.link(pool.memset(o["kst"][p][MAXROW:P, :, :], 0.0))
            pc.link(pool.affine_select(out=o["ident"][:], in_=o["ident"][:], compare_op=ALU.not_equal, fill=1.0,
                                       base=0, pattern=[[-1, P]], channel_multiplier=1))
            pc.link(pool.affine_select(out=o["sel"][:], in_=o["sel"][:], compare_op=ALU.is_ge, fill=0.0,
                                       base=DH * SUMROW, pattern=[[1, P]], channel_multiplier=-DH))
            pc.link(pool.affine_select(out=o["sel"][:], in_=o["sel"][:], compare_op=ALU.is_ge, fill=0.0,
                                       base=DH - 1 - DH * SUMROW, pattern=[[-1, P]], channel_multiplier=DH))
            for p in range(2):
                pc.link(pool.memset(o["kst"][p][MAXROW:MAXROW + 2, :, :], 1.0))
                for h0, n in GROUPS:
                    for s in range(n):
                        pc.link(pool.memset(o["vw"][p][:, :, h0 + s, SUMROW + s:SUMROW + s + 1], 1.0))
            pool.sem_inc(consts, 1)

        @block.scalar
        def _(act):
            act.wait_ge(loaded, 16 * NLOAD)
            act.activation(o["gates"][:], gin[:, 0:4], ACT.Tanh).then_inc(tanhd, 1)
            act.wait_ge(tanhd, 1)

        jobs = []
        for n in ("wq", "wk", "wv"):
            for a in range(C):
                for c in range(C):
                    jobs.append((raw[n][:, a, c * P:c * P + P], o[n + "T"][:, c, a * P:a * P + P], P, None))
        for g, (h0, n) in enumerate(GROUPS):
            for a in range(C):
                jobs.append((raw["wo"][:, a, DH * h0:DH * (h0 + n)], o["woT"][0:DH * n, g, a * P:a * P + P], DH * n, None))
        for a in range(C):
            for f in range(FT):
                jobs.append((wpr[:, a, f * P:f * P + P], o["wprT"][:, f, a * P:a * P + P], P, None))
        for f in range(FT):
            for c in range(C):
                jobs.append((wfc[:, f, c * P:c * P + P], o["wfcT"][:, c, f * P:f * P + P], P, (f, c)))

        @block.vector
        def _(v):
            ch = Chain(v, vch)
            v.wait_ge(loaded, 16 * NLOAD)
            quantise_rows(v, ch, wfc, scl[:, 0:FT], rsc[:, 0:FT], FT, D)
            quantise_rows(v, ch, wpr, scl[:, FT:FT + C], rsc[:, FT:FT + C], C, F)
            v.sem_inc(quant, 1)
            for f in range(FT):
                v.wait_ge(turned, f + 1)
                v.tensor_copy(uT[:, f * P:f * P + P], ps[f % 2][0:RANK, 0:P]).then_inc(copied, 1)
            v.wait_ge(turned, FT + 1)
            v.tensor_copy(fbv[:], ps[2][0:RANK, 0:D]).then_inc(copied, 1)
            v.wait_ge(consts, 1)
            for k, (_, dst, rows, lowrank) in enumerate(jobs):
                v.wait_ge(turned, FT + 2 + k)
                if lowrank is None:
                    v.tensor_copy(dst, ps[k % 2][0:rows, 0:P]).then_inc(copied, 1)
                else:
                    ch.link(v.tensor_copy(dst, ps[k % 2][0:rows, 0:P]))
                    v.scalar_tensor_tensor(dst, ps[2 + k % 2][0:rows, 0:P], gin[:, 4:5], dst, ALU.mult, ALU.add)\
                        .then_inc(copied, 1)
            v.wait_ge(copied, FT + 1 + len(jobs))

        @block.tensor
        def _(pe):
            pe.wait_ge(consts, 1)
            pe.wait_ge(loaded, 16 * NLOAD)
            for f in range(FT):
                if f >= 2:
                    pe.wait_ge(copied, f - 1)
                pe.transpose(ps[f % 2][0:RANK, 0:P], u[:, f, :], o["ident"][:]).then_inc(turned, 1)
            pe.matmul(ps[2][0:RANK, 0:D], fbT[:], vv[:], start=True, stop=True).then_inc(turned, 1)
            pe.wait_ge(quant, 1)
            for k, (src, _, rows, lowrank) in enumerate(jobs):
                pe.wait_ge(copied, FT + k if k < 2 else FT + k)
                if lowrank is not None:
                    f, c = lowrank
                    pe.matmul(ps[2 + k % 2][:, 0:P], fbv[:, c * P:c * P + P], uT[:, f * P:f * P + P],
                              start=True, stop=True)
                pe.transpose(ps[k % 2][0:rows, 0:P], src, o["ident"][:]).then_inc(turned, 1)


def quantise_rows(v, ch, w, scl, rsc, n, width):
    for a in range(n):
        ch.tick(v.tensor_reduce(scl[:, a:a + 1], w[:, a, :], AX.X, ALU.add, apply_absolute_value=True))
    ch.hold()
    ch.link(v.tensor_scalar(scl, scl, 1.0 / width, 1e-5, ALU.mult, ALU.max))
    ch.link(v.reciprocal(rsc, scl))
    for a in range(n):
        ch.tick(v.tensor_scalar(w[:, a, :], w[:, a, :], rsc[:, a:a + 1], MAGIC, ALU.mult, ALU.add))
    ch.hold()
    for a in range(n):
        ch.tick(v.tensor_scalar(w[:, a, :], w[:, a, :], MAGIC, 1.0, ALU.subtract, ALU.min))
    ch.hold()
    for a in range(n):
        ch.tick(v.tensor_scalar(w[:, a, :], w[:, a, :], -1.0, scl[:, a:a + 1], ALU.max, ALU.mult))
    ch.hold()


def alignment_phase(nc, io, scr):
    with ExitStack() as ctx:
        def sb(name, shape, dt=F32):
            return ctx.enter_context(nc.sbuf_tensor(name, shape, dt))

        def sem(name):
            return ctx.enter_context(nc.semaphore(name))

        dist = [sb(f"rows_d{p}", [NB, ROWS, S]) for p in range(2)]
        cost = [sb(f"rows_r{p}", [NB, ROWS, S + 1]) for p in range(2)]
        best = sb("best", [NB, S])
        d_in = [sem(f"d_in{p}") for p in range(2)]
        r_out = [sem(f"r_out{p}") for p in range(2)]
        v_out, rooted, costed, edge, rch, tick = (sem(n) for n in ("virtual_out", "rooted", "costed", "edge", "row_chain", "sp_tick2"))
        block = ctx.enter_context(nc.Block())
        dram_d = scr["d"].rearrange("i b s -> b i s")

        @block.sync
        def _(sp):
            sp.dma_start(dist[0][:], dram_d[:, 0:ROWS, :]).then_inc(d_in[0], 16)
            sp.dma_start(dist[1][:], dram_d[:, ROWS:2 * ROWS, :]).then_inc(d_in[1], 16)
            sp.wait_ge(edge, 1)
            sp.dma_start(scr["r"][:, 0:1, :], cost[1][:, ROWS - 1:ROWS, :]).then_inc(v_out, 16)
            sp.wait_ge(v_out, 16)
            sp.sem_inc(edge, 1)

            def chunk(h, p, more):
                done(sp, costed, 2 * h + p + 1, NCH, tick)
                sp.dma_start(scr["r"][:, bass.ds((2 * h + p) * ROWS + 1, ROWS), :], cost[p][:]).then_inc(r_out[p], 16)
                if more:
                    sp.dma_start(dist[p][:], dram_d[:, bass.ds((2 * h + p + 2) * ROWS, ROWS), :]).then_inc(d_in[p], 16)
            with sp.Fori(0, NCH // 2 - 1) as h:
                chunk(h, 0, True)
                chunk(h, 1, True)
            chunk(NCH // 2 - 1, 0, False)
            chunk(NCH // 2 - 1, 1, False)
            for p in range(2):
                sp.wait_ge(r_out[p], 16 * NCH // 2)

        @block.scalar
        def _(act):
            def chunk(h, p):
                act.wait_ge(d_in[p], 16 * (h + 1))
                act.activation(dist[p][:], dist[p][:], ACT.Sqrt).then_inc(rooted, 1)
            with act.Fori(0, NCH // 2) as h:
                chunk(h, 0)
                chunk(h, 1)

        @block.vector
        def _(v):
            ch = Chain(v, rch)
            ch.link(v.memset(cost[0][:, :, 0:1], BIG))
            ch.link(v.memset(cost[1][:, :, 0:1], BIG))
            ch.link(v.memset(cost[1][:, ROWS - 1, :], BIG))
            ch.link(v.memset(cost[1][:, ROWS - 1, 0:1], 0.0))
            v.sem_inc(edge, 1)
            v.wait_ge(edge, 2)

            def chunk(h, p, full):
                v.wait_ge(rooted, 2 * h + p + 1)
                if full:
                    v.wait_ge(r_out[p], 16 * h)
                for i in range(ROWS):
                    prev = cost[p][:, i - 1, :] if i else cost[1 - p][:, ROWS - 1, :]
                    ch.link(v.tensor_tensor(best[:], prev[:, 1:S + 1], prev[:, 0:S], ALU.min))
                    row = v.tensor_tensor_scan(cost[p][:, i, 1:S + 1], best[:], dist[p][:, i, :], BIG, ALU.min, ALU.add)
                    ch.link(row)
                v.sem_inc(costed, 1)

            chunk(0, 0, False)
            ch.link(v.memset(cost[1][:, ROWS - 1, 0:1], BIG))
            chunk(0, 1, False)
            start = ch.n
            with v.Fori(1, NCH // 2) as h:
                ch.base = (h - 1) * (4 * ROWS)
                chunk(h, 0, True)
                chunk(h, 1, True)
            assert ch.n - start == 4 * ROWS


def path_phase(nc, io, scr, vin, vout):
    with ExitStack() as ctx:
        def sb(name, shape, dt=F32):
            return ctx.enter_context(nc.sbuf_tensor(name, shape, dt))

        def sem(name):
            return ctx.enter_context(nc.semaphore(name))

        W = S + 1
        cur = [sb(f"cur{p}", [P, T, W]) for p in range(2)]
        prv = [sb(f"prv{p}", [P, T, W]) for p in range(2)]
        m, dg, nl = sb("m", [P, T, S]), sb("dg", [P, T, S]), sb("nl", [P, T, S])
        hh = sb("hh", [P, T, S])
        last_ = sb("last_", [P, T, W])
        step = [sb(f"step{p}", [P, T, S]) for p in range(2)]
        iota = sb("iota", [P, T, S])
        ident = sb("ident2", [NB, NB])
        rows = [sb(f"rows_g{p}", [NB, ROWS, S]) for p in range(2)]
        hop = sb("hop", [NB, S])
        cell = sb("cell", [NB, ROWS + 1])
        path = sb("path", [NB, S + 1])
        ps = [ctx.enter_context(nc.psum_tensor(f"pp{r}", [P, 512], F32)) for r in range(4)]
        r_in = [sem(f"rr_in{p}") for p in range(2)]
        g_out = [sem(f"g_out{p}") for p in range(2)]
        g_in = [sem(f"g_in{p}") for p in range(2)]
        consts, used, pch, vch, held, ran, copied, stepped, turned, tick = (sem(n) for n in (
            "consts2", "cells_used", "pool_chain2", "v_chain2", "held", "ran", "path_cp", "stepped", "turned2", "sp_tick3"))
        ptick, gdone = sem("pool_tick3"), sem("chunk_used")
        block = ctx.enter_context(nc.Block())

        @block.sync
        def _(sp):
            def load(n, h, p):
                sp.dma_start(cur[p][:], scr["r"][n, 1:S + 1, :].rearrange("(t p) s -> p t s", p=P)).then_inc(r_in[p], 16)
                sp.dma_start(prv[p][:], scr["r"][n, 0:S, :].rearrange("(t p) s -> p t s", p=P)).then_inc(r_in[p], 16)

            def store(n, h, p):
                done(sp, stepped, n + 1, NB, tick)
                sp.dma_start(scr["g"].rearrange("(t p) b s -> p t b s", p=P)[:, :, n, :], step[p][:]).then_inc(g_out[p], 16)
            load(0, 0, 0)
            load(1, 0, 1)
            with sp.Fori(0, NB // 2 - 1) as h:
                for p in range(2):
                    store(2 * h + p, h, p)
                    done(sp, used, 2 * h + p + 1, NB, tick)
                    load(2 * h + p + 2, h + 1, p)
            store(NB - 2, 0, 0)
            store(NB - 1, 0, 1)
            for p in range(2):
                sp.wait_ge(g_out[p], 16 * NB // 2)
            dram_g = scr["g"].rearrange("i b s -> b i s")

            def rows_in(k, p):
                sp.dma_start(rows[p][:], dram_g[:, bass.ds((NCH - 1 - k) * ROWS, ROWS), :]).then_inc(g_in[p], 16)
            rows_in(0, 0)
            rows_in(1, 1)
            with sp.Fori(0, NCH // 2 - 1) as h:
                for p in range(2):
                    done(sp, gdone, 2 * h + p + 1, NCH, tick)
                    rows_in(2 * h + p + 2, p)

        @block.gpsimd
        def _(pool):
            pc = Chain(pool, pch)
            pc.link(pool.iota(iota[:], pattern=[[0, T], [1, S]], base=0, channel_multiplier=0,
                              allow_small_or_imprecise_dtypes=True))
            pc.link(pool.memset(ident[:], 0.0))
            pc.link(pool.affine_select(out=ident[:], in_=ident[:], compare_op=ALU.not_equal, fill=1.0,
                                       base=0, pattern=[[-1, NB]], channel_multiplier=1))
            pc.link(pool.memset(last_[:, :, 0:1], 0.0))
            pool.sem_inc(consts, 1)

            def seq(n, h, p, full):
                done(pool, ran, n + 1, NB, ptick)
                if full:
                    done(pool, g_out[p], 16 * h, 16 * NB, ptick)
                pool.tensor_tensor(step[p][:], last_[:, :, 1:W], last_[:, :, 0:S], ALU.subtract).then_inc(stepped, 1)
            seq(0, 0, 0, False)
            seq(1, 0, 1, False)
            with pool.Fori(1, NB // 2) as h:
                seq(2 * h, h, 0, True)
                seq(2 * h + 1, h, 1, True)

        @block.vector
        def _(v):
            ch = Chain(v, vch)
            v.wait_ge(consts, 1)

            def seq(n, h, p, full):
                v.wait_ge(r_in[p], 32 * (h + 1))
                c, r = cur[p], prv[p]
                ch.tick(v.tensor_tensor(m[:], r[:, :, 1:W], r[:, :, 0:S], ALU.min))
                ch.tick(v.tensor_tensor(dg[:], r[:, :, 0:S], r[:, :, 1:W], ALU.is_le))
                ch.hold()
                ch.tick(v.tensor_tensor(nl[:], m[:], c[:, :, 0:S], ALU.is_le))
                ch.tick(v.scalar_tensor_tensor(hh[:], dg[:], -0.75, iota[:], ALU.mult, ALU.add))
                ch.hold()
                v.sem_inc(used, 1)
                ch.link(v.tensor_tensor(hh[:], hh[:], nl[:], ALU.mult))
                if full:
                    v.wait_ge(stepped, n)
                for t in range(T):
                    last = v.tensor_tensor_scan(last_[:, t, 1:W], hh[:, t, :], hh[:, t, :], 0.0, ALU.max, ALU.max)
                last.then_inc(ran, 1)
            seq(0, 0, 0, False)
            seq(1, 0, 1, True)
            start = ch.n
            with v.Fori(1, NB // 2) as h:
                ch.base = (h - 1) * 10
                seq(2 * h, h, 0, True)
                seq(2 * h + 1, h, 1, True)
            assert ch.n - start == 10
            ch.base = (NB // 2 - 2) * 10

            ch.link(v.memset(path[:], 0.0))
            ch.link(v.memset(path[:, S:S + 1], float(S - 1)))
            ch.link(v.memset(cell[:, 0:1], float(S - 1)))

            def chunk(k, h, p):
                v.wait_ge(g_in[p], 16 * (h + 1))
                ch.link(v.tensor_copy(cell[:, ROWS:ROWS + 1], cell[:, 0:1]))
                for i in range(ROWS - 1, -1, -1):
                    ch.link(v.scalar_tensor_tensor(hop[:], iota[0:NB, 0, :], cell[:, i + 1:i + 2], rows[p][:, i, :],
                                                   ALU.is_le, ALU.mult, accum_out=cell[:, i:i + 1]))
                ch.link(v.tensor_copy(path[:, bass.ds((NCH - 1 - k) * ROWS, ROWS)], cell[:, 0:ROWS]))
                v.sem_inc(gdone, 1)
            start, base = ch.n, ch.base
            with v.Fori(0, NCH // 2) as h:
                ch.base = h * (2 * (ROWS + 2)) + base
                chunk(2 * h, h, 0)
                chunk(2 * h + 1, h, 1)
            assert ch.n - start == 2 * (ROWS + 2)
            ch.base = base + (NCH // 2 - 1) * 2 * (ROWS + 2)
            ch.link(v.memset(path[:, 0:1], 0.0))
            v.sem_inc(held, 1)
            for t in range(T):
                v.wait_ge(turned, 2 * t + 2)
                v.tensor_copy(vout[:, t, :], ps[2 * t][:, 0:NB]).then_inc(copied, 1)
                v.tensor_copy(vin[:, t, :], ps[2 * t + 1][:, 0:NB]).then_inc(copied, 1)
            v.wait_ge(copied, 2 * T)

        @block.tensor
        def _(pe):
            pe.wait_ge(consts, 1)
            pe.wait_ge(held, 1)
            for t in range(T):
                pe.transpose(ps[2 * t][:, 0:NB], path[:, t * P:t * P + P], ident[:]).then_inc(turned, 1)
                pe.transpose(ps[2 * t + 1][:, 0:NB], path[:, t * P + 1:t * P + P + 1], ident[:]).then_inc(turned, 1)


def last_layer_phase(nc, io, scr, vin, vout, out):
    with ExitStack() as ctx:
        def sb(name, shape, dt=F32):
            return ctx.enter_context(nc.sbuf_tensor(name, shape, dt))

        def sem(name):
            return ctx.enter_context(nc.semaphore(name))

        w1T, w2T = sb("w1T", [P, C, F], BF16), sb("w2T", [P, FT, D], BF16)
        identb, iota = sb("identb", [P, P], BF16), sb("iota3", [P, S])
        gates, wscale = sb("gates3", [P, 4]), sb("wscale", [P, 2])
        b1, b2 = sb("b1", [P, F]), sb("b2", [P, D])
        setup_last_weights(nc, io, dict(w1T=w1T, w2T=w2T, identb=identb, iota=iota, gates=gates, wscale=wscale,
                                        b1=b1, b2=b2))

        x2 = [sb(f"x2_{p}", [P, T, D]) for p in range(2)]
        cx = [sb(f"cx_{p}", [P, T, D]) for p in range(2)]
        before_, mask = sb("before_", [P, T, S]), sb("mask", [P, T, S])
        x3 = [sb(f"x3_{p}", [P, T, D]) for p in range(2)]
        xc, xr = sb("xc", [P, T, D]), sb("xr", [P, T, D])
        xq = sb("xq", [P, T, D], BF16)
        xqT = [sb(f"xqT{p}", [P, C, S], BF16) for p in range(2)]
        c1 = [sb(f"c1_{p}", [P, T]) for p in range(2)]
        small = sb("small", [P, 12])
        wk_ = {"st": sb("ln_st3", [P, T, 6]), "mv": sb("ln_mv3", [P, T, 2]), "v": sb("ln_v3", [P, T]),
               "y": sb("ln_y3", [P, T]), "a": sb("ln_a3", [P, T])}
        hb = [sb(f"hb{t}", [P, F]) for t in range(T)]
        gl = [sb(f"gl{t}", [P, F]) for t in range(T)]
        sq = sb("sq", [P, F])
        ssum = [sb(f"ssum{t}", [P, 1]) for t in range(T)]
        hr_ = [sb(f"hr{t}", [P, F]) for t in range(T)]
        hq = [sb(f"hq{t}", [P, F], BF16) for t in range(T)]
        hqT = [sb(f"hqT{t}", [P, FT, P], BF16) for t in range(T)]
        hs = [sb(f"hs{t}", [P, 6]) for t in range(T)]
        xo = [sb(f"xo{p}", [P, T, D]) for p in range(2)]
        x3b = [sb(f"x3b{p}", [P, T, D]) for p in range(2)]

        pe_x = ctx.enter_context(nc.psum_tensor("pe_x", [P, T, D], F32))
        pt_x = ctx.enter_context(nc.psum_tensor("pt_x", [P, C, S], BF16))
        ph = [ctx.enter_context(nc.psum_tensor(f"ph{t}", [P, F], F32)) for t in range(T)]
        pt_h = ctx.enter_context(nc.psum_tensor("pt_h", [P, FT, P], BF16))
        po = ctx.enter_context(nc.psum_tensor("po", [P, T, D], F32))

        names = ["expand", "xq_t", "h_mm", "hq_t", "o_mm",
                 "xqT_cp", "gelu", "squares", "hqT_cp", "x_round",
                 "masked", "x3_res", "x_scaled", "h_bias", "h_scaled", "x4_res",
                 "x3_bias", "h_round", "chain3", "tick_sp3", "tick_pool3"]
        e = {n: sem(n) for n in names}
        x_in = [sem(f"x2_in{p}") for p in range(2)]
        o_out = [sem(f"o_out{p}") for p in range(2)]
        block = ctx.enter_context(nc.Block())
        tok = "(t p) d -> p t d"

        def run(front, back, eng, chain=None):
            front(Batch(0, 0))
            front(Batch(0, 1))
            back(Batch(0, 0))
            before = chain.n if chain else 0
            front(Batch(1, 0))
            back(Batch(0, 1))
            front(Batch(1, 1))
            back(Batch(1, 0))
            start = chain.n if chain else 0
            step = start - before
            with eng.Fori(2, NB // 2) as h:
                if chain:
                    chain.base = (h - 2) * step
                front(Batch(h, 0))
                back(Batch(h - 1, 1))
                front(Batch(h, 1))
                back(Batch(h, 0))
            if chain:
                assert chain.n - start == step
                chain.base = (NB // 2 - 3) * step
            back(Batch(NB // 2 - 1, 1))

        @block.sync
        def _(sp):
            def w(s, count, most=NB):
                done(sp, s, count, most, e["tick_sp3"])

            def load(b):
                w(e["x3_res"], b.n - 1)
                sp.dma_start(x2[b.p][:], scr["x2"][b.n].rearrange(tok, p=P)).then_inc(x_in[b.p], 16)
                sp.dma_start(cx[b.p][:], io["ctx_1024"][b.n].rearrange(tok, p=P)).then_inc(x_in[b.p], 16)

            def store(b):
                w(e["x4_res"], 2 * (b.n + 1), 2 * NB)
                sp.dma_start(out[b.n].rearrange(tok, p=P), xo[b.p][:]).then_inc(o_out[b.p], 16)
            run(load, store, sp)
            for p in range(2):
                sp.wait_ge(o_out[p], 16 * NB // 2)

        @block.tensor
        def _(pe):
            def w(s, count, most=NB):
                done(pe, e[s] if isinstance(s, str) else s, count, most)

            def front(b):
                w("masked", b.n + 1), w("x3_res", b.n)
                w(x_in[b.p], 32 * (b.half + 1), 32 * NB)
                for j in range(T):
                    for t in range(T):
                        last = pe.matmul(pe_x[:, j, :], mask[:, t, j * P:j * P + P], cx[b.p][:, t, :],
                                         start=(t == 0), stop=(t == T - 1))
                last.then_inc(e["expand"], 1)
                w("x_round", b.n + 1), w("xqT_cp", b.n)
                for c in range(C):
                    for t in range(T):
                        last = pe.transpose(pt_x[:, c, t * P:t * P + P], xq[:, t, c * P:c * P + P], identb[:])
                last.then_inc(e["xq_t"], 1)

            def back(b):
                w("xqT_cp", b.n + 1)
                for t in range(T):
                    w("h_bias", 2 * b.n + t - 1, 2 * NB)
                    for j in range(2):
                        for c in range(C):
                            last = pe.matmul(ph[t][:, 512 * j:512 * j + 512], xqT[b.p][:, c, t * P:t * P + P],
                                             w1T[:, c, 512 * j:512 * j + 512], start=(c == 0), stop=(c == C - 1))
                    last.then_inc(e["h_mm"], 1)
                for t in range(T):
                    w("h_round", 2 * b.n + t + 1, 2 * NB), w("hqT_cp", 2 * b.n + t, 2 * NB)
                    for f in range(FT):
                        last = pe.transpose(pt_h[:, f, :], hq[t][:, f * P:f * P + P], identb[:])
                    last.then_inc(e["hq_t"], 1)
                for t in range(T):
                    w("hqT_cp", 2 * b.n + t + 1, 2 * NB)
                    w("x4_res", 2 * b.n + t, 2 * NB)
                    for f in range(FT):
                        last = pe.matmul(po[:, t, :], hqT[t][:, f, :], w2T[:, f, :], start=(f == 0), stop=(f == FT - 1))
                    last.then_inc(e["o_mm"], 1)
            run(front, back, pe)

        @block.scalar
        def _(act):
            def w(s, count, most=NB):
                done(act, e[s] if isinstance(s, str) else s, count, most)

            def front(b):
                w("x_scaled", b.n + 1), w("xq_t", b.n)
                act.activation(xq[:], xr[:], ACT.Copy, bias=-MAGIC).then_inc(e["x_round"], 1)
                w("xq_t", b.n + 1), w("h_mm", 2 * (b.n - 1), 2 * NB)
                act.activation(xqT[b.p][:], pt_x[:], ACT.Copy).then_inc(e["xqT_cp"], 1)

            def back(b):
                for t in range(T):
                    w("h_bias", 2 * b.n + t + 1, 2 * NB), w("h_scaled", 2 * b.n + t - 1, 2 * NB)
                    act.activation(gl[t][:], hb[t][:], ACT.Gelu).then_inc(e["gelu"], 1)
                    w("gelu", 2 * b.n + t + 1, 2 * NB), w("squares", 2 * b.n + t, 2 * NB)
                    act.activation(sq[:], gl[t][:], ACT.Square, accum_out=ssum[t][:]).then_inc(e["squares"], 1)
                for t in range(T):
                    w("hq_t", 2 * b.n + t + 1, 2 * NB), w("o_mm", 2 * b.n + t - 1, 2 * NB)
                    act.activation(hqT[t][:], pt_h[:], ACT.Copy).then_inc(e["hqT_cp"], 1)
            run(front, back, act)

        @block.gpsimd
        def _(pool):
            def w(s, count, most=NB):
                done(pool, e[s], count, most, e["tick_pool3"])

            def front(b):
                w("x3_res", b.n + 1), w("x4_res", 2 * (b.n - 1), 2 * NB)
                for t in range(T):
                    last = pool.tensor_tensor(x3b[b.p][:, t, :], x3[b.p][:, t, :], b2[:], ALU.add)
                last.then_inc(e["x3_bias"], 1)

            def back(b):
                for t in range(T):
                    w("h_scaled", 2 * b.n + t + 1, 2 * NB), w("hq_t", 2 * b.n + t - 1, 2 * NB)
                    pool.tensor_scalar(hq[t][:], hr_[t][:], -MAGIC, 1.0, ALU.add, ALU.mult).then_inc(e["h_round"], 1)
            run(front, back, pool)

        @block.vector
        def _(v):
            ch = Chain(v, e["chain3"])

            def w(s, count, most=NB):
                done(v, e[s] if isinstance(s, str) else s, count, most)

            def scale_and_inverse(amax, y, q, inv):
                ch.link(v.tensor_tensor(inv, amax, y, ALU.mult))
                ch.link(v.tensor_scalar(inv, inv, 1e-5, 1.0 / 127, ALU.max, ALU.mult))
                ch.link(v.reciprocal(q, inv))
                ch.link(v.tensor_tensor(q, q, y, ALU.mult))

            def front(b):
                for t in range(T):
                    row = vin[:, t, bass.ds(b.n, 1)], vout[:, t, bass.ds(b.n, 1)]
                    ch.tick(v.tensor_copy(small[:, t:t + 1], row[0]))
                    ch.tick(v.tensor_copy(small[:, 2 + t:3 + t], row[1]))
                ch.hold()
                w("expand", b.n)
                for t in range(T):
                    ch.tick(v.tensor_scalar(before_[:, t, :], iota[:], small[:, t:t + 1], None, ALU.is_le))
                ch.hold()
                for t in range(T):
                    last = v.scalar_tensor_tensor(mask[:, t, :], iota[:], small[:, 2 + t:3 + t], before_[:, t, :],
                                                  ALU.is_ge, ALU.mult)
                last.then_inc(e["masked"], 1)
                w("expand", b.n + 1), w("x3_bias", b.n - 1)
                w(x_in[b.p], 32 * (b.half + 1), 32 * NB)
                v.scalar_tensor_tensor(x3[b.p][:], pe_x[:], gates[:, 1:2], x2[b.p][:], ALU.mult, ALU.add)\
                    .then_inc(e["x3_res"], 1)
                w("x3_res", b.n + 1)
                layer_stats(v, ch, x3[b.p], wk_)
                ms, y2 = small[:, 4:6], small[:, 6:8]
                ch.link(v.tensor_tensor(ms, wk_["y"][:], wk_["y"][:], ALU.mult))
                ch.link(v.tensor_tensor(ms, ms, wk_["mv"][:, :, 1], ALU.mult))
                ch.link(v.tensor_scalar(ms, ms, EPS, None, ALU.add))
                newton_rsqrt(v, ch, ms, y2, wk_["a"][:])
                ch.link(v.tensor_tensor(y2, y2, wk_["y"][:], ALU.mult))
                for t in range(T):
                    ch.tick(v.tensor_scalar(xc[:, t, :], x3[b.p][:, t, :], wk_["mv"][:, t, 0:1], None, ALU.subtract))
                ch.hold()
                ch.link(v.tensor_reduce(ms, xc[:], AX.X, ALU.max, apply_absolute_value=True))
                w("h_bias", 2 * (b.n - 1), 2 * NB)
                q = small[:, 8:10]
                scale_and_inverse(ms, y2, q, c1[b.p][:])
                ch.link(v.tensor_scalar(c1[b.p][:], c1[b.p][:], wscale[:, 0:1], None, ALU.mult))
                w("x_round", b.n)
                for t in range(T):
                    last = v.tensor_scalar(xr[:, t, :], xc[:, t, :], q[:, t:t + 1], MAGIC, ALU.mult, ALU.add)
                last.then_inc(e["x_scaled"], 1)

            def back(b):
                for t in range(T):
                    w("h_mm", 2 * b.n + t + 1, 2 * NB), w("gelu", 2 * b.n + t - 1, 2 * NB)
                    v.scalar_tensor_tensor(hb[t][:], ph[t][:], c1[b.p][:, t:t + 1], b1[:], ALU.mult, ALU.add)\
                        .then_inc(e["h_bias"], 1)
                for t in range(T):
                    k = hs[t]
                    w("gelu", 2 * b.n + t + 1, 2 * NB)
                    ch.tick(v.tensor_reduce(k[:, 0:1], gl[t][:], AX.X, ALU.max, apply_absolute_value=True))
                    w("squares", 2 * b.n + t + 1, 2 * NB)
                    ch.tick(v.tensor_scalar(k[:, 1:2], ssum[t][:], 1.0 / F, EPS, ALU.mult, ALU.add))
                    ch.hold()
                    newton_rsqrt(v, ch, k[:, 1:2], k[:, 2:3], k[:, 3:4])
                    scale_and_inverse(k[:, 0:1], k[:, 2:3], k[:, 4:5], k[:, 5:6])
                    w("h_round", 2 * b.n + t - 1, 2 * NB)
                    v.tensor_scalar(hr_[t][:], gl[t][:], k[:, 4:5], MAGIC, ALU.mult, ALU.add).then_inc(e["h_scaled"], 1)
                    ch.link(v.tensor_scalar(k[:, 5:6], k[:, 5:6], wscale[:, 1:2], None, ALU.mult))
                w("x3_bias", b.n + 1), w(o_out[b.p], 16 * b.half, 16 * NB)
                for t in range(T):
                    w("o_mm", 2 * b.n + t + 1, 2 * NB)
                    v.scalar_tensor_tensor(xo[b.p][:, t, :], po[:, t, :], hs[t][:, 5:6], x3b[b.p][:, t, :], ALU.mult, ALU.add)\
                        .then_inc(e["x4_res"], 1)
            run(front, back, v, ch)


def setup_last_weights(nc, io, o):
    with ExitStack() as ctx:
        def sb(name, shape, dt=F32):
            return ctx.enter_context(nc.sbuf_tensor(name, shape, dt))

        def sem(name):
            return ctx.enter_context(nc.semaphore(name))

        w1, w2 = sb("w1", [P, FT, D]), sb("w2", [P, C, F])
        w1b, w2b = sb("w1b", [P, FT, D], BF16), sb("w2b", [P, C, F], BF16)
        gin, ones = sb("gin3", [P, 4]), sb("ones3", [P, P])
        part, scl, rsc = sb("part", [P, 2]), sb("scl3", [P, 2]), sb("rsc3", [P, 2])
        ps = [ctx.enter_context(nc.psum_tensor(f"sl{r}", [P, P], BF16)) for r in range(2)]
        tot = ctx.enter_context(nc.psum_tensor("tot", [P, 512], F32))
        loaded, consts, summed, totals, quant, turned, copied, tanhd, vch, pch = (sem(n) for n in (
            "l_loaded", "l_consts", "l_summed", "l_totals", "l_quant", "l_turned", "l_copied", "l_tanh", "l_chain",
            "l_pchain"))
        block = ctx.enter_context(nc.Block())

        @block.sync
        def _(sp):
            sp.dma_start(w1[:], io["L1_ffn_w1"].rearrange("(a p) d -> p a d", p=P)).then_inc(loaded, 16)
            sp.dma_start(w2[:], io["L1_ffn_w2"].rearrange("(a p) f -> p a f", p=P)).then_inc(loaded, 16)
            sp.dma_start(o["b1"][:], io["L1_ffn_b1"].partition_broadcast(P)).then_inc(loaded, 16)
            sp.dma_start(o["b2"][:], io["L1_ffn_b2"].partition_broadcast(P)).then_inc(loaded, 16)
            sp.dma_start(gin[:, 0:2], io["g_xattn"].partition_broadcast(P)).then_inc(loaded, 16)
            sp.dma_start(gin[:, 2:4], io["g_ffn"].partition_broadcast(P)).then_inc(loaded, 16)
            sp.wait_ge(loaded, 96)

        @block.gpsimd
        def _(pool):
            pc = Chain(pool, pch)
            pc.link(pool.memset(ones[:], 1.0))
            pc.link(pool.memset(o["identb"][:], 0.0))
            pc.link(pool.affine_select(out=o["identb"][:], in_=o["identb"][:], compare_op=ALU.not_equal, fill=1.0,
                                       base=0, pattern=[[-1, P]], channel_multiplier=1))
            pc.link(pool.iota(o["iota"][:], pattern=[[1, S]], base=0, channel_multiplier=0,
                              allow_small_or_imprecise_dtypes=True))
            pool.sem_inc(consts, 1)

        @block.scalar
        def _(act):
            act.wait_ge(loaded, 96)
            act.activation(o["gates"][:], gin[:], ACT.Tanh).then_inc(tanhd, 1)
            act.wait_ge(tanhd, 1)

        jobs = [(w1b[:, f, c * P:c * P + P], o["w1T"][:, c, f * P:f * P + P]) for f in range(FT) for c in range(C)]
        jobs += [(w2b[:, a, f * P:f * P + P], o["w2T"][:, f, a * P:a * P + P]) for a in range(C) for f in range(FT)]

        @block.vector
        def _(v):
            ch = Chain(v, vch)
            v.wait_ge(loaded, 96)
            ch.tick(v.tensor_reduce(part[:, 0:1], w1[:], AX.XY, ALU.add, apply_absolute_value=True))
            ch.link(v.tensor_reduce(part[:, 1:2], w2[:], AX.XY, ALU.add, apply_absolute_value=True))
            v.sem_inc(summed, 1)
            v.wait_ge(totals, 1)
            ch.link(v.tensor_scalar(scl[:], tot[:, 0:2], 1.0 / (D * F), 1e-5, ALU.mult, ALU.max))
            ch.link(v.reciprocal(rsc[:], scl[:]))
            for k, (w_, b_) in enumerate(((w1, w1b), (w2, w2b))):
                ch.link(v.tensor_scalar(w_[:], w_[:], rsc[:, k:k + 1], MAGIC, ALU.mult, ALU.add))
                ch.link(v.tensor_scalar(w_[:], w_[:], MAGIC, 1.0, ALU.subtract, ALU.min))
                ch.link(v.tensor_scalar(b_[:], w_[:], -1.0, None, ALU.max))
            v.sem_inc(quant, 1)
            v.wait_ge(tanhd, 1)
            ch.link(v.tensor_copy(o["wscale"][:, 0:1], scl[:, 0:1]))
            ch.link(v.tensor_tensor(o["wscale"][:, 1:2], scl[:, 1:2], o["gates"][:, 3:4], ALU.mult))
            ch.link(v.tensor_scalar(o["b2"][:], o["b2"][:], o["gates"][:, 3:4], None, ALU.mult))
            for k, (_, dst) in enumerate(jobs):
                v.wait_ge(turned, k + 1)
                v.tensor_copy(dst, ps[k % 2][:]).then_inc(copied, 1)
            v.wait_ge(copied, len(jobs))

        @block.tensor
        def _(pe):
            pe.wait_ge(consts, 1)
            pe.wait_ge(summed, 1)
            pe.matmul(tot[:, 0:2], ones[:], part[:], start=True, stop=True).then_inc(totals, 1)
            pe.wait_ge(quant, 1)
            for k, (src, _) in enumerate(jobs):
                if k >= 2:
                    pe.wait_ge(copied, k - 1)
                pe.transpose(ps[k % 2][:], src, o["identb"][:]).then_inc(turned, 1)


def build(nc, io, out):
    scr = {
        "q": nc.dram_tensor("q_parts_dram", (3, D, S), BF16).ap(),
        "k": nc.dram_tensor("k_parts_dram", (3, D, S), BF16).ap(),
        "x2": nc.dram_tensor("x2_dram", (NB, S, D), F32).ap(),
        "d": nc.dram_tensor("dist_dram", (S, NB, S), F32).ap(),
        "r": nc.dram_tensor("cost_dram", (NB, S + 1, S + 1), F32).ap(),
        "g": nc.dram_tensor("step_dram", (S, NB, S), F32).ap(),
    }
    attention_phase(nc, io, scr)
    with nc.sbuf_tensor("vin", [P, T, NB], F32) as vin, nc.sbuf_tensor("vout", [P, T, NB], F32) as vout:
        alignment_phase(nc, io, scr)
        path_phase(nc, io, scr, vin, vout)
        last_layer_phase(nc, io, scr, vin, vout, out)


_INS = ['x', 'ctx_1024', 'g_xattn', 'g_ffn', 'L0_xattn_wq', 'L0_xattn_wk', 'L0_xattn_wv', 'L0_xattn_wo',
        'L0_ffn_fast_b', 'L0_ffn_w_fc', 'L0_ffn_w_proj', 'L0_ffn_u', 'L0_ffn_v', 'L0_ffn_gate',
        'L1_ffn_w1', 'L1_ffn_b1', 'L1_ffn_w2', 'L1_ffn_b2']


def kernel(**inputs):
    import numpy as _np
    import concourse.bacc as _bacc
    from concourse import mybir as _mybir
    from concourse.bass_utils import run_bass_kernel_spmd as _run

    nc = _bacc.Bacc("TRN2", target_bir_lowering=False, num_devices=1)
    arrays, io = {}, {}
    for name in _INS:
        a = _np.ascontiguousarray(inputs[name])
        if name == 'L0_ffn_gate':
            a = a.reshape(1)
        arrays[f"in_{name}_dram"] = a
        io[name] = nc.dram_tensor(f"in_{name}_dram", a.shape, _mybir.dt.from_np(a.dtype), kind="ExternalInput").ap()
    out = nc.dram_tensor("out_0_dram", (NB, S, D), F32, kind="ExternalOutput").ap()
    build(nc, io, out)
    r = _run(nc, [arrays], core_ids=[0])
    return r.results[0]["out_0_dram"]
```

```python
from contextlib import ExitStack

import numpy as np
import concourse.bass as bass
from concourse import mybir

F32 = mybir.dt.float32
BF16 = mybir.dt.bfloat16
I32 = mybir.dt.int32
ALU = mybir.AluOpType
ACT = mybir.ActivationFunctionType
AX = mybir.AxisListType

P = 128
NB, S, D = 32, 256, 256
NH, DH = 16, 16
F = 1024
RANK = 16
T = S // P
C = D // P
FT = F // P
EPS = 1e-5
BIG = 3.0e38
MAGIC = 12582912.0
RSQRT_SEED = float(0x5F3759DF)

GROUPS = [(0, 6), (6, 6), (12, 4)]
SUMROW = 96
NPAIR = 8

Q_PARTS = [0, 1, 0, 1, 2, 0]
K_PARTS = [0, 0, 1, 1, 0, 2]
MAXROW = DH * len(Q_PARTS)

ROWS = 16
NCH = S // ROWS


class Batch:

    def __init__(self, half, p):
        self.half, self.p = half, p
        self.n = 2 * half + p

    def off(self, k):
        k += self.p
        return Batch(self.half + k // 2, k % 2)


def done(eng, sem, count, most, tick=None):
    if isinstance(count, int):
        if count <= 0:
            return
        count = min(count, most)
        eng.wait_ge(sem, count)
        return
    eng.wait_ge(sem, count)
    if tick is not None:
        eng.sem_inc(tick, 1)


class Chain:

    def __init__(self, eng, sem):
        self.eng, self.sem, self.base, self.n = eng, sem, 0, 0

    def tick(self, ins):
        self.n += 1
        ins.then_inc(self.sem, 1)

    def link(self, ins):
        self.tick(ins)
        self.hold()

    def hold(self):
        self.eng.wait_ge(self.sem, self.base + self.n)

    def tick_event(self):
        self.n += 1
        self.eng.sem_inc(self.sem, 1)


def layer_stats(v, ch, src, w, n=T):
    for t in range(n):
        ch.tick(v.bn_stats(w["st"][:, t, :], src[:, t, :]))
    ch.hold()
    ch.tick_event()
    for t in range(n):
        ch.tick(v.bn_aggr(w["mv"][:, t, :], w["st"][:, t, :]))
    ch.hold()
    ch.link(v.tensor_scalar(w["v"][:, 0:n], w["mv"][:, 0:n, 1], EPS, None, ALU.add))
    newton_rsqrt(v, ch, w["v"][:, 0:n], w["y"][:, 0:n], w["a"][:, 0:n])


def newton_rsqrt(v, ch, x, y, a):
    ch.link(v.tensor_scalar(y.bitcast(I32), x.bitcast(I32), -0.5, RSQRT_SEED, ALU.mult, ALU.add))
    for _ in range(3):
        ch.link(v.scalar_tensor_tensor(a, y, -0.5, y, ALU.mult, ALU.mult))
        ch.link(v.tensor_tensor(a, a, x, ALU.mult))
        ch.link(v.scalar_tensor_tensor(y, a, 1.5, y, ALU.add, ALU.mult))


def attention_phase(nc, io, scr):
    with ExitStack() as ctx:
        def sb(name, shape, dt=F32):
            return ctx.enter_context(nc.sbuf_tensor(name, shape, dt))

        def sem(name):
            return ctx.enter_context(nc.semaphore(name))

        wqT, wkT, wvT = sb("wqT", [P, C, D]), sb("wkT", [P, C, D]), sb("wvT", [P, C, D])
        woT = sb("woT", [P, len(GROUPS), D])
        wfcT = sb("wfcT", [P, C, F])
        wprT = sb("wprT", [P, FT, D])
        ident = sb("ident", [P, P])
        ones = sb("ones", [P, P])
        sel = sb("sel", [P, P])
        gates = sb("gates", [P, 4])
        xin = [sb(f"xin{p}", [P, T, D]) for p in range(2)]
        cin = [sb(f"cin{p}", [P, T, D]) for p in range(2)]
        xres = [sb(f"xres{p}", [P, T, D]) for p in range(2)]
        xhat, xT = sb("xhat", [P, T, D]), sb("xT", [P, C, S])
        cT = [sb(f"cT{p}", [P, C, S]) for p in range(2)]
        cD = sb("cD", [P, C, S])
        qp, kp = sb("qp", [P, 3, C, S], BF16), sb("kp", [P, 3, C, S], BF16)
        qr, kr = sb("qr", [P, C, S]), sb("kr", [P, C, S])
        qst = [sb(f"qst{p}", [P, NH, S], BF16) for p in range(2)]
        kst = [sb(f"kst{p}", [P, NH, S], BF16) for p in range(2)]
        vw = [sb(f"vw{p}", [P, T, NH, P]) for p in range(2)]
        nmax = sb("nmax", [P, 2 * NH])
        nsp = sb("nsp", [2 * NH, 2, P], BF16)
        pt = [sb(f"pt{r}", [P, 4, S]) for r in range(2)]
        osb, on = sb("osb", [P, len(GROUPS), S]), sb("on", [P, len(GROUPS), S])
        rc = sb("rc", [P, len(GROUPS), S])
        x1, xh2, x2T = sb("x1", [P, T, D]), sb("xh2", [P, T, D]), sb("x2T", [P, C, S])
        rl = sb("rl", [P, 2, 2, S])
        r2 = sb("r2", [P, FT, S])
        x2 = sb("x2", [P, T, D])
        yn, yT, ysq = sb("yn", [P, T, D]), sb("yT", [P, C, S]), sb("ysq", [P, C, S])
        bbs, dt_, dd = sb("bbs", [P, S]), sb("dt_", [P, T, S]), sb("dd", [P, T, S])
        aa = [sb(f"aa{p}", [P, T]) for p in range(2)]
        aaD = sb("aaD", [P, T])
        junk = sb("junk", [P, D])
        wk_ = {"st": sb("ln_st", [P, T, 6]), "mv": sb("ln_mv", [P, T, 2]), "v": sb("ln_v", [P, T]),
               "y": sb("ln_y", [P, T]), "a": sb("ln_a", [P, T])}

        setup_weights(nc, io, dict(wqT=wqT, wkT=wkT, wvT=wvT, woT=woT, wfcT=wfcT, wprT=wprT, ident=ident,
                                   ones=ones, sel=sel, gates=gates, vw=vw, qst=qst, kst=kst, rc=rc))

        sc = [ctx.enter_context(nc.psum_tensor(f"sc{r}", [P, 4, S], F32)) for r in range(2)]
        oacc = ctx.enter_context(nc.psum_tensor("oacc", [P, 2, S], F32))
        wb = [ctx.enter_context(nc.psum_tensor(f"wb{r}", [P, 2, S], F32)) for r in range(3)]

        names = ["xhat_t", "ctx_t", "q_mm", "k_mm", "v_mm", "max_t", "sum_bc01", "sum_bc2", "wo_mm", "xh2_t",
                 "fc_mm", "pr_mm", "y_t", "bb_mm", "ab_mm", "s1_mm", "s2_mm", "av_mm",
                 "xT_cp", "cT_cp", "qh_cp", "kh_cp", "vw_cp", "x2T_cp", "relu", "expd", "o_cp", "yT_cp", "bb_cp",
                 "dist", "aa_half", "aa_sum",
                 "ln1", "q_rem", "k_rem", "maxed", "max_split", "recip", "normed", "x1_res", "ln2", "x2_res", "ln3",
                 "d_part",
                 "q_parts_mid", "k_parts_mid", "q_parts", "k_parts", "squared", "y_sq", "maxrow_zero", "cD_cp",
                 "q_out", "k_out", "max_in", "x2_out", "d_out", "vchain", "sp_tick", "pool_tick"]
        e = {n: sem(n) for n in names}
        x_in = [sem(f"x_in{p}") for p in range(2)]
        c_in = [sem(f"c_in{p}") for p in range(2)]
        xr_in = [sem(f"xr_in{p}") for p in range(2)]
        q_in = [sem(f"q_in{p}") for p in range(2)]
        k_in = [sem(f"k_in{p}") for p in range(2)]
        NQ = len(Q_PARTS)

        tok = "(t p) d -> p t d"
        x_d, c_d = io["x"], io["ctx_1024"]
        block = ctx.enter_context(nc.Block())

        def run(iteration, eng, chain=None):
            iteration(Batch(-1, 1))
            iteration(Batch(0, 0))
            before = chain.n if chain else 0
            iteration(Batch(0, 1))
            step = 2 * (chain.n - before) if chain else 0
            start = chain.n if chain else 0
            with eng.Fori(1, NB // 2 - 1) as h:
                if chain:
                    chain.base = (h - 1) * step
                iteration(Batch(h, 0))
                iteration(Batch(h, 1))
            if chain:
                assert chain.n - start == step
                chain.base = (NB // 2 - 3) * step
            iteration(Batch(NB // 2 - 1, 0))
            iteration(Batch(NB // 2 - 1, 1))
            iteration(Batch(NB // 2, 0))

        def there(b):
            return not isinstance(b.n, int) or 0 <= b.n < NB

        @block.sync
        def _(sp):
            def w(s, count, most=NB):
                done(sp, s, count, most, e["sp_tick"])

            def load_x_ctx(b):
                w(e["ln1"], b.n - 1)
                sp.dma_start(xin[b.p][:], x_d[b.n].rearrange(tok, p=P)).then_inc(x_in[b.p], 16)
                w(e["ctx_t"], b.n - 1)
                w(e["aa_sum"], b.n - 1)
                sp.dma_start(cin[b.p][:], c_d[b.n].rearrange(tok, p=P)).then_inc(c_in[b.p], 16)

            def load_res(b):
                w(e["x1_res"], b.n - 1)
                sp.dma_start(xres[b.p][:], x_d[b.n].rearrange(tok, p=P)).then_inc(xr_in[b.p], 16)

            def restack(b):
                for parts, made, out, dram, st, inn, order in (
                        (qp, "q_parts", "q_out", scr["q"], qst, q_in, Q_PARTS),
                        (kp, "k_parts", "k_out", scr["k"], kst, k_in, K_PARTS)):
                    w(e[made], b.n + 1)
                    w(inn[1 - b.p], 16 * NQ * (b.off(-1).half + 1), 16 * NQ * NB)
                    sp.dma_start(dram.rearrange("a (m p) t -> p (a m) t", p=P),
                                 parts[:].rearrange("p a m t -> p (a m) t")).then_inc(e[out], 16)
                for out, dram, st, inn, order in (("q_out", scr["q"], qst, q_in, Q_PARTS),
                                                  ("k_out", scr["k"], kst, k_in, K_PARTS)):
                    w(e["s2_mm"], NPAIR * (b.n - 1), NPAIR * NB)
                    w(e[out], 16 * (b.n + 1), 16 * NB)
                    for blk, part in enumerate(order):
                        sp.dma_start(st[b.p][DH * blk:DH * blk + DH, :, :],
                                     dram[part].rearrange("(h r) t -> r h t", r=DH)).then_inc(inn[b.p], 16)

            def max_rows(b):
                w(e["max_split"], b.n + 1)
                w(e["s1_mm"], NPAIR * (b.n + 1), NPAIR * NB)
                for part in range(2):
                    sp.dma_start(qst[b.p][MAXROW + part:MAXROW + part + 1, :, :].rearrange("o h (a t) -> o (h a) t", t=P),
                                 nsp[:, part:part + 1, :].rearrange("m o t -> m o t")).then_inc(e["max_in"], 16)

            def store_x2(b):
                w(e["x2_res"], b.n + 1)
                sp.dma_start(scr["x2"][b.n].rearrange(tok, p=P), x2[:]).then_inc(e["x2_out"], 16)

            def store_d(b):
                w(e["dist"], b.n + 1)
                sp.dma_start(scr["d"].rearrange("(t p) b s -> p t b s", p=P)[:, :, b.n, :], dd[:])\
                    .then_inc(e["d_out"], 16)

            load_x_ctx(Batch(0, 0))

            def iteration(i):
                if there(i.off(2)):
                    load_x_ctx(i.off(2))
                if there(i):
                    load_res(i)
                if there(i.off(1)):
                    restack(i.off(1))
                if there(i):
                    max_rows(i)
                if there(i.off(-1)):
                    store_x2(i.off(-1))
                    store_d(i.off(-1))
            run(iteration, sp)
            sp.wait_ge(e["x2_out"], 16 * NB)
            sp.wait_ge(e["d_out"], 16 * NB)

        @block.tensor
        def _(pe):
            def w(s, count, most=NB):
                done(pe, e[s] if isinstance(s, str) else s, count, most)

            def transposes(dst, src):
                for c in range(C):
                    for t in range(T):
                        last = pe.transpose(dst[:, c, t * P:t * P + P], src[:, t, c * P:c * P + P], ident[:])
                return last

            def turn_x(b):
                w("ln1", b.n + 1)
                w("yT_cp", b.n - 2)
                w("qh_cp", b.n), w("q_rem", b.n)
                transposes(wb[0], xhat).then_inc(e["xhat_t"], 1)

            def turn_ctx(b):
                w(c_in[b.p], 16 * (b.half + 1), 16 * NB)
                w("bb_cp", b.n - 2), w("vw_cp", b.n), w("max_split", b.n - 1)
                transposes(wb[1], cin[b.p]).then_inc(e["ctx_t"], 1)

            def project(b, wt, src, bank, s):
                for m in range(C):
                    for c in range(C):
                        last = pe.matmul(wb[bank][:, m, :], wt[:, c, m * P:m * P + P], src[:, c, :],
                                         start=(c == 0), stop=(c == C - 1))
                last.then_inc(e[s], 1)

            def keys(b):
                w("cT_cp", b.n + 1)
                project(b, wkT, cT[b.p], 1, "k_mm")

            def queries(b):
                w("xT_cp", b.n + 1)
                w("normed", b.n - 1)
                project(b, wqT, xT, 0, "q_mm")

            def values_proj(b):
                w("kh_cp", b.n + 1), w("k_rem", b.n + 1)
                for t in range(T):
                    for c in range(C):
                        last = pe.matmul(wb[1][:, t, :], cT[b.p][:, c, t * P:t * P + P], wvT[:, c, :],
                                         start=(c == 0), stop=(c == C - 1))
                last.then_inc(e["v_mm"], 1)

            def sums01(b):
                w("recip", 3 * b.n + 2, 3 * NB)
                w("d_part", b.n)
                for g in range(2):
                    last = pe.matmul(wb[2][:, g, :], sel[:], rc[:, g, :], start=True, stop=True)
                last.then_inc(e["sum_bc01"], 1)

            def sums2(b):
                w("recip", 3 * b.n + 3, 3 * NB)
                w("xT_cp", b.n + 3), w("yT_cp", b.n)
                pe.matmul(wb[0][:, 0, :], sel[:], rc[:, 2, :], start=True, stop=True).then_inc(e["sum_bc2"], 1)

            def out_proj(b):
                w("normed", b.n + 1)
                for t in range(T):
                    for g in range(len(GROUPS)):
                        last = pe.matmul(wb[2][:, t, :], on[:, g, t * P:t * P + P], woT[:, g, :],
                                         start=(g == 0), stop=(g == len(GROUPS) - 1))
                last.then_inc(e["wo_mm"], 1)

            def scores1(b, c):
                if c < 2:
                    w("expd", NPAIR * b.n + c - 1, NPAIR * NB)
                else:
                    w("maxed", NPAIR * b.n + c - 1, NPAIR * NB)
                if c == 0:
                    w(q_in[b.p], 16 * NQ * (b.half + 1), 16 * NQ * NB)
                    w(k_in[b.p], 16 * NQ * (b.half + 1), 16 * NQ * NB)
                    w("maxrow_zero", b.n - 1)
                for u in range(4):
                    h, t = 2 * c + u // 2, u % 2
                    last = pe.matmul(sc[c % 2][:, u, :], qst[b.p][:, h, t * P:t * P + P], kst[b.p][:, h, :],
                                     start=True, stop=True)
                last.then_inc(e["s1_mm"], 1)

            def max_transpose(b):
                w("maxed", NPAIR * (b.n + 1), NPAIR * NB)
                w("relu", 4 * (b.n - 1) + 2, 4 * NB), w("vw_cp", b.n + 2)
                pe.transpose(wb[1][0:2 * NH, 0, 0:P], nmax[:], ident[:]).then_inc(e["max_t"], 1)

            def scores2(b, c):
                if c < 2:
                    w("maxed", NPAIR * b.n + NPAIR - 1 + c, NPAIR * NB)
                else:
                    w("expd", NPAIR * b.n + c - 1, NPAIR * NB)
                if c == 0:
                    w("max_in", 32 * (b.n + 1), 32 * NB)
                for u in range(4):
                    h, t = 2 * c + u // 2, u % 2
                    last = pe.matmul(sc[c % 2][:, u, :], kst[b.p][:, h, t * P:t * P + P], qst[b.p][:, h, :],
                                     start=True, stop=True)
                last.then_inc(e["s2_mm"], 1)

            def values(b, c):
                w("expd", NPAIR * b.n + c + 1, NPAIR * NB)
                if c == 0:
                    w("vw_cp", b.n + 1)
                for u in range(2):
                    h = 2 * c + u
                    g = [k for k, (h0, n) in enumerate(GROUPS) if h0 <= h < h0 + n][0]
                    h0, n = GROUPS[g]
                    if h == h0:
                        w("o_cp", 3 * b.n + g, 3 * NB)
                    for t in range(T):
                        last = pe.matmul(oacc[:, g % 2, :], vw[b.p][:, t, h, :], pt[c % 2][:, 2 * u + t, :],
                                         start=(h == h0 and t == 0), stop=(h == h0 + n - 1 and t == T - 1))
                last.then_inc(e["av_mm"], 1)

            def xh2_transposes(b):
                w("ln2", b.n + 1)
                w("x1_res", b.n + 1)
                transposes(wb[2], xh2).then_inc(e["xh2_t"], 1)

            def fc(b, k):
                bank = (0, 1, 2, 0)[k]
                if k == 0:
                    w("x2T_cp", b.n + 1)
                    w("qh_cp", b.n + 3), w("q_rem", b.n + 3), w("normed", b.n + 1)
                elif k == 1:
                    w("vw_cp", b.n + 3), w("bb_cp", b.n)
                elif k == 3:
                    w("relu", 4 * b.n + 1, 4 * NB)
                for j in range(2):
                    f = 2 * k + j
                    for c in range(C):
                        last = pe.matmul(wb[bank][:, j, :], wfcT[:, c, f * P:f * P + P], x2T[:, c, :],
                                         start=(c == 0), stop=(c == C - 1))
                last.then_inc(e["fc_mm"], 1)

            def proj(b, t):
                if t == 0:
                    w("relu", 4 * b.n + 3, 4 * NB)
                    w("squared", 4 * (b.n + 1), 4 * NB)
                for f in range(FT):
                    last = pe.matmul(wb[2][:, t, :], r2[:, f, t * P:t * P + P], wprT[:, f, :],
                                     start=(f == 0), stop=(f == FT - 1))
                if t == T - 1:
                    last.then_inc(e["pr_mm"], 1)

            def y_transposes(b):
                w("ln3", b.n + 1)
                w("relu", 4 * (b.n + 1), 4 * NB)
                transposes(wb[0], yn).then_inc(e["y_t"], 1)

            def row_norms(b):
                w("y_sq", b.n + 1)
                w("max_split", b.n + 2), w("relu", 4 * b.n + 2, 4 * NB)
                for c in range(C):
                    last = pe.matmul(wb[1][:, 0, :], ones[:], ysq[:, c, :], start=(c == 0), stop=(c == C - 1))
                last.then_inc(e["bb_mm"], 1)

            def products(b):
                w("yT_cp", b.n + 1), w("cD_cp", b.n + 1)
                w("x2_res", b.n + 1)
                for t in range(T):
                    for c in range(C):
                        last = pe.matmul(wb[2][:, t, :], cD[:, c, t * P:t * P + P], yT[:, c, :],
                                         start=(c == 0), stop=(c == C - 1))
                last.then_inc(e["ab_mm"], 1)

            def iteration(i):
                a, z = i.off(1), i.off(-1)
                if there(a):
                    turn_x(a)
                    turn_ctx(a)
                if there(z):
                    sums01(z)
                    sums2(z)
                if there(a):
                    keys(a)
                if there(z):
                    out_proj(z)
                if there(a):
                    queries(a)
                    values_proj(a)
                if there(i):
                    scores1(i, 0)
                    scores1(i, 1)
                if there(z):
                    xh2_transposes(z)
                for k in range(4):
                    if there(z):
                        fc(z, k)
                    if there(i) and k < 2:
                        scores1(i, 2 * k + 2)
                        scores1(i, 2 * k + 3)
                if there(i):
                    scores1(i, 6)
                    scores1(i, 7)
                if there(z):
                    proj(z, 0)
                if there(i):
                    max_transpose(i)
                if there(z):
                    proj(z, 1)
                for c in range(NPAIR + 1):
                    if there(i):
                        if c < NPAIR:
                            scores2(i, c)
                        if c >= 1:
                            values(i, c - 1)
                    if there(z):
                        if c == 2:
                            y_transposes(z)
                        if c == 3:
                            row_norms(z)
                        if c == 5:
                            products(z)
            run(iteration, pe)

        @block.scalar
        def _(act):
            def w(s, count, most=NB):
                done(act, e[s] if isinstance(s, str) else s, count, most)

            def copy_group(b, g):
                h0, n = GROUPS[g]
                w("av_mm", NPAIR * b.n + (h0 + n - 1) // 2 + 1, NPAIR * NB)
                if g == 0:
                    w("normed", b.n)
                act.activation(osb[:, g, :], oacc[:, g % 2, :], ACT.Copy).then_inc(e["o_cp"], 1)

            def before(b):
                w("xhat_t", b.n + 1), w("q_mm", b.n)
                act.activation(xT[:], wb[0][:], ACT.Copy).then_inc(e["xT_cp"], 1)
                w("ctx_t", b.n + 1), w("cD_cp", b.n - 1), w("v_mm", b.n - 1)
                act.activation(cT[b.p][:], wb[1][:], ACT.Copy).then_inc(e["cT_cp"], 1)
                w("k_mm", b.n + 1), w("k_out", 16 * b.n, 16 * NB)
                act.activation(kp[:, 0, :, :], wb[1][:], ACT.Copy).then_inc(e["kh_cp"], 1)
                w("q_mm", b.n + 1), w("q_out", 16 * b.n, 16 * NB)
                act.activation(qp[:, 0, :, :], wb[0][:], ACT.Copy, scale=1.0 / 16).then_inc(e["qh_cp"], 1)
                w("v_mm", b.n + 1), w("av_mm", NPAIR * (b.n - 1), NPAIR * NB)
                for g, (h0, n) in enumerate(GROUPS):
                    for t in range(T):
                        dst = vw[b.p][:, t, h0:h0 + n, :].rearrange("p h m -> p (h m)")
                        dst = diagonal(dst, n)
                        last = act.activation(dst, wb[1][:, t, DH * h0:DH * (h0 + n)].rearrange("p (h m) -> p h m", m=DH),
                                              ACT.Copy)
                last.then_inc(e["vw_cp"], 1)
                w("cD_cp", b.n - 1)
                for t in range(T):
                    if t:
                        act.wait_ge(e["aa_half"], b.n + 1)
                    ins = act.activation(junk[:], cin[b.p][:, t, :], ACT.Square, accum_out=aa[b.p][:, t:t + 1])
                    ins.then_inc(e["aa_half"] if t == 0 else e["aa_sum"], 1)

            def xh2_copy(b):
                w("xh2_t", b.n + 1), w("fc_mm", 4 * b.n, 4 * NB)
                act.activation(x2T[:], wb[2][:], ACT.Copy).then_inc(e["x2T_cp"], 1)

            def relu(b, k):
                w("fc_mm", 4 * b.n + k + 1, 4 * NB)
                w("squared", 4 * b.n + k - 1, 4 * NB)
                act.activation(rl[:, k % 2], wb[(0, 1, 2, 0)[k]][:], ACT.Relu).then_inc(e["relu"], 1)

            def exps(b, c):
                w("s2_mm", NPAIR * b.n + c + 1, NPAIR * NB)
                w("av_mm", NPAIR * b.n + c - 1, NPAIR * NB)
                act.activation(pt[c % 2][:], sc[c % 2][:], ACT.Exp).then_inc(e["expd"], 1)

            def yT_copy(b):
                w("y_t", b.n + 1), w("ab_mm", b.n), w("y_sq", b.n)
                act.activation(yT[:], wb[0][:], ACT.Copy).then_inc(e["yT_cp"], 1)

            def bb_copy(b):
                w("bb_mm", b.n + 1), w("d_part", b.n)
                act.activation(bbs[:], wb[1][:, 0, :], ACT.Copy).then_inc(e["bb_cp"], 1)

            def distance(b):
                w("d_part", b.n + 1), w("d_out", 16 * b.n, 16 * NB), w("cD_cp", b.n + 1)
                for t in range(T):
                    last = act.activation(dd[:, t, :], dt_[:, t, :], ACT.Relu, bias=aaD[:, t:t + 1])
                last.then_inc(e["dist"], 1)

            def iteration(i):
                a, z = i.off(1), i.off(-1)
                if there(z):
                    copy_group(z, 2)
                if there(a):
                    before(a)
                if there(z):
                    xh2_copy(z)
                    for k in range(4):
                        relu(z, k)
                for c in range(NPAIR):
                    if there(i):
                        exps(i, c)
                        if c == 3:
                            copy_group(i, 0)
                        if c == 6:
                            copy_group(i, 1)
                    if there(z):
                        if c == 2:
                            yT_copy(z)
                        if c == 3:
                            bb_copy(z)
                        if c == 6:
                            distance(z)
            run(iteration, act)

        @block.vector
        def _(v):
            ch = Chain(v, e["vchain"])

            def w(s, count, most=NB):
                done(v, e[s] if isinstance(s, str) else s, count, most)

            def apply_norm(dst, src, s):
                for t in range(T):
                    last = v.tensor_scalar(dst[:, t, :], src[:, t, :], wk_["mv"][:, t, 0:1], wk_["y"][:, t:t + 1],
                                           ALU.subtract, ALU.mult)
                last.then_inc(e[s], 1)

            def ln1(b):
                w(x_in[b.p], 16 * (b.half + 1), 16 * NB)
                layer_stats(v, ch, xin[b.p], wk_)
                w("xhat_t", b.n)
                apply_norm(xhat, xin[b.p], "ln1")
                w("ln1", b.n + 1)

            def recip(b, g):
                h0, n = GROUPS[g]
                w("o_cp", 3 * b.n + g + 1, 3 * NB)
                w("sum_bc01" if g < 2 else "sum_bc2", b.n)
                v.reciprocal(rc[SUMROW:SUMROW + n, g, :], osb[SUMROW:SUMROW + n, g, :]).then_inc(e["recip"], 1)

            def normalise(b):
                w("sum_bc01", b.n + 1), w("wo_mm", b.n)
                v.tensor_tensor(on[:, 0:2, :], osb[:, 0:2, :], wb[2][:], ALU.mult)
                w("sum_bc2", b.n + 1)
                v.tensor_tensor(on[:, 2, :], osb[:, 2, :], wb[0][:, 0, :], ALU.mult).then_inc(e["normed"], 1)

            def residual1(b):
                w("wo_mm", b.n + 1), w(xr_in[b.p], 16 * (b.half + 1), 16 * NB)
                v.scalar_tensor_tensor(x1[:], wb[2][:], gates[:, 0:1], xres[b.p][:], ALU.mult, ALU.add)\
                    .then_inc(e["x1_res"], 1)
                w("x1_res", b.n + 1)
                layer_stats(v, ch, x1, wk_)
                w("xh2_t", b.n)
                apply_norm(xh2, x1, "ln2")
                w("ln2", b.n + 1)

            def k_remainder(b):
                w("k_mm", b.n + 1), w("kh_cp", b.n + 1), w("k_parts", b.n)
                v.tensor_tensor(kr[:], wb[1][:], kp[:, 0, :, :], ALU.subtract).then_inc(e["k_rem"], 1)

            def q_remainder(b):
                w("q_mm", b.n + 1), w("qh_cp", b.n + 1), w("q_parts", b.n)
                v.scalar_tensor_tensor(qr[:], wb[0][:], 1.0 / 16, qp[:, 0, :, :], ALU.mult, ALU.subtract)\
                    .then_inc(e["q_rem"], 1)

            def maxima(b, c):
                w("s1_mm", NPAIR * b.n + c + 1, NPAIR * NB)
                if c == 0:
                    w("max_t", b.n)
                v.tensor_reduce(nmax[:, 4 * c:4 * c + 4], sc[c % 2][:], AX.X, ALU.max, negate=True)\
                    .then_inc(e["maxed"], 1)

            def split_max(b):
                w("max_t", b.n + 1), w("max_in", 32 * b.n, 32 * NB)
                ch.link(v.tensor_copy(nsp[:, 0, :], wb[1][0:2 * NH, 0, 0:P]))
                v.tensor_tensor(nsp[:, 1, :], wb[1][0:2 * NH, 0, 0:P], nsp[:, 0, :], ALU.subtract)\
                    .then_inc(e["max_split"], 1)

            def residual2(b):
                w("pr_mm", b.n + 1), w("x2_out", 16 * b.n, 16 * NB)
                v.scalar_tensor_tensor(x2[:], wb[2][:], gates[:, 2:3], x1[:], ALU.mult, ALU.add)\
                    .then_inc(e["x2_res"], 1)
                w("x2_res", b.n + 1)
                layer_stats(v, ch, x2, wk_)
                w("y_t", b.n)
                apply_norm(yn, x2, "ln3")
                w("ln3", b.n + 1)

            def distance_part(b):
                w("ab_mm", b.n + 1), w("bb_cp", b.n + 1), w("dist", b.n)
                for t in range(T):
                    last = v.scalar_tensor_tensor(dt_[:, t, :], wb[2][:, t, :], -2.0, bbs[:], ALU.mult, ALU.add)
                last.then_inc(e["d_part"], 1)

            ln1(Batch(0, 0))

            def iteration(i):
                a, z = i.off(1), i.off(-1)
                if there(z):
                    recip(z, 2)
                    normalise(z)
                if there(a):
                    k_remainder(a)
                if there(z):
                    residual1(z)
                if there(a):
                    q_remainder(a)
                if there(i):
                    for c in range(NPAIR):
                        maxima(i, c)
                    split_max(i)
                if there(z):
                    residual2(z)
                if there(i.off(2)):
                    ln1(i.off(2))
                if there(z):
                    distance_part(z)
                if there(i):
                    recip(i, 0)
                    recip(i, 1)
            run(iteration, v, ch)

        @block.gpsimd
        def _(pool):
            def w(s, count, most=NB):
                done(pool, e[s], count, most, e["pool_tick"])

            def parts(b):
                for rem, made, r, pt_, out in (("k_rem", "k_parts", kr, kp, "k_out"), ("q_rem", "q_parts", qr, qp, "q_out")):
                    w(rem, b.n + 1), w(out, 16 * b.n, 16 * NB)
                    pool.tensor_copy(pt_[:, 1, :, :], r[:]).then_inc(e[made + "_mid"], 1)
                    w(made + "_mid", b.n + 1)
                    pool.tensor_tensor(pt_[:, 2, :, :], r[:], pt_[:, 1, :, :], ALU.subtract).then_inc(e[made], 1)

            def squares(b):
                for k in range(4):
                    w("relu", 4 * b.n + k + 1, 4 * NB)
                    if k == 0:
                        w("pr_mm", b.n)
                    pool.tensor_tensor(r2[:, 2 * k:2 * k + 2, :], rl[:, k % 2], rl[:, k % 2], ALU.mult)\
                        .then_inc(e["squared"], 1)

            def y_squares(b):
                w("yT_cp", b.n + 1), w("bb_mm", b.n)
                pool.tensor_tensor(ysq[:], yT[:], yT[:], ALU.mult).then_inc(e["y_sq"], 1)

            def zero_max_rows(b):
                w("s2_mm", NPAIR * (b.n + 1), NPAIR * NB)
                w("cD_cp", b.n + 1)
                pool.memset(qst[b.p][MAXROW:MAXROW + 2, :, :].bitcast(F32), 0.0).then_inc(e["maxrow_zero"], 1)
                w("maxrow_zero", b.n + 1)

            def keep_ctx(b):
                w("aa_sum", b.n + 1), w("dist", b.n)
                pool.tensor_copy(aaD[:], aa[b.p][:])
                w("cT_cp", b.n + 1), w("ab_mm", b.n)
                pool.tensor_copy(cD[:], cT[b.p][:]).then_inc(e["cD_cp"], 1)

            def iteration(i):
                a, z = i.off(1), i.off(-1)
                if there(z):
                    zero_max_rows(z)
                if there(a):
                    parts(a)
                if there(z):
                    squares(z)
                    y_squares(z)
                if there(i):
                    keep_ctx(i)
            run(iteration, pool)


def diagonal(ap, n):
    return bass.AP(ap.tensor, ap.offset, [list(ap.ap[0]), [P + DH, n], [1, DH]])


def setup_weights(nc, io, o):
    with ExitStack() as ctx:
        def sb(name, shape, dt=F32):
            return ctx.enter_context(nc.sbuf_tensor(name, shape, dt))

        def sem(name):
            return ctx.enter_context(nc.semaphore(name))

        raw = {n: sb("raw_" + n, [P, C, D]) for n in ("wq", "wk", "wv", "wo")}
        wfc, wpr = sb("wfc", [P, FT, D]), sb("wpr", [P, C, F])
        u, vv, fbT = sb("u", [P, FT, RANK]), sb("vv", [RANK, D]), sb("fbT", [RANK, RANK])
        uT, fbv = sb("uT", [RANK, F]), sb("fbv", [RANK, D])
        scl = sb("scl", [P, FT + C])
        rsc = sb("rsc", [P, FT + C])
        gin = sb("gin", [P, 5])
        ps = [ctx.enter_context(nc.psum_tensor(f"su{r}", [P, 512], F32)) for r in range(4)]
        loaded, consts, quant, turned, copied, tanhd, vch = (sem(n) for n in (
            "w_loaded", "consts", "quantised", "turned", "copied", "tanhd", "w_chain"))
        pch = sem("w_pool_chain")
        block = ctx.enter_context(nc.Block())
        NLOAD = 12

        @block.sync
        def _(sp):
            for n in ("wq", "wk", "wv", "wo"):
                sp.dma_start(raw[n][:], io["L0_xattn_" + n].rearrange("(a p) d -> p a d", p=P)).then_inc(loaded, 16)
            sp.dma_start(wfc[:], io["L0_ffn_w_fc"].rearrange("(a p) d -> p a d", p=P)).then_inc(loaded, 16)
            sp.dma_start(wpr[:], io["L0_ffn_w_proj"].rearrange("(a p) f -> p a f", p=P)).then_inc(loaded, 16)
            sp.dma_start(u[:], io["L0_ffn_u"].rearrange("(a p) r -> p a r", p=P)).then_inc(loaded, 16)
            sp.dma_start(vv[:], io["L0_ffn_v"]).then_inc(loaded, 16)
            sp.dma_start(fbT[:], io["L0_ffn_fast_b"].rearrange("a b -> b a"), allow_slow_non_contiguous=True)\
                .then_inc(loaded, 16)
            sp.dma_start(gin[:, 0:2], io["g_xattn"].partition_broadcast(P)).then_inc(loaded, 16)
            sp.dma_start(gin[:, 2:4], io["g_ffn"].partition_broadcast(P)).then_inc(loaded, 16)
            sp.dma_start(gin[:, 4:5], io["L0_ffn_gate"].partition_broadcast(P)).then_inc(loaded, 16)
            sp.wait_ge(loaded, 16 * NLOAD)

        @block.gpsimd
        def _(pool):
            pc = Chain(pool, pch)
            pc.link(pool.memset(o["ident"][:], 0.0))
            pc.link(pool.memset(o["sel"][:], 1.0))
            pc.link(pool.memset(o["ones"][:], 1.0))
            pc.link(pool.memset(o["woT"][:], 0.0))
            pc.link(pool.memset(o["rc"][:], 0.0))
            for p in range(2):
                pc.link(pool.memset(o["vw"][p][:], 0.0))
                pc.link(pool.memset(o["qst"][p][MAXROW:P, :, :], 0.0))
                pc.link(pool.memset(o["kst"][p][MAXROW:P, :, :], 0.0))
            pc.link(pool.affine_select(out=o["ident"][:], in_=o["ident"][:], compare_op=ALU.not_equal, fill=1.0,
                                       base=0, pattern=[[-1, P]], channel_multiplier=1))
            pc.link(pool.affine_select(out=o["sel"][:], in_=o["sel"][:], compare_op=ALU.is_ge, fill=0.0,
                                       base=DH * SUMROW, pattern=[[1, P]], channel_multiplier=-DH))
            pc.link(pool.affine_select(out=o["sel"][:], in_=o["sel"][:], compare_op=ALU.is_ge, fill=0.0,
                                       base=DH - 1 - DH * SUMROW, pattern=[[-1, P]], channel_multiplier=DH))
            for p in range(2):
                pc.link(pool.memset(o["kst"][p][MAXROW:MAXROW + 2, :, :], 1.0))
                for h0, n in GROUPS:
                    for s in range(n):
                        pc.link(pool.memset(o["vw"][p][:, :, h0 + s, SUMROW + s:SUMROW + s + 1], 1.0))
            pool.sem_inc(consts, 1)

        @block.scalar
        def _(act):
            act.wait_ge(loaded, 16 * NLOAD)
            act.activation(o["gates"][:], gin[:, 0:4], ACT.Tanh).then_inc(tanhd, 1)
            act.wait_ge(tanhd, 1)

        jobs = []
        for n in ("wq", "wk", "wv"):
            for a in range(C):
                for c in range(C):
                    jobs.append((raw[n][:, a, c * P:c * P + P], o[n + "T"][:, c, a * P:a * P + P], P, None))
        for g, (h0, n) in enumerate(GROUPS):
            for a in range(C):
                jobs.append((raw["wo"][:, a, DH * h0:DH * (h0 + n)], o["woT"][0:DH * n, g, a * P:a * P + P], DH * n, None))
        for a in range(C):
            for f in range(FT):
                jobs.append((wpr[:, a, f * P:f * P + P], o["wprT"][:, f, a * P:a * P + P], P, None))
        for f in range(FT):
            for c in range(C):
                jobs.append((wfc[:, f, c * P:c * P + P], o["wfcT"][:, c, f * P:f * P + P], P, (f, c)))

        @block.vector
        def _(v):
            ch = Chain(v, vch)
            v.wait_ge(loaded, 16 * NLOAD)
            quantise_rows(v, ch, wfc, scl[:, 0:FT], rsc[:, 0:FT], FT, D)
            quantise_rows(v, ch, wpr, scl[:, FT:FT + C], rsc[:, FT:FT + C], C, F)
            v.sem_inc(quant, 1)
            for f in range(FT):
                v.wait_ge(turned, f + 1)
                v.tensor_copy(uT[:, f * P:f * P + P], ps[f % 2][0:RANK, 0:P]).then_inc(copied, 1)
            v.wait_ge(turned, FT + 1)
            v.tensor_copy(fbv[:], ps[2][0:RANK, 0:D]).then_inc(copied, 1)
            v.wait_ge(consts, 1)
            for k, (_, dst, rows, lowrank) in enumerate(jobs):
                v.wait_ge(turned, FT + 2 + k)
                if lowrank is None:
                    v.tensor_copy(dst, ps[k % 2][0:rows, 0:P]).then_inc(copied, 1)
                else:
                    ch.link(v.tensor_copy(dst, ps[k % 2][0:rows, 0:P]))
                    v.scalar_tensor_tensor(dst, ps[2 + k % 2][0:rows, 0:P], gin[:, 4:5], dst, ALU.mult, ALU.add)\
                        .then_inc(copied, 1)
            v.wait_ge(copied, FT + 1 + len(jobs))

        @block.tensor
        def _(pe):
            pe.wait_ge(consts, 1)
            pe.wait_ge(loaded, 16 * NLOAD)
            for f in range(FT):
                if f >= 2:
                    pe.wait_ge(copied, f - 1)
                pe.transpose(ps[f % 2][0:RANK, 0:P], u[:, f, :], o["ident"][:]).then_inc(turned, 1)
            pe.matmul(ps[2][0:RANK, 0:D], fbT[:], vv[:], start=True, stop=True).then_inc(turned, 1)
            pe.wait_ge(quant, 1)
            for k, (src, _, rows, lowrank) in enumerate(jobs):
                pe.wait_ge(copied, FT + k if k < 2 else FT + k)
                if lowrank is not None:
                    f, c = lowrank
                    pe.matmul(ps[2 + k % 2][:, 0:P], fbv[:, c * P:c * P + P], uT[:, f * P:f * P + P],
                              start=True, stop=True)
                pe.transpose(ps[k % 2][0:rows, 0:P], src, o["ident"][:]).then_inc(turned, 1)


def quantise_rows(v, ch, w, scl, rsc, n, width):
    for a in range(n):
        ch.tick(v.tensor_reduce(scl[:, a:a + 1], w[:, a, :], AX.X, ALU.add, apply_absolute_value=True))
    ch.hold()
    ch.link(v.tensor_scalar(scl, scl, 1.0 / width, 1e-5, ALU.mult, ALU.max))
    ch.link(v.reciprocal(rsc, scl))
    for a in range(n):
        ch.tick(v.tensor_scalar(w[:, a, :], w[:, a, :], rsc[:, a:a + 1], MAGIC, ALU.mult, ALU.add))
    ch.hold()
    for a in range(n):
        ch.tick(v.tensor_scalar(w[:, a, :], w[:, a, :], MAGIC, 1.0, ALU.subtract, ALU.min))
    ch.hold()
    for a in range(n):
        ch.tick(v.tensor_scalar(w[:, a, :], w[:, a, :], -1.0, scl[:, a:a + 1], ALU.max, ALU.mult))
    ch.hold()


def alignment_phase(nc, io, scr):
    with ExitStack() as ctx:
        def sb(name, shape, dt=F32):
            return ctx.enter_context(nc.sbuf_tensor(name, shape, dt))

        def sem(name):
            return ctx.enter_context(nc.semaphore(name))

        dist = [sb(f"rows_d{p}", [NB, ROWS, S]) for p in range(2)]
        cost = [sb(f"rows_r{p}", [NB, ROWS, S + 1]) for p in range(2)]
        best = sb("best", [NB, S])
        d_in = [sem(f"d_in{p}") for p in range(2)]
        r_out = [sem(f"r_out{p}") for p in range(2)]
        v_out, rooted, costed, edge, rch, tick = (sem(n) for n in ("virtual_out", "rooted", "costed", "edge", "row_chain", "sp_tick2"))
        block = ctx.enter_context(nc.Block())
        dram_d = scr["d"].rearrange("i b s -> b i s")

        @block.sync
        def _(sp):
            sp.dma_start(dist[0][:], dram_d[:, 0:ROWS, :]).then_inc(d_in[0], 16)
            sp.dma_start(dist[1][:], dram_d[:, ROWS:2 * ROWS, :]).then_inc(d_in[1], 16)
            sp.wait_ge(edge, 1)
            sp.dma_start(scr["r"][:, 0:1, :], cost[1][:, ROWS - 1:ROWS, :]).then_inc(v_out, 16)
            sp.wait_ge(v_out, 16)
            sp.sem_inc(edge, 1)

            def chunk(h, p, more):
                done(sp, costed, 2 * h + p + 1, NCH, tick)
                sp.dma_start(scr["r"][:, bass.ds((2 * h + p) * ROWS + 1, ROWS), :], cost[p][:]).then_inc(r_out[p], 16)
                if more:
                    sp.dma_start(dist[p][:], dram_d[:, bass.ds((2 * h + p + 2) * ROWS, ROWS), :]).then_inc(d_in[p], 16)
            with sp.Fori(0, NCH // 2 - 1) as h:
                chunk(h, 0, True)
                chunk(h, 1, True)
            chunk(NCH // 2 - 1, 0, False)
            chunk(NCH // 2 - 1, 1, False)
            for p in range(2):
                sp.wait_ge(r_out[p], 16 * NCH // 2)

        @block.scalar
        def _(act):
            def chunk(h, p):
                act.wait_ge(d_in[p], 16 * (h + 1))
                act.activation(dist[p][:], dist[p][:], ACT.Sqrt).then_inc(rooted, 1)
            with act.Fori(0, NCH // 2) as h:
                chunk(h, 0)
                chunk(h, 1)

        @block.vector
        def _(v):
            ch = Chain(v, rch)
            ch.link(v.memset(cost[0][:, :, 0:1], BIG))
            ch.link(v.memset(cost[1][:, :, 0:1], BIG))
            ch.link(v.memset(cost[1][:, ROWS - 1, :], BIG))
            ch.link(v.memset(cost[1][:, ROWS - 1, 0:1], 0.0))
            v.sem_inc(edge, 1)
            v.wait_ge(edge, 2)

            def chunk(h, p, full):
                v.wait_ge(rooted, 2 * h + p + 1)
                if full:
                    v.wait_ge(r_out[p], 16 * h)
                for i in range(ROWS):
                    prev = cost[p][:, i - 1, :] if i else cost[1 - p][:, ROWS - 1, :]
                    ch.link(v.tensor_tensor(best[:], prev[:, 1:S + 1], prev[:, 0:S], ALU.min))
                    row = v.tensor_tensor_scan(cost[p][:, i, 1:S + 1], best[:], dist[p][:, i, :], BIG, ALU.min, ALU.add)
                    ch.link(row)
                v.sem_inc(costed, 1)

            chunk(0, 0, False)
            ch.link(v.memset(cost[1][:, ROWS - 1, 0:1], BIG))
            chunk(0, 1, False)
            start = ch.n
            with v.Fori(1, NCH // 2) as h:
                ch.base = (h - 1) * (4 * ROWS)
                chunk(h, 0, True)
                chunk(h, 1, True)
            assert ch.n - start == 4 * ROWS


def path_phase(nc, io, scr, vin, vout):
    with ExitStack() as ctx:
        def sb(name, shape, dt=F32):
            return ctx.enter_context(nc.sbuf_tensor(name, shape, dt))

        def sem(name):
            return ctx.enter_context(nc.semaphore(name))

        W = S + 1
        cur = [sb(f"cur{p}", [P, T, W]) for p in range(2)]
        prv = [sb(f"prv{p}", [P, T, W]) for p in range(2)]
        m, dg, nl = sb("m", [P, T, S]), sb("dg", [P, T, S]), sb("nl", [P, T, S])
        hh = sb("hh", [P, T, S])
        last_ = sb("last_", [P, T, W])
        step = [sb(f"step{p}", [P, T, S]) for p in range(2)]
        iota = sb("iota", [P, T, S])
        ident = sb("ident2", [NB, NB])
        rows = [sb(f"rows_g{p}", [NB, ROWS, S]) for p in range(2)]
        hop = sb("hop", [NB, S])
        cell = sb("cell", [NB, ROWS + 1])
        path = sb("path", [NB, S + 1])
        ps = [ctx.enter_context(nc.psum_tensor(f"pp{r}", [P, 512], F32)) for r in range(4)]
        r_in = [sem(f"rr_in{p}") for p in range(2)]
        g_out = [sem(f"g_out{p}") for p in range(2)]
        g_in = [sem(f"g_in{p}") for p in range(2)]
        consts, used, pch, vch, held, ran, copied, stepped, turned, tick = (sem(n) for n in (
            "consts2", "cells_used", "pool_chain2", "v_chain2", "held", "ran", "path_cp", "stepped", "turned2", "sp_tick3"))
        ptick, gdone = sem("pool_tick3"), sem("chunk_used")
        block = ctx.enter_context(nc.Block())

        @block.sync
        def _(sp):
            def load(n, h, p):
                sp.dma_start(cur[p][:], scr["r"][n, 1:S + 1, :].rearrange("(t p) s -> p t s", p=P)).then_inc(r_in[p], 16)
                sp.dma_start(prv[p][:], scr["r"][n, 0:S, :].rearrange("(t p) s -> p t s", p=P)).then_inc(r_in[p], 16)

            def store(n, h, p):
                done(sp, stepped, n + 1, NB, tick)
                sp.dma_start(scr["g"].rearrange("(t p) b s -> p t b s", p=P)[:, :, n, :], step[p][:]).then_inc(g_out[p], 16)
            load(0, 0, 0)
            load(1, 0, 1)
            with sp.Fori(0, NB // 2 - 1) as h:
                for p in range(2):
                    store(2 * h + p, h, p)
                    done(sp, used, 2 * h + p + 1, NB, tick)
                    load(2 * h + p + 2, h + 1, p)
            store(NB - 2, 0, 0)
            store(NB - 1, 0, 1)
            for p in range(2):
                sp.wait_ge(g_out[p], 16 * NB // 2)
            dram_g = scr["g"].rearrange("i b s -> b i s")

            def rows_in(k, p):
                sp.dma_start(rows[p][:], dram_g[:, bass.ds((NCH - 1 - k) * ROWS, ROWS), :]).then_inc(g_in[p], 16)
            rows_in(0, 0)
            rows_in(1, 1)
            with sp.Fori(0, NCH // 2 - 1) as h:
                for p in range(2):
                    done(sp, gdone, 2 * h + p + 1, NCH, tick)
                    rows_in(2 * h + p + 2, p)

        @block.gpsimd
        def _(pool):
            pc = Chain(pool, pch)
            pc.link(pool.iota(iota[:], pattern=[[0, T], [1, S]], base=0, channel_multiplier=0,
                              allow_small_or_imprecise_dtypes=True))
            pc.link(pool.memset(ident[:], 0.0))
            pc.link(pool.affine_select(out=ident[:], in_=ident[:], compare_op=ALU.not_equal, fill=1.0,
                                       base=0, pattern=[[-1, NB]], channel_multiplier=1))
            pc.link(pool.memset(last_[:, :, 0:1], 0.0))
            pool.sem_inc(consts, 1)

            def seq(n, h, p, full):
                done(pool, ran, n + 1, NB, ptick)
                if full:
                    done(pool, g_out[p], 16 * h, 16 * NB, ptick)
                pool.tensor_tensor(step[p][:], last_[:, :, 1:W], last_[:, :, 0:S], ALU.subtract).then_inc(stepped, 1)
            seq(0, 0, 0, False)
            seq(1, 0, 1, False)
            with pool.Fori(1, NB // 2) as h:
                seq(2 * h, h, 0, True)
                seq(2 * h + 1, h, 1, True)

        @block.vector
        def _(v):
            ch = Chain(v, vch)
            v.wait_ge(consts, 1)

            def seq(n, h, p, full):
                v.wait_ge(r_in[p], 32 * (h + 1))
                c, r = cur[p], prv[p]
                ch.tick(v.tensor_tensor(m[:], r[:, :, 1:W], r[:, :, 0:S], ALU.min))
                ch.tick(v.tensor_tensor(dg[:], r[:, :, 0:S], r[:, :, 1:W], ALU.is_le))
                ch.hold()
                ch.tick(v.tensor_tensor(nl[:], m[:], c[:, :, 0:S], ALU.is_le))
                ch.tick(v.scalar_tensor_tensor(hh[:], dg[:], -0.75, iota[:], ALU.mult, ALU.add))
                ch.hold()
                v.sem_inc(used, 1)
                ch.link(v.tensor_tensor(hh[:], hh[:], nl[:], ALU.mult))
                if full:
                    v.wait_ge(stepped, n)
                for t in range(T):
                    last = v.tensor_tensor_scan(last_[:, t, 1:W], hh[:, t, :], hh[:, t, :], 0.0, ALU.max, ALU.max)
                last.then_inc(ran, 1)
            seq(0, 0, 0, False)
            seq(1, 0, 1, True)
            start = ch.n
            with v.Fori(1, NB // 2) as h:
                ch.base = (h - 1) * 10
                seq(2 * h, h, 0, True)
                seq(2 * h + 1, h, 1, True)
            assert ch.n - start == 10
            ch.base = (NB // 2 - 2) * 10

            ch.link(v.memset(path[:], 0.0))
            ch.link(v.memset(path[:, S:S + 1], float(S - 1)))
            ch.link(v.memset(cell[:, 0:1], float(S - 1)))

            def chunk(k, h, p):
                v.wait_ge(g_in[p], 16 * (h + 1))
                ch.link(v.tensor_copy(cell[:, ROWS:ROWS + 1], cell[:, 0:1]))
                for i in range(ROWS - 1, -1, -1):
                    ch.link(v.scalar_tensor_tensor(hop[:], iota[0:NB, 0, :], cell[:, i + 1:i + 2], rows[p][:, i, :],
                                                   ALU.is_le, ALU.mult, accum_out=cell[:, i:i + 1]))
                ch.link(v.tensor_copy(path[:, bass.ds((NCH - 1 - k) * ROWS, ROWS)], cell[:, 0:ROWS]))
                v.sem_inc(gdone, 1)
            start, base = ch.n, ch.base
            with v.Fori(0, NCH // 2) as h:
                ch.base = h * (2 * (ROWS + 2)) + base
                chunk(2 * h, h, 0)
                chunk(2 * h + 1, h, 1)
            assert ch.n - start == 2 * (ROWS + 2)
            ch.base = base + (NCH // 2 - 1) * 2 * (ROWS + 2)
            ch.link(v.memset(path[:, 0:1], 0.0))
            v.sem_inc(held, 1)
            for t in range(T):
                v.wait_ge(turned, 2 * t + 2)
                v.tensor_copy(vout[:, t, :], ps[2 * t][:, 0:NB]).then_inc(copied, 1)
                v.tensor_copy(vin[:, t, :], ps[2 * t + 1][:, 0:NB]).then_inc(copied, 1)
            v.wait_ge(copied, 2 * T)

        @block.tensor
        def _(pe):
            pe.wait_ge(consts, 1)
            pe.wait_ge(held, 1)
            for t in range(T):
                pe.transpose(ps[2 * t][:, 0:NB], path[:, t * P:t * P + P], ident[:]).then_inc(turned, 1)
                pe.transpose(ps[2 * t + 1][:, 0:NB], path[:, t * P + 1:t * P + P + 1], ident[:]).then_inc(turned, 1)


def last_layer_phase(nc, io, scr, vin, vout, out):
    with ExitStack() as ctx:
        def sb(name, shape, dt=F32):
            return ctx.enter_context(nc.sbuf_tensor(name, shape, dt))

        def sem(name):
            return ctx.enter_context(nc.semaphore(name))

        w1T, w2T = sb("w1T", [P, C, F], BF16), sb("w2T", [P, FT, D], BF16)
        identb, iota = sb("identb", [P, P], BF16), sb("iota3", [P, S])
        gates, wscale = sb("gates3", [P, 4]), sb("wscale", [P, 2])
        b1, b2 = sb("b1", [P, F]), sb("b2", [P, D])
        setup_last_weights(nc, io, dict(w1T=w1T, w2T=w2T, identb=identb, iota=iota, gates=gates, wscale=wscale,
                                        b1=b1, b2=b2))

        x2 = [sb(f"x2_{p}", [P, T, D]) for p in range(2)]
        cx = [sb(f"cx_{p}", [P, T, D]) for p in range(2)]
        before_, mask = sb("before_", [P, T, S]), sb("mask", [P, T, S])
        x3 = sb("x3", [P, T, D])
        x3b = [sb(f"x3b{p}", [P, T, D]) for p in range(2)]
        xc, xr = sb("xc", [P, T, D]), sb("xr", [P, T, D])
        xq, xqT = sb("xq", [P, T, D], BF16), sb("xqT", [P, C, S], BF16)
        st, mv = sb("st3", [P, T, 6]), sb("mv3", [P, T, 2])
        var, amax, y, tmp, q = (sb(n, [P, 2 * T]) for n in ("var4", "amax4", "y4", "tmp4", "q4"))
        back_ = [sb(f"back{p}", [P, 2 * T]) for p in range(2)]
        hb = [sb(f"hb{t}", [P, F]) for t in range(T)]
        gl = [sb(f"gl{t}", [P, F]) for t in range(T)]
        sq = sb("sq", [P, F])
        ssum = sb("ssum", [P, T])
        hr_ = [sb(f"hr{t}", [P, F]) for t in range(T)]
        hq = [sb(f"hq{t}", [P, F], BF16) for t in range(T)]
        hqT = [sb(f"hqT{t}", [P, FT, P], BF16) for t in range(T)]
        xo = [sb(f"xo{p}", [P, T, D]) for p in range(2)]

        pe_x = ctx.enter_context(nc.psum_tensor("pe_x", [P, T, D], F32))
        pt_x = ctx.enter_context(nc.psum_tensor("pt_x", [P, C, S], BF16))
        ph = [ctx.enter_context(nc.psum_tensor(f"ph{t}", [P, F], F32)) for t in range(T)]
        pt_h = ctx.enter_context(nc.psum_tensor("pt_h", [P, FT, P], BF16))
        po = ctx.enter_context(nc.psum_tensor("po", [P, T, D], F32))

        names = ["expand", "xq_t", "h_mm", "hq_t", "o_mm",
                 "xqT_cp", "gelu", "squares", "hqT_cp", "x_round",
                 "masked", "x3_res", "x_scaled", "h_bias", "h_scaled", "x4_res",
                 "x3_bias", "h_round", "chain3", "tick_sp3", "tick_pool3"]
        e = {n: sem(n) for n in names}
        x_in = [sem(f"x2_in{p}") for p in range(2)]
        o_out = [sem(f"o_out{p}") for p in range(2)]
        block = ctx.enter_context(nc.Block())
        tok = "(t p) d -> p t d"

        def there(b):
            return not isinstance(b.n, int) or 0 <= b.n < NB

        def run(iteration, eng, chain=None):
            iteration(Batch(-1, 0))
            iteration(Batch(-1, 1))
            iteration(Batch(0, 0))
            before = chain.n if chain else 0
            iteration(Batch(0, 1))
            start = chain.n if chain else 0
            step = 2 * (start - before)
            with eng.Fori(1, NB // 2 - 2) as h:
                if chain:
                    chain.base = (h - 1) * step
                iteration(Batch(h, 0))
                iteration(Batch(h, 1))
            if chain:
                assert chain.n - start == step
                chain.base = (NB // 2 - 4) * step
            iteration(Batch(NB // 2 - 2, 0))
            iteration(Batch(NB // 2 - 2, 1))
            iteration(Batch(NB // 2 - 1, 0))
            iteration(Batch(NB // 2 - 1, 1))
            iteration(Batch(NB // 2, 0))

        @block.sync
        def _(sp):
            def w(s, count, most=NB):
                done(sp, s, count, most, e["tick_sp3"])

            def load(b):
                w(e["expand"], b.n - 1)
                w(e["x3_res"], b.n - 1)
                sp.dma_start(x2[b.p][:], scr["x2"][b.n].rearrange(tok, p=P)).then_inc(x_in[b.p], 16)
                sp.dma_start(cx[b.p][:], io["ctx_1024"][b.n].rearrange(tok, p=P)).then_inc(x_in[b.p], 16)

            def store(b):
                w(e["x4_res"], b.n + 1)
                sp.dma_start(out[b.n].rearrange(tok, p=P), xo[b.p][:]).then_inc(o_out[b.p], 16)
            load(Batch(0, 0))

            def iteration(i):
                if there(i.off(3)):
                    load(i.off(3))
                if there(i.off(-1)):
                    store(i.off(-1))
            run(iteration, sp)
            for p in range(2):
                sp.wait_ge(o_out[p], 16 * NB // 2)

        @block.tensor
        def _(pe):
            def w(s, count, most=NB):
                done(pe, e[s] if isinstance(s, str) else s, count, most)

            def expand(b):
                w("masked", b.n + 1), w("x3_res", b.n)
                w(x_in[b.p], 32 * (b.half + 1), 32 * NB)
                for j in range(T):
                    for t in range(T):
                        last = pe.matmul(pe_x[:, j, :], mask[:, t, j * P:j * P + P], cx[b.p][:, t, :],
                                         start=(t == 0), stop=(t == T - 1))
                last.then_inc(e["expand"], 1)

            def hidden(b):
                w("x_round", b.n + 1), w("xqT_cp", b.n)
                for c in range(C):
                    for t in range(T):
                        last = pe.transpose(pt_x[:, c, t * P:t * P + P], xq[:, t, c * P:c * P + P], identb[:])
                last.then_inc(e["xq_t"], 1)
                w("xqT_cp", b.n + 1)
                for t in range(T):
                    w("h_bias", 2 * b.n + t - 1, 2 * NB)
                    for j in range(2):
                        for c in range(C):
                            last = pe.matmul(ph[t][:, 512 * j:512 * j + 512], xqT[:, c, t * P:t * P + P],
                                             w1T[:, c, 512 * j:512 * j + 512], start=(c == 0), stop=(c == C - 1))
                    last.then_inc(e["h_mm"], 1)

            def output(b):
                for t in range(T):
                    w("h_round", 2 * b.n + t + 1, 2 * NB), w("hqT_cp", 2 * b.n + t, 2 * NB)
                    for f in range(FT):
                        last = pe.transpose(pt_h[:, f, :], hq[t][:, f * P:f * P + P], identb[:])
                    last.then_inc(e["hq_t"], 1)
                w("x4_res", b.n)
                for t in range(T):
                    w("hqT_cp", 2 * b.n + t + 1, 2 * NB)
                    for f in range(FT):
                        last = pe.matmul(po[:, t, :], hqT[t][:, f, :], w2T[:, f, :], start=(f == 0), stop=(f == FT - 1))
                last.then_inc(e["o_mm"], 1)

            def iteration(i):
                if there(i.off(2)):
                    expand(i.off(2))
                if there(i.off(1)):
                    hidden(i.off(1))
                if there(i):
                    output(i)
            run(iteration, pe)

        @block.scalar
        def _(act):
            def w(s, count, most=NB):
                done(act, e[s] if isinstance(s, str) else s, count, most)

            def activate(b):
                for t in range(T):
                    w("h_bias", 2 * b.n + t + 1, 2 * NB), w("h_scaled", 2 * b.n + t - 1, 2 * NB)
                    act.activation(gl[t][:], hb[t][:], ACT.Gelu).then_inc(e["gelu"], 1)
                for t in range(T):
                    w("gelu", 2 * b.n + t + 1, 2 * NB), w("squares", 2 * b.n + t, 2 * NB)
                    w("x_scaled", b.n + 1)
                    act.activation(sq[:], gl[t][:], ACT.Square, accum_out=ssum[:, t:t + 1]).then_inc(e["squares"], 1)

            def turn_x(b):
                w("x_scaled", b.n + 1), w("xq_t", b.n)
                act.activation(xq[:], xr[:], ACT.Copy, bias=-MAGIC).then_inc(e["x_round"], 1)
                w("xq_t", b.n + 1), w("h_mm", 2 * b.n, 2 * NB)
                act.activation(xqT[:], pt_x[:], ACT.Copy).then_inc(e["xqT_cp"], 1)

            def turn_h(b):
                for t in range(T):
                    w("hq_t", 2 * b.n + t + 1, 2 * NB), w("o_mm", b.n)
                    act.activation(hqT[t][:], pt_h[:], ACT.Copy).then_inc(e["hqT_cp"], 1)

            def iteration(i):
                if there(i):
                    activate(i)
                if there(i.off(1)):
                    turn_x(i.off(1))
                if there(i):
                    turn_h(i)
            run(iteration, act)

        @block.gpsimd
        def _(pool):
            def w(s, count, most=NB):
                done(pool, e[s], count, most, e["tick_pool3"])

            def iteration(i):
                a = i.off(1)
                if there(a):
                    w("x3_res", a.n + 1), w("x4_res", a.n - 1)
                    for t in range(T):
                        last = pool.tensor_tensor(x3b[a.p][:, t, :], x3[:, t, :], b2[:], ALU.add)
                    last.then_inc(e["x3_bias"], 1)
                if there(i):
                    for t in range(T):
                        w("h_scaled", 2 * i.n + t + 1, 2 * NB), w("hq_t", 2 * i.n + t - 1, 2 * NB)
                        pool.tensor_scalar(hq[t][:], hr_[t][:], -MAGIC, 1.0, ALU.add, ALU.mult).then_inc(e["h_round"], 1)
            run(iteration, pool)

        @block.vector
        def _(v):
            ch = Chain(v, e["chain3"])

            def w(s, count, most=NB):
                done(v, e[s] if isinstance(s, str) else s, count, most)

            def path_mask(b):
                w("masked", b.n)
                for t in range(T):
                    ch.tick(v.tensor_scalar(before_[:, t, :], iota[:], vin[:, t, bass.ds(b.n, 1)], None, ALU.is_le))
                ch.hold()
                w("expand", b.n)
                for t in range(T):
                    last = v.scalar_tensor_tensor(mask[:, t, :], iota[:], vout[:, t, bass.ds(b.n, 1)],
                                                  before_[:, t, :], ALU.is_ge, ALU.mult)
                last.then_inc(e["masked"], 1)

            def bias(b):
                for t in range(T):
                    w("h_mm", 2 * b.n + t + 1, 2 * NB), w("gelu", 2 * b.n + t - 1, 2 * NB)
                    v.scalar_tensor_tensor(hb[t][:], ph[t][:], back_[b.p][:, t:t + 1], b1[:], ALU.mult, ALU.add)\
                        .then_inc(e["h_bias"], 1)

            def residual(b):
                w("expand", b.n + 1), w("x3_bias", b.n)
                v.scalar_tensor_tensor(x3[:], pe_x[:], gates[:, 1:2], x2[b.p][:], ALU.mult, ALU.add)\
                    .then_inc(e["x3_res"], 1)
                w("x3_res", b.n + 1)
                for t in range(T):
                    ch.tick(v.bn_stats(st[:, t, :], x3[:, t, :]))
                ch.hold()
                ch.tick_event()
                for t in range(T):
                    ch.tick(v.bn_aggr(mv[:, t, :], st[:, t, :]))
                ch.hold()
                for t in range(T):
                    ch.tick(v.tensor_scalar(xc[:, t, :], x3[:, t, :], mv[:, t, 0:1], None, ALU.subtract))
                ch.tick(v.tensor_scalar(var[:, 0:T], mv[:, :, 1], 1.0 + EPS, EPS * EPS, ALU.mult, ALU.add))
                ch.hold()
                ch.tick(v.tensor_reduce(amax[:, 0:T], xc[:], AX.X, ALU.max, apply_absolute_value=True))

            def maxima(b):
                for t in range(T):
                    w("gelu", 2 * b.n + t + 1, 2 * NB)
                    ch.tick(v.tensor_reduce(amax[:, T + t:T + t + 1], gl[t][:], AX.X, ALU.max, apply_absolute_value=True))
                w("squares", 2 * (b.n + 1), 2 * NB)
                ch.tick(v.tensor_scalar(var[:, T:2 * T], ssum[:], 1.0 / F, EPS, ALU.mult, ALU.add))

            def factors(lo, hi, to):
                ch.hold()
                newton_rsqrt(v, ch, var[:, lo:hi], y[:, lo:hi], tmp[:, lo:hi])
                ch.link(v.tensor_tensor(tmp[:, lo:hi], amax[:, lo:hi], y[:, lo:hi], ALU.mult))
                ch.link(v.tensor_scalar(tmp[:, lo:hi], tmp[:, lo:hi], 1e-5, 1.0 / 127, ALU.max, ALU.mult))
                ch.tick(v.reciprocal(q[:, lo:hi], tmp[:, lo:hi]))
                for cols, dst, k in ((slice(0, T), to[0], 0), (slice(T, 2 * T), to[1], 1)):
                    if dst is not None:
                        ch.tick(v.tensor_scalar(dst[:, cols], tmp[:, cols], wscale[:, k:k + 1], None, ALU.mult))
                ch.hold()
                ch.link(v.tensor_tensor(q[:, lo:hi], q[:, lo:hi], y[:, lo:hi], ALU.mult))

            def scale_x(b):
                w("x_round", b.n)
                for t in range(T):
                    last = v.tensor_scalar(xr[:, t, :], xc[:, t, :], q[:, t:t + 1], MAGIC, ALU.mult, ALU.add)
                last.then_inc(e["x_scaled"], 1)

            def scale_h(b):
                for t in range(T):
                    w("h_round", 2 * b.n + t - 1, 2 * NB)
                    v.tensor_scalar(hr_[t][:], gl[t][:], q[:, T + t:T + t + 1], MAGIC, ALU.mult, ALU.add)\
                        .then_inc(e["h_scaled"], 1)

            def output(b):
                w("x3_bias", b.n + 1), w(o_out[b.p], 16 * b.half, 16 * NB), w("o_mm", b.n + 1)
                for t in range(T):
                    last = v.scalar_tensor_tensor(xo[b.p][:, t, :], po[:, t, :], back_[b.p][:, T + t:T + t + 1],
                                                  x3b[b.p][:, t, :], ALU.mult, ALU.add)
                last.then_inc(e["x4_res"], 1)

            def iteration(i):
                a, z = i.off(1), i.off(-1)
                if there(i):
                    bias(i)
                if there(a):
                    residual(a)
                if there(i):
                    maxima(i)
                lo, hi = (0 if there(a) else T), (2 * T if there(i) else T)
                if lo < hi:
                    factors(lo, hi, (back_[a.p] if there(a) else None, back_[i.p] if there(i) else None))
                if there(a):
                    scale_x(a)
                if there(i):
                    scale_h(i)
                if there(z):
                    output(z)
                if there(i.off(3)):
                    path_mask(i.off(3))
            path_mask(Batch(0, 0))
            run(iteration, v, ch)


def setup_last_weights(nc, io, o):
    with ExitStack() as ctx:
        def sb(name, shape, dt=F32):
            return ctx.enter_context(nc.sbuf_tensor(name, shape, dt))

        def sem(name):
            return ctx.enter_context(nc.semaphore(name))

        w1, w2 = sb("w1", [P, FT, D]), sb("w2", [P, C, F])
        w1b, w2b = sb("w1b", [P, FT, D], BF16), sb("w2b", [P, C, F], BF16)
        gin, ones = sb("gin3", [P, 4]), sb("ones3", [P, P])
        part, scl, rsc = sb("part", [P, 2]), sb("scl3", [P, 2]), sb("rsc3", [P, 2])
        ps = [ctx.enter_context(nc.psum_tensor(f"sl{r}", [P, P], BF16)) for r in range(2)]
        tot = ctx.enter_context(nc.psum_tensor("tot", [P, 512], F32))
        loaded, consts, summed, totals, quant, turned, copied, tanhd, vch, pch = (sem(n) for n in (
            "l_loaded", "l_consts", "l_summed", "l_totals", "l_quant", "l_turned", "l_copied", "l_tanh", "l_chain",
            "l_pchain"))
        block = ctx.enter_context(nc.Block())

        @block.sync
        def _(sp):
            sp.dma_start(w1[:], io["L1_ffn_w1"].rearrange("(a p) d -> p a d", p=P)).then_inc(loaded, 16)
            sp.dma_start(w2[:], io["L1_ffn_w2"].rearrange("(a p) f -> p a f", p=P)).then_inc(loaded, 16)
            sp.dma_start(o["b1"][:], io["L1_ffn_b1"].partition_broadcast(P)).then_inc(loaded, 16)
            sp.dma_start(o["b2"][:], io["L1_ffn_b2"].partition_broadcast(P)).then_inc(loaded, 16)
            sp.dma_start(gin[:, 0:2], io["g_xattn"].partition_broadcast(P)).then_inc(loaded, 16)
            sp.dma_start(gin[:, 2:4], io["g_ffn"].partition_broadcast(P)).then_inc(loaded, 16)
            sp.wait_ge(loaded, 96)

        @block.gpsimd
        def _(pool):
            pc = Chain(pool, pch)
            pc.link(pool.memset(ones[:], 1.0))
            pc.link(pool.memset(o["identb"][:], 0.0))
            pc.link(pool.affine_select(out=o["identb"][:], in_=o["identb"][:], compare_op=ALU.not_equal, fill=1.0,
                                       base=0, pattern=[[-1, P]], channel_multiplier=1))
            pc.link(pool.iota(o["iota"][:], pattern=[[1, S]], base=0, channel_multiplier=0,
                              allow_small_or_imprecise_dtypes=True))
            pool.sem_inc(consts, 1)

        @block.scalar
        def _(act):
            act.wait_ge(loaded, 96)
            act.activation(o["gates"][:], gin[:], ACT.Tanh).then_inc(tanhd, 1)
            act.wait_ge(tanhd, 1)

        jobs = [(w1b[:, f, c * P:c * P + P], o["w1T"][:, c, f * P:f * P + P]) for f in range(FT) for c in range(C)]
        jobs += [(w2b[:, a, f * P:f * P + P], o["w2T"][:, f, a * P:a * P + P]) for a in range(C) for f in range(FT)]

        @block.vector
        def _(v):
            ch = Chain(v, vch)
            v.wait_ge(loaded, 96)
            ch.tick(v.tensor_reduce(part[:, 0:1], w1[:], AX.XY, ALU.add, apply_absolute_value=True))
            ch.link(v.tensor_reduce(part[:, 1:2], w2[:], AX.XY, ALU.add, apply_absolute_value=True))
            v.sem_inc(summed, 1)
            v.wait_ge(totals, 1)
            ch.link(v.tensor_scalar(scl[:], tot[:, 0:2], 1.0 / (D * F), 1e-5, ALU.mult, ALU.max))
            ch.link(v.reciprocal(rsc[:], scl[:]))
            for k, (w_, b_) in enumerate(((w1, w1b), (w2, w2b))):
                ch.link(v.tensor_scalar(w_[:], w_[:], rsc[:, k:k + 1], MAGIC, ALU.mult, ALU.add))
                ch.link(v.tensor_scalar(w_[:], w_[:], MAGIC, 1.0, ALU.subtract, ALU.min))
                ch.link(v.tensor_scalar(b_[:], w_[:], -1.0, None, ALU.max))
            v.sem_inc(quant, 1)
            v.wait_ge(tanhd, 1)
            ch.link(v.tensor_copy(o["wscale"][:, 0:1], scl[:, 0:1]))
            ch.link(v.tensor_tensor(o["wscale"][:, 1:2], scl[:, 1:2], o["gates"][:, 3:4], ALU.mult))
            ch.link(v.tensor_scalar(o["b2"][:], o["b2"][:], o["gates"][:, 3:4], None, ALU.mult))
            for k, (_, dst) in enumerate(jobs):
                v.wait_ge(turned, k + 1)
                v.tensor_copy(dst, ps[k % 2][:]).then_inc(copied, 1)
            v.wait_ge(copied, len(jobs))

        @block.tensor
        def _(pe):
            pe.wait_ge(consts, 1)
            pe.wait_ge(summed, 1)
            pe.matmul(tot[:, 0:2], ones[:], part[:], start=True, stop=True).then_inc(totals, 1)
            pe.wait_ge(quant, 1)
            for k, (src, _) in enumerate(jobs):
                if k >= 2:
                    pe.wait_ge(copied, k - 1)
                pe.transpose(ps[k % 2][:], src, o["identb"][:]).then_inc(turned, 1)


def build(nc, io, out):
    scr = {
        "q": nc.dram_tensor("q_parts_dram", (3, D, S), BF16).ap(),
        "k": nc.dram_tensor("k_parts_dram", (3, D, S), BF16).ap(),
        "x2": nc.dram_tensor("x2_dram", (NB, S, D), F32).ap(),
        "d": nc.dram_tensor("dist_dram", (S, NB, S), F32).ap(),
        "r": nc.dram_tensor("cost_dram", (NB, S + 1, S + 1), F32).ap(),
        "g": nc.dram_tensor("step_dram", (S, NB, S), F32).ap(),
    }
    attention_phase(nc, io, scr)
    with nc.sbuf_tensor("vin", [P, T, NB], F32) as vin, nc.sbuf_tensor("vout", [P, T, NB], F32) as vout:
        alignment_phase(nc, io, scr)
        path_phase(nc, io, scr, vin, vout)
        last_layer_phase(nc, io, scr, vin, vout, out)


_INS = ['x', 'ctx_1024', 'g_xattn', 'g_ffn', 'L0_xattn_wq', 'L0_xattn_wk', 'L0_xattn_wv', 'L0_xattn_wo',
        'L0_ffn_fast_b', 'L0_ffn_w_fc', 'L0_ffn_w_proj', 'L0_ffn_u', 'L0_ffn_v', 'L0_ffn_gate',
        'L1_ffn_w1', 'L1_ffn_b1', 'L1_ffn_w2', 'L1_ffn_b2']


def kernel(**inputs):
    import numpy as _np
    import concourse.bacc as _bacc
    from concourse import mybir as _mybir
    from concourse.bass_utils import run_bass_kernel_spmd as _run

    nc = _bacc.Bacc("TRN2", target_bir_lowering=False, num_devices=1)
    arrays, io = {}, {}
    for name in _INS:
        a = _np.ascontiguousarray(inputs[name])
        if name == 'L0_ffn_gate':
            a = a.reshape(1)
        arrays[f"in_{name}_dram"] = a
        io[name] = nc.dram_tensor(f"in_{name}_dram", a.shape, _mybir.dt.from_np(a.dtype), kind="ExternalInput").ap()
    out = nc.dram_tensor("out_0_dram", (NB, S, D), F32, kind="ExternalOutput").ap()
    build(nc, io, out)
    r = _run(nc, [arrays], core_ids=[0])
    return r.results[0]["out_0_dram"]
```

```python
from contextlib import ExitStack

import numpy as np
import concourse.bass as bass
from concourse import mybir

F32 = mybir.dt.float32
BF16 = mybir.dt.bfloat16
I32 = mybir.dt.int32
ALU = mybir.AluOpType
ACT = mybir.ActivationFunctionType
AX = mybir.AxisListType

P = 128
NB, S, D = 32, 256, 256
NH, DH = 16, 16
F = 1024
RANK = 16
T = S // P
C = D // P
FT = F // P
EPS = 1e-5
BIG = 3.0e38
MAGIC = 12582912.0
RSQRT_SEED = float(0x5F3759DF)

HPG = 4
NG = NH // HPG
HW = P // HPG
NPAIR = 8

Q_PARTS = [0, 1, 0, 1, 2, 0]
K_PARTS = [0, 0, 1, 1, 0, 2]
MAXROW = DH * len(Q_PARTS)

ROWS = 16
NCH = S // ROWS


class Batch:

    def __init__(self, half, p):
        self.half, self.p = half, p
        self.n = 2 * half + p

    def off(self, k):
        k += self.p
        return Batch(self.half + k // 2, k % 2)


def done(eng, sem, count, most, tick=None):
    if isinstance(count, int):
        if count <= 0:
            return
        count = min(count, most)
        eng.wait_ge(sem, count)
        return
    eng.wait_ge(sem, count)
    if tick is not None:
        eng.sem_inc(tick, 1)


class Chain:

    def __init__(self, eng, sem):
        self.eng, self.sem, self.base, self.n = eng, sem, 0, 0

    def tick(self, ins):
        self.n += 1
        ins.then_inc(self.sem, 1)

    def link(self, ins):
        self.tick(ins)
        self.hold()

    def hold(self):
        self.eng.wait_ge(self.sem, self.base + self.n)

    def tick_event(self):
        self.n += 1
        self.eng.sem_inc(self.sem, 1)


def moments(v, ch, src, w, slot):
    for t in range(T):
        ch.tick(v.bn_stats(w["st"][:, T * slot + t, :], src[:, t, :]))
    ch.hold()
    ch.tick_event()
    for t in range(T):
        ch.tick(v.bn_aggr(w["mv"][:, T * slot + t, :], w["st"][:, T * slot + t, :]))
    ch.hold()


def norm_factors(v, ch, w, lo, hi):
    c = slice(T * lo, T * hi)
    ch.link(v.tensor_scalar(w["v"][:, c], w["mv"][:, c, 1], EPS, None, ALU.add))
    newton_rsqrt(v, ch, w["v"][:, c], w["y"][:, c], w["a"][:, c])


def newton_rsqrt(v, ch, x, y, a):
    ch.link(v.tensor_scalar(y.bitcast(I32), x.bitcast(I32), -0.5, RSQRT_SEED, ALU.mult, ALU.add))
    for _ in range(3):
        ch.link(v.scalar_tensor_tensor(a, y, -0.5, y, ALU.mult, ALU.mult))
        ch.link(v.tensor_tensor(a, a, x, ALU.mult))
        ch.link(v.scalar_tensor_tensor(y, a, 1.5, y, ALU.add, ALU.mult))


def attention_phase(nc, io, scr):
    with ExitStack() as ctx:
        def sb(name, shape, dt=F32):
            return ctx.enter_context(nc.sbuf_tensor(name, shape, dt))

        def sem(name):
            return ctx.enter_context(nc.semaphore(name))

        wqT, wkT, wvT = sb("wqT", [P, C, D]), sb("wkT", [P, C, D]), sb("wvT", [P, C, D])
        woT = sb("woT", [P, NG, D])
        wfcT = sb("wfcT", [P, C, F])
        wprT = sb("wprT", [P, FT, D])
        ident = sb("ident", [P, P])
        ones = sb("ones", [P, P])
        sel = sb("sel", [P, P])
        gates = sb("gates", [P, 4])
        xin = [sb(f"xin{p}", [P, T, D]) for p in range(2)]
        cin = [sb(f"cin{p}", [P, T, D]) for p in range(2)]
        xres = [sb(f"xres{p}", [P, T, D]) for p in range(2)]
        xhat, xT = sb("xhat", [P, T, D]), sb("xT", [P, C, S])
        cT = [sb(f"cT{p}", [P, C, S]) for p in range(2)]
        cD = [sb(f"cD{p}", [P, C, S]) for p in range(2)]
        qp, kp = sb("qp", [P, 3, C, S], BF16), sb("kp", [P, 3, C, S], BF16)
        qr, kr = sb("qr", [P, C, S]), sb("kr", [P, C, S])
        qst = [sb(f"qst{p}", [P, NH, S], BF16) for p in range(2)]
        kst = [sb(f"kst{p}", [P, NH, S], BF16) for p in range(2)]
        vw = [sb(f"vw{p}", [P, T, NH, HW]) for p in range(2)]
        nmax = sb("nmax", [P, 2 * NH])
        nsp = sb("nsp", [2 * NH, 2, P], BF16)
        pt = [sb(f"pt{r}", [P, 4, S]) for r in range(4)]
        osb, on = sb("osb", [P, NG, S]), sb("on", [P, NG, S])
        rc = sb("rc", [P, NG, S])
        x1 = [sb(f"x1_{p}", [P, T, D]) for p in range(2)]
        xh2, x2T = sb("xh2", [P, T, D]), sb("x2T", [P, C, S])
        rl = sb("rl", [P, 2, 2, S])
        r2 = sb("r2", [P, FT, S])
        x2 = sb("x2", [P, T, D])
        yn, yT, ysq = sb("yn", [P, T, D]), sb("yT", [P, C, S]), sb("ysq", [P, C, S])
        bbs, dt_, dd = sb("bbs", [P, S]), sb("dt_", [P, T, S]), sb("dd", [P, T, S])
        aa = [sb(f"aa{p}", [P, T]) for p in range(2)]
        aaD = [sb(f"aaD{p}", [P, T]) for p in range(2)]
        junk = sb("junk", [P, D])
        wk_ = {"st": sb("ln_st", [P, 3 * T, 6]), "mv": sb("ln_mv", [P, 3 * T, 2]), "v": sb("ln_v", [P, 3 * T]),
               "y": sb("ln_y", [P, 3 * T]), "a": sb("ln_a", [P, 3 * T])}

        setup_weights(nc, io, dict(wqT=wqT, wkT=wkT, wvT=wvT, woT=woT, wfcT=wfcT, wprT=wprT, ident=ident,
                                   ones=ones, sel=sel, gates=gates, vw=vw, qst=qst, kst=kst))

        sc = [ctx.enter_context(nc.psum_tensor(f"sc{r}", [P, 4, S], F32)) for r in range(2)]
        oacc = ctx.enter_context(nc.psum_tensor("oacc", [P, 2, S], F32))
        wb = [ctx.enter_context(nc.psum_tensor(f"wb{r}", [P, 2, S], F32)) for r in range(3)]

        names = ["xhat_t", "ctx_t", "q_mm", "k_mm", "v_mm", "max_t", "sum_bc", "wo_mm", "xh2_t",
                 "fc_mm", "pr_mm", "y_t", "bb_mm", "ab_mm", "s1_mm", "s2_mm", "av_mm",
                 "xT_cp", "cT_cp", "qh_cp", "kh_cp", "vw_cp", "x2T_cp", "relu", "expd", "o_cp", "yT_cp", "bb_cp",
                 "dist", "aa_half", "aa_sum",
                 "ln1", "q_rem", "k_rem", "maxed", "max_split", "recip", "normed", "x1_res", "ln2", "x2_res", "ln3",
                 "d_part",
                 "q_parts_mid", "k_parts_mid", "q_parts", "k_parts", "squared", "y_sq", "maxrow_zero", "cD_cp",
                 "q_out", "k_out", "max_in", "x2_out", "d_out", "vchain", "sp_tick", "pool_tick"]
        e = {n: sem(n) for n in names}
        x_in = [sem(f"x_in{p}") for p in range(2)]
        c_in = [sem(f"c_in{p}") for p in range(2)]
        xr_in = [sem(f"xr_in{p}") for p in range(2)]
        q_in = [sem(f"q_in{p}") for p in range(2)]
        k_in = [sem(f"k_in{p}") for p in range(2)]
        NQ = len(Q_PARTS)
        FC_BANKS = (0, 1, 2, 0)

        tok = "(t p) d -> p t d"
        x_d, c_d = io["x"], io["ctx_1024"]
        block = ctx.enter_context(nc.Block())

        def run(iteration, eng, chain=None):
            iteration(Batch(-1, 1))
            for n in range(3):
                iteration(Batch(n // 2, n % 2))
            before = chain.n if chain else 0
            iteration(Batch(1, 1))
            start = chain.n if chain else 0
            step = 2 * (start - before)
            with eng.Fori(2, NB // 2 - 1) as h:
                if chain:
                    chain.base = (h - 2) * step
                iteration(Batch(h, 0))
                iteration(Batch(h, 1))
            if chain:
                assert chain.n - start == step
                chain.base = (NB // 2 - 4) * step
            for n in range(NB - 2, NB + 2):
                iteration(Batch(n // 2, n % 2))

        def there(b):
            return not isinstance(b.n, int) or 0 <= b.n < NB

        @block.sync
        def _(sp):
            def w(s, count, most=NB):
                done(sp, s, count, most, e["sp_tick"])

            def load_x_ctx(b):
                w(e["ln1"], b.n - 1)
                sp.dma_start(xin[b.p][:], x_d[b.n].rearrange(tok, p=P)).then_inc(x_in[b.p], 16)
                w(e["ctx_t"], b.n - 1)
                w(e["aa_sum"], b.n - 1)
                sp.dma_start(cin[b.p][:], c_d[b.n].rearrange(tok, p=P)).then_inc(c_in[b.p], 16)

            def load_res(b):
                w(e["x1_res"], b.n - 1)
                sp.dma_start(xres[b.p][:], x_d[b.n].rearrange(tok, p=P)).then_inc(xr_in[b.p], 16)

            def restack(b):
                for parts, made, out, dram, st, inn, order in (
                        (kp, "k_parts", "k_out", scr["k"], kst, k_in, K_PARTS),
                        (qp, "q_parts", "q_out", scr["q"], qst, q_in, Q_PARTS)):
                    w(e[made], b.n + 1)
                    w(inn[1 - b.p], 16 * NQ * (b.off(-1).half + 1), 16 * NQ * NB)
                    sp.dma_start(dram.rearrange("a (m p) t -> p (a m) t", p=P),
                                 parts[:].rearrange("p a m t -> p (a m) t")).then_inc(e[out], 16)
                    w(e["s2_mm"], NPAIR * (b.n - 1), NPAIR * NB)
                    w(e[out], 16 * (b.n + 1), 16 * NB)
                    for blk, part in enumerate(order):
                        sp.dma_start(st[b.p][DH * blk:DH * blk + DH, :, :],
                                     dram[part].rearrange("(h r) t -> r h t", r=DH)).then_inc(inn[b.p], 16)

            def max_rows(b):
                w(e["max_split"], b.n + 1)
                w(e["s1_mm"], NPAIR * (b.n + 1), NPAIR * NB)
                for part in range(2):
                    sp.dma_start(qst[b.p][MAXROW + part:MAXROW + part + 1, :, :].rearrange("o h (a t) -> o (h a) t", t=P),
                                 nsp[:, part:part + 1, :].rearrange("m o t -> m o t")).then_inc(e["max_in"], 16)

            def store_x2(b):
                w(e["x2_res"], b.n + 1)
                sp.dma_start(scr["x2"][b.n].rearrange(tok, p=P), x2[:]).then_inc(e["x2_out"], 16)

            def store_d(b):
                w(e["dist"], b.n + 1)
                sp.dma_start(scr["d"].rearrange("(t p) b s -> p t b s", p=P)[:, :, b.n, :], dd[:])\
                    .then_inc(e["d_out"], 16)

            load_x_ctx(Batch(0, 0))

            def iteration(i):
                if there(i.off(2)):
                    load_x_ctx(i.off(2))
                if there(i):
                    load_res(i)
                    max_rows(i)
                if there(i.off(-2)):
                    store_x2(i.off(-2))
                if there(i.off(1)):
                    restack(i.off(1))
                if there(i.off(-2)):
                    store_d(i.off(-2))
            run(iteration, sp)
            sp.wait_ge(e["x2_out"], 16 * NB)
            sp.wait_ge(e["d_out"], 16 * NB)

        @block.tensor
        def _(pe):
            def w(s, count, most=NB):
                done(pe, e[s] if isinstance(s, str) else s, count, most)

            def transposes(dst, src):
                for c in range(C):
                    for t in range(T):
                        last = pe.transpose(dst[:, c, t * P:t * P + P], src[:, t, c * P:c * P + P], ident[:])
                return last

            def turn_x(b):
                w("ln1", b.n + 1)
                w("max_split", b.n)
                w("qh_cp", b.n), w("q_rem", b.n)
                transposes(wb[0], xhat).then_inc(e["xhat_t"], 1)

            def turn_ctx(b):
                w(c_in[b.p], 16 * (b.half + 1), 16 * NB)
                w("vw_cp", b.n), w("x1_res", b.n - 1)
                transposes(wb[1], cin[b.p]).then_inc(e["ctx_t"], 1)

            def project(b, wt, src, bank, s):
                for m in range(C):
                    for c in range(C):
                        last = pe.matmul(wb[bank][:, m, :], wt[:, c, m * P:m * P + P], src[:, c, :],
                                         start=(c == 0), stop=(c == C - 1))
                last.then_inc(e[s], 1)

            def keys(b):
                w("cT_cp", b.n + 1)
                project(b, wkT, cT[b.p], 1, "k_mm")

            def queries(b):
                w("xT_cp", b.n + 1)
                project(b, wqT, xT, 0, "q_mm")

            def values_proj(b):
                w("kh_cp", b.n + 1), w("k_rem", b.n + 1)
                for t in range(T):
                    for c in range(C):
                        last = pe.matmul(wb[1][:, t, :], cT[b.p][:, c, t * P:t * P + P], wvT[:, c, :],
                                         start=(c == 0), stop=(c == C - 1))
                last.then_inc(e["v_mm"], 1)

            def sums(b, half):
                w("o_cp", NG * b.n + 2 * half + 2, NG * NB)
                w("x2_res", b.n - 1)
                w("recip", 2 * b.n + half, 2 * NB)
                for g in range(2):
                    last = pe.matmul(wb[2][:, g, :], sel[:], osb[:, 2 * half + g, :], start=True, stop=True)
                last.then_inc(e["sum_bc"], 1)

            def out_proj(b):
                w("normed", 2 * (b.n + 1), 2 * NB)
                w("relu", 4 * (b.n - 1) + 2, 4 * NB)
                w("vw_cp", b.n + 2)
                for t in range(T):
                    for g in range(NG):
                        last = pe.matmul(wb[1][:, t, :], on[:, g, t * P:t * P + P], woT[:, g, :],
                                         start=(g == 0), stop=(g == NG - 1))
                last.then_inc(e["wo_mm"], 1)

            def scores1(b, c):
                if c < 2:
                    w("expd", NPAIR * b.n + c - 1, NPAIR * NB)
                else:
                    w("maxed", NPAIR * b.n + c - 1, NPAIR * NB)
                if c == 0:
                    w(q_in[b.p], 16 * NQ * (b.half + 1), 16 * NQ * NB)
                    w(k_in[b.p], 16 * NQ * (b.half + 1), 16 * NQ * NB)
                    w("maxrow_zero", b.n - 1)
                for u in range(4):
                    h, t = 2 * c + u // 2, u % 2
                    last = pe.matmul(sc[c % 2][:, u, :], qst[b.p][:, h, t * P:t * P + P], kst[b.p][:, h, :],
                                     start=True, stop=True)
                last.then_inc(e["s1_mm"], 1)

            def max_transpose(b):
                w("maxed", NPAIR * (b.n + 1), NPAIR * NB)
                w("relu", 4 * (b.n - 1), 4 * NB)
                w("qh_cp", b.n + 1), w("q_rem", b.n + 1)
                pe.transpose(wb[0][0:2 * NH, 0, 0:P], nmax[:], ident[:]).then_inc(e["max_t"], 1)

            def scores2(b, c):
                if c < 2:
                    w("maxed", NPAIR * b.n + NPAIR - 1 + c, NPAIR * NB)
                else:
                    w("expd", NPAIR * b.n + c - 1, NPAIR * NB)
                if c == 0:
                    w("max_in", 32 * (b.n + 1), 32 * NB)
                for u in range(4):
                    h, t = 2 * c + u // 2, u % 2
                    last = pe.matmul(sc[c % 2][:, u, :], kst[b.p][:, h, t * P:t * P + P], qst[b.p][:, h, :],
                                     start=True, stop=True)
                last.then_inc(e["s2_mm"], 1)

            def values(b, g):
                w("expd", NPAIR * b.n + 2 * g + 2, NPAIR * NB)
                if g == 0:
                    w("vw_cp", b.n + 1)
                w("o_cp", NG * b.n + g, NG * NB)
                for t in range(T):
                    for j in range(HPG):
                        last = pe.matmul(oacc[HW * j:HW * j + HW, g % 2, :], vw[b.p][:, t, HPG * g + j, :],
                                         pt[(2 * g + j // 2) % 4][:, 2 * (j % 2) + t, :],
                                         start=(t == 0), stop=(t == T - 1))
                last.then_inc(e["av_mm"], 1)

            def xh2_transposes(b):
                w("ln2", b.n + 1)
                w("x1_res", b.n + 1), w("vw_cp", b.n + 3)
                transposes(wb[1], xh2).then_inc(e["xh2_t"], 1)

            def fc(b, k):
                bank = FC_BANKS[k]
                if k == 0:
                    w("x2T_cp", b.n + 1)
                    w("d_part", b.n), w("max_split", b.n + 2)
                    w("qh_cp", b.n + 3), w("q_rem", b.n + 3)
                elif k == 1:
                    w("bb_cp", b.n)
                elif k == 2:
                    w("recip", 2 * (b.n + 2), 2 * NB)
                elif k == 3:
                    w("relu", 4 * b.n + 1, 4 * NB)
                for j in range(2):
                    f = 2 * k + j
                    for c in range(C):
                        last = pe.matmul(wb[bank][:, j, :], wfcT[:, c, f * P:f * P + P], x2T[:, c, :],
                                         start=(c == 0), stop=(c == C - 1))
                last.then_inc(e["fc_mm"], 1)

            def proj(b, t):
                if t == 0:
                    w("relu", 4 * b.n + 3, 4 * NB)
                    w("squared", 4 * (b.n + 1), 4 * NB)
                for f in range(FT):
                    last = pe.matmul(wb[2][:, t, :], r2[:, f, t * P:t * P + P], wprT[:, f, :],
                                     start=(f == 0), stop=(f == FT - 1))
                if t == T - 1:
                    last.then_inc(e["pr_mm"], 1)

            def y_transposes(b):
                w("ln3", b.n + 1)
                w("qh_cp", b.n + 4), w("q_rem", b.n + 4)
                w("max_split", b.n + 3)
                transposes(wb[0], yn).then_inc(e["y_t"], 1)

            def row_norms(b):
                w("y_sq", b.n + 1)
                w("vw_cp", b.n + 4), w("x2T_cp", b.n + 2)
                for c in range(C):
                    last = pe.matmul(wb[1][:, 0, :], ones[:], ysq[:, c, :], start=(c == 0), stop=(c == C - 1))
                last.then_inc(e["bb_mm"], 1)

            def products(b):
                w("yT_cp", b.n + 1), w("cD_cp", b.n + 1)
                for t in range(T):
                    for c in range(C):
                        last = pe.matmul(wb[0][:, t, :], cD[b.p][:, c, t * P:t * P + P], yT[:, c, :],
                                         start=(c == 0), stop=(c == C - 1))
                last.then_inc(e["ab_mm"], 1)

            def iteration(i):
                a, z, y = i.off(1), i.off(-1), i.off(-2)
                for k in range(4):
                    if there(y):
                        fc(y, k)
                    if there(i):
                        scores1(i, 2 * k)
                        scores1(i, 2 * k + 1)
                if there(z):
                    out_proj(z)
                if there(i):
                    max_transpose(i)
                if there(y):
                    proj(y, 0)
                if there(a):
                    turn_x(a)
                    turn_ctx(a)
                if there(y):
                    proj(y, 1)
                for c in range(NPAIR):
                    if there(i):
                        scores2(i, c)
                        if c % 2 == 1 and c >= 3:
                            values(i, (c - 3) // 2)
                    if there(a):
                        if c == 0:
                            keys(a)
                        if c == 2:
                            queries(a)
                        if c == 4:
                            values_proj(a)
                    if there(i) and c == 6:
                        sums(i, 0)
                if there(y):
                    y_transposes(y)
                if there(i):
                    values(i, NG - 1)
                if there(z):
                    xh2_transposes(z)
                if there(y):
                    products(y)
                    row_norms(y)
                if there(i):
                    sums(i, 1)
            run(iteration, pe)

        @block.scalar
        def _(act):
            def w(s, count, most=NB):
                done(act, e[s] if isinstance(s, str) else s, count, most)

            def copy_group(b, g):
                w("av_mm", NG * b.n + g + 1, NG * NB)
                w("normed", 2 * (b.n - 1) + g // 2 + 1, 2 * NB)
                act.activation(osb[:, g, :], oacc[:, g % 2, :], ACT.Copy).then_inc(e["o_cp"], 1)

            def xT_copy(b):
                w("xhat_t", b.n + 1), w("q_mm", b.n)
                act.activation(xT[:], wb[0][:], ACT.Copy).then_inc(e["xT_cp"], 1)

            def cT_copy(b):
                w("ctx_t", b.n + 1), w("cD_cp", b.n - 1), w("v_mm", b.n - 1)
                act.activation(cT[b.p][:], wb[1][:], ACT.Copy).then_inc(e["cT_cp"], 1)

            def kh_copy(b):
                w("k_mm", b.n + 1), w("k_out", 16 * b.n, 16 * NB)
                act.activation(kp[:, 0, :, :], wb[1][:], ACT.Copy).then_inc(e["kh_cp"], 1)

            def qh_copy(b):
                w("q_mm", b.n + 1), w("q_out", 16 * b.n, 16 * NB)
                act.activation(qp[:, 0, :, :], wb[0][:], ACT.Copy, scale=1.0 / 16).then_inc(e["qh_cp"], 1)

            def middle_part(b, rem, r, parts, s):
                w(rem, b.n + 1)
                act.activation(parts[:, 1, :, :], r[:], ACT.Copy).then_inc(e[s], 1)

            def values_copy(b):
                w("v_mm", b.n + 1), w("av_mm", NG * (b.n - 1), NG * NB)
                for t in range(T):
                    last = act.activation(vw[b.p][:, t, :, 0:DH], wb[1][:, t, :].rearrange("p (h m) -> p h m", m=DH),
                                          ACT.Copy)
                last.then_inc(e["vw_cp"], 1)

            def ctx_squares(b):
                w("cD_cp", b.n - 1)
                for t in range(T):
                    if t:
                        act.wait_ge(e["aa_half"], b.n + 1)
                    ins = act.activation(junk[:], cin[b.p][:, t, :], ACT.Square, accum_out=aa[b.p][:, t:t + 1])
                    ins.then_inc(e["aa_half"] if t == 0 else e["aa_sum"], 1)

            def xh2_copy(b):
                w("xh2_t", b.n + 1), w("fc_mm", 4 * b.n, 4 * NB)
                act.activation(x2T[:], wb[1][:], ACT.Copy).then_inc(e["x2T_cp"], 1)

            def relu(b, k):
                w("fc_mm", 4 * b.n + k + 1, 4 * NB)
                w("squared", 4 * b.n + k - 1, 4 * NB)
                act.activation(rl[:, k % 2], wb[FC_BANKS[k]][:], ACT.Relu).then_inc(e["relu"], 1)

            def exps(b, c):
                w("s2_mm", NPAIR * b.n + c + 1, NPAIR * NB)
                w("av_mm", NG * b.n + c // 2 - 1, NG * NB)
                act.activation(pt[c % 4][:], sc[c % 2][:], ACT.Exp).then_inc(e["expd"], 1)

            def yT_copy(b):
                w("y_t", b.n + 1), w("ab_mm", b.n), w("y_sq", b.n)
                act.activation(yT[:], wb[0][:], ACT.Copy).then_inc(e["yT_cp"], 1)

            def bb_copy(b):
                w("bb_mm", b.n + 1), w("d_part", b.n)
                act.activation(bbs[:], wb[1][:, 0, :], ACT.Copy).then_inc(e["bb_cp"], 1)

            def distance(b):
                w("d_part", b.n + 1), w("d_out", 16 * b.n, 16 * NB), w("cD_cp", b.n + 1)
                for t in range(T):
                    last = act.activation(dd[:, t, :], dt_[:, t, :], ACT.Relu, bias=aaD[b.p][:, t:t + 1])
                last.then_inc(e["dist"], 1)

            def iteration(i):
                a, z, y = i.off(1), i.off(-1), i.off(-2)
                if there(y):
                    for k in range(4):
                        relu(y, k)
                if there(a):
                    xT_copy(a)
                    cT_copy(a)
                for c in range(NPAIR):
                    if there(i):
                        exps(i, c)
                        if c % 2 == 1 and c >= 3:
                            copy_group(i, (c - 3) // 2)
                    if there(a):
                        if c == 1:
                            kh_copy(a)
                        if c == 2:
                            middle_part(a, "k_rem", kr, kp, "k_parts_mid")
                        if c == 3:
                            qh_copy(a)
                        if c == 4:
                            middle_part(a, "q_rem", qr, qp, "q_parts_mid")
                        if c == 5:
                            values_copy(a)
                if there(y):
                    yT_copy(y)
                if there(z):
                    xh2_copy(z)
                if there(i):
                    copy_group(i, NG - 1)
                if there(y):
                    bb_copy(y)
                if there(a):
                    ctx_squares(a)
                if there(y):
                    distance(y)
            run(iteration, act)

        @block.vector
        def _(v):
            ch = Chain(v, e["vchain"])

            def w(s, count, most=NB):
                done(v, e[s] if isinstance(s, str) else s, count, most)

            def apply_norm(dst, src, s, slot):
                for t in range(T):
                    col = T * slot + t
                    last = v.tensor_scalar(dst[:, t, :], src[:, t, :], wk_["mv"][:, col, 0:1],
                                           wk_["y"][:, col:col + 1], ALU.subtract, ALU.mult)
                last.then_inc(e[s], 1)

            def x_moments(b):
                w(x_in[b.p], 16 * (b.half + 1), 16 * NB)
                moments(v, ch, xin[b.p], wk_, 0)

            def ln1(b):
                w("xhat_t", b.n)
                apply_norm(xhat, xin[b.p], "ln1", 0)

            def normalise(b, half):
                w("sum_bc", 2 * b.n + half + 1, 2 * NB), w("normed", 2 * b.n + half - 1, 2 * NB)
                g = slice(2 * half, 2 * half + 2)
                v.reciprocal(rc[:, g, :], wb[2][:]).then_inc(e["recip"], 1)
                w("recip", 2 * b.n + half + 1, 2 * NB), w("wo_mm", b.n)
                v.tensor_tensor(on[:, g, :], osb[:, g, :], rc[:, g, :], ALU.mult).then_inc(e["normed"], 1)

            def residual1(b):
                w("wo_mm", b.n + 1), w(xr_in[b.p], 16 * (b.half + 1), 16 * NB)
                w("x2_res", b.n - 1)
                v.scalar_tensor_tensor(x1[b.p][:], wb[1][:], gates[:, 0:1], xres[b.p][:], ALU.mult, ALU.add)\
                    .then_inc(e["x1_res"], 1)
                w("x1_res", b.n + 1)
                moments(v, ch, x1[b.p], wk_, 1)

            def ln2(b):
                w("xh2_t", b.n)
                apply_norm(xh2, x1[b.p], "ln2", 1)

            def k_remainder(b):
                w("k_mm", b.n + 1), w("kh_cp", b.n + 1), w("k_parts", b.n)
                v.tensor_tensor(kr[:], wb[1][:], kp[:, 0, :, :], ALU.subtract).then_inc(e["k_rem"], 1)

            def q_remainder(b):
                w("q_mm", b.n + 1), w("qh_cp", b.n + 1), w("q_parts", b.n)
                v.scalar_tensor_tensor(qr[:], wb[0][:], 1.0 / 16, qp[:, 0, :, :], ALU.mult, ALU.subtract)\
                    .then_inc(e["q_rem"], 1)

            def maxima(b, c):
                w("s1_mm", NPAIR * b.n + c + 1, NPAIR * NB)
                if c == 0:
                    w("max_t", b.n)
                v.tensor_reduce(nmax[:, 4 * c:4 * c + 4], sc[c % 2][:], AX.X, ALU.max, negate=True)\
                    .then_inc(e["maxed"], 1)

            def split_max(b):
                w("max_t", b.n + 1), w("max_in", 32 * b.n, 32 * NB)
                ch.link(v.tensor_copy(nsp[:, 0, :], wb[0][0:2 * NH, 0, 0:P]))
                v.tensor_tensor(nsp[:, 1, :], wb[0][0:2 * NH, 0, 0:P], nsp[:, 0, :], ALU.subtract)\
                    .then_inc(e["max_split"], 1)

            def residual2(b):
                w("pr_mm", b.n + 1), w("x2_out", 16 * b.n, 16 * NB)
                v.scalar_tensor_tensor(x2[:], wb[2][:], gates[:, 2:3], x1[b.p][:], ALU.mult, ALU.add)\
                    .then_inc(e["x2_res"], 1)
                w("x2_res", b.n + 1)
                moments(v, ch, x2, wk_, 2)

            def ln3(b):
                w("y_t", b.n)
                apply_norm(yn, x2, "ln3", 2)

            def distance_part(b):
                w("ab_mm", b.n + 1), w("bb_cp", b.n + 1), w("dist", b.n)
                for t in range(T):
                    last = v.scalar_tensor_tensor(dt_[:, t, :], wb[0][:, t, :], -2.0, bbs[:], ALU.mult, ALU.add)
                last.then_inc(e["d_part"], 1)

            x_moments(Batch(0, 0))
            norm_factors(v, ch, wk_, 0, 1)
            ln1(Batch(0, 0))
            w("ln1", 1)

            def iteration(i):
                a, nx, z, y = i.off(1), i.off(2), i.off(-1), i.off(-2)
                if there(i):
                    for c in range(NPAIR):
                        maxima(i, c)
                    split_max(i)
                slots = [k for k, b in enumerate((nx, z, y)) if there(b)]
                if there(z):
                    residual1(z)
                if there(nx):
                    x_moments(nx)
                if there(y):
                    residual2(y)
                if there(a):
                    k_remainder(a)
                if slots:
                    norm_factors(v, ch, wk_, slots[0], slots[-1] + 1)
                if there(y):
                    ln3(y)
                if there(a):
                    q_remainder(a)
                if there(z):
                    ln2(z)
                if there(nx):
                    ln1(nx)
                if there(y):
                    w("ln3", y.n + 1)
                if there(z):
                    w("ln2", z.n + 1)
                if there(nx):
                    w("ln1", nx.n + 1)
                if there(i):
                    normalise(i, 0)
                if there(y):
                    distance_part(y)
                if there(i):
                    normalise(i, 1)
            run(iteration, v, ch)

        @block.gpsimd
        def _(pool):
            def w(s, count, most=NB):
                done(pool, e[s], count, most, e["pool_tick"])

            def parts(b):
                for made, r, pt_ in (("k_parts", kr, kp), ("q_parts", qr, qp)):
                    w(made + "_mid", b.n + 1)
                    pool.tensor_tensor(pt_[:, 2, :, :], r[:], pt_[:, 1, :, :], ALU.subtract).then_inc(e[made], 1)

            def squares(b):
                for k in range(4):
                    w("relu", 4 * b.n + k + 1, 4 * NB)
                    if k == 0:
                        w("pr_mm", b.n)
                    pool.tensor_tensor(r2[:, 2 * k:2 * k + 2, :], rl[:, k % 2], rl[:, k % 2], ALU.mult)\
                        .then_inc(e["squared"], 1)

            def y_squares(b):
                w("yT_cp", b.n + 1), w("bb_mm", b.n)
                pool.tensor_tensor(ysq[:], yT[:], yT[:], ALU.mult).then_inc(e["y_sq"], 1)

            def zero_max_rows(b):
                w("s2_mm", NPAIR * (b.n + 1), NPAIR * NB)
                w("cD_cp", b.n + 1)
                pool.memset(qst[b.p][MAXROW:MAXROW + 2, :, :].bitcast(F32), 0.0).then_inc(e["maxrow_zero"], 1)
                w("maxrow_zero", b.n + 1)

            def keep_ctx(b):
                w("aa_sum", b.n + 1), w("dist", b.n - 1)
                pool.tensor_copy(aaD[b.p][:], aa[b.p][:])
                w("cT_cp", b.n + 1), w("ab_mm", b.n - 1)
                pool.tensor_copy(cD[b.p][:], cT[b.p][:]).then_inc(e["cD_cp"], 1)

            def iteration(i):
                a, z, y = i.off(1), i.off(-1), i.off(-2)
                if there(z):
                    keep_ctx(z)
                    zero_max_rows(z)
                if there(y):
                    squares(y)
                if there(a):
                    parts(a)
                if there(y):
                    y_squares(y)
            run(iteration, pool)


def setup_weights(nc, io, o):
    with ExitStack() as ctx:
        def sb(name, shape, dt=F32):
            return ctx.enter_context(nc.sbuf_tensor(name, shape, dt))

        def sem(name):
            return ctx.enter_context(nc.semaphore(name))

        raw = {n: sb("raw_" + n, [P, C, D]) for n in ("wq", "wk", "wv", "wo")}
        wfc, wpr = sb("wfc", [P, FT, D]), sb("wpr", [P, C, F])
        u, vv, fbT = sb("u", [P, FT, RANK]), sb("vv", [RANK, D]), sb("fbT", [RANK, RANK])
        uT, fbv = sb("uT", [RANK, F]), sb("fbv", [RANK, D])
        wop = sb("wop", [P, C, NH, HW])
        scl = sb("scl", [P, FT + C])
        rsc = sb("rsc", [P, FT + C])
        gin = sb("gin", [P, 5])
        ps = [ctx.enter_context(nc.psum_tensor(f"su{r}", [P, 512], F32)) for r in range(4)]
        loaded, consts, quant, turned, copied, tanhd, vch = (sem(n) for n in (
            "w_loaded", "consts", "quantised", "turned", "copied", "tanhd", "w_chain"))
        pch = sem("w_pool_chain")
        block = ctx.enter_context(nc.Block())
        NLOAD = 12

        @block.sync
        def _(sp):
            for n in ("wq", "wk", "wv", "wo"):
                sp.dma_start(raw[n][:], io["L0_xattn_" + n].rearrange("(a p) d -> p a d", p=P)).then_inc(loaded, 16)
            sp.dma_start(wfc[:], io["L0_ffn_w_fc"].rearrange("(a p) d -> p a d", p=P)).then_inc(loaded, 16)
            sp.dma_start(wpr[:], io["L0_ffn_w_proj"].rearrange("(a p) f -> p a f", p=P)).then_inc(loaded, 16)
            sp.dma_start(u[:], io["L0_ffn_u"].rearrange("(a p) r -> p a r", p=P)).then_inc(loaded, 16)
            sp.dma_start(vv[:], io["L0_ffn_v"]).then_inc(loaded, 16)
            sp.dma_start(fbT[:], io["L0_ffn_fast_b"].rearrange("a b -> b a"), allow_slow_non_contiguous=True)\
                .then_inc(loaded, 16)
            sp.dma_start(gin[:, 0:2], io["g_xattn"].partition_broadcast(P)).then_inc(loaded, 16)
            sp.dma_start(gin[:, 2:4], io["g_ffn"].partition_broadcast(P)).then_inc(loaded, 16)
            sp.dma_start(gin[:, 4:5], io["L0_ffn_gate"].partition_broadcast(P)).then_inc(loaded, 16)
            sp.wait_ge(loaded, 16 * NLOAD)

        @block.gpsimd
        def _(pool):
            pc = Chain(pool, pch)
            pc.link(pool.memset(o["ident"][:], 0.0))
            pc.link(pool.memset(o["sel"][:], 1.0))
            pc.link(pool.memset(o["ones"][:], 1.0))
            pc.link(pool.memset(wop[:], 0.0))
            for p in range(2):
                pc.link(pool.memset(o["vw"][p][:], 0.0))
                pc.link(pool.memset(o["qst"][p][MAXROW:P, :, :], 0.0))
                pc.link(pool.memset(o["kst"][p][MAXROW:P, :, :], 0.0))
            pc.link(pool.affine_select(out=o["ident"][:], in_=o["ident"][:], compare_op=ALU.not_equal, fill=1.0,
                                       base=0, pattern=[[-1, P]], channel_multiplier=1))
            for k in range(HPG):
                blk = o["sel"][:, HW * k:HW * k + HW]
                pc.link(pool.affine_select(out=blk, in_=blk, compare_op=ALU.is_equal, fill=0.0,
                                           base=-(HW * k + DH), pattern=[[0, HW]], channel_multiplier=1))
            for p in range(2):
                pc.link(pool.memset(o["kst"][p][MAXROW:MAXROW + 2, :, :], 1.0))
                pc.link(pool.memset(o["vw"][p][:, :, :, DH:DH + 1], 1.0))
            pool.wait_ge(loaded, 16 * NLOAD)
            pc.link(pool.tensor_copy(wop[:, :, :, 0:DH], raw["wo"][:].rearrange("p a (h m) -> p a h m", m=DH)))
            pool.sem_inc(consts, 1)

        @block.scalar
        def _(act):
            act.wait_ge(loaded, 16 * NLOAD)
            act.activation(o["gates"][:], gin[:, 0:4], ACT.Tanh).then_inc(tanhd, 1)
            act.wait_ge(tanhd, 1)

        jobs = []
        for n in ("wq", "wk", "wv"):
            for a in range(C):
                for c in range(C):
                    jobs.append((raw[n][:, a, c * P:c * P + P], o[n + "T"][:, c, a * P:a * P + P], P, None))
        for g in range(NG):
            for a in range(C):
                jobs.append((wop[:, a, HPG * g:HPG * g + HPG, :].rearrange("p h m -> p (h m)"),
                             o["woT"][:, g, a * P:a * P + P], P, None))
        for a in range(C):
            for f in range(FT):
                jobs.append((wpr[:, a, f * P:f * P + P], o["wprT"][:, f, a * P:a * P + P], P, None))
        for f in range(FT):
            for c in range(C):
                jobs.append((wfc[:, f, c * P:c * P + P], o["wfcT"][:, c, f * P:f * P + P], P, (f, c)))

        @block.vector
        def _(v):
            ch = Chain(v, vch)
            v.wait_ge(loaded, 16 * NLOAD)
            quantise_rows(v, ch, wfc, scl[:, 0:FT], rsc[:, 0:FT], FT, D)
            quantise_rows(v, ch, wpr, scl[:, FT:FT + C], rsc[:, FT:FT + C], C, F)
            v.sem_inc(quant, 1)
            for f in range(FT):
                v.wait_ge(turned, f + 1)
                v.tensor_copy(uT[:, f * P:f * P + P], ps[f % 2][0:RANK, 0:P]).then_inc(copied, 1)
            v.wait_ge(turned, FT + 1)
            v.tensor_copy(fbv[:], ps[2][0:RANK, 0:D]).then_inc(copied, 1)
            for k, (_, dst, rows, lowrank) in enumerate(jobs):
                v.wait_ge(turned, FT + 2 + k)
                if lowrank is None:
                    v.tensor_copy(dst, ps[k % 2][0:rows, 0:P]).then_inc(copied, 1)
                else:
                    ch.link(v.tensor_copy(dst, ps[k % 2][0:rows, 0:P]))
                    v.scalar_tensor_tensor(dst, ps[2 + k % 2][0:rows, 0:P], gin[:, 4:5], dst, ALU.mult, ALU.add)\
                        .then_inc(copied, 1)
            v.wait_ge(copied, FT + 1 + len(jobs))

        @block.tensor
        def _(pe):
            pe.wait_ge(consts, 1)
            pe.wait_ge(loaded, 16 * NLOAD)
            for f in range(FT):
                if f >= 2:
                    pe.wait_ge(copied, f - 1)
                pe.transpose(ps[f % 2][0:RANK, 0:P], u[:, f, :], o["ident"][:]).then_inc(turned, 1)
            pe.matmul(ps[2][0:RANK, 0:D], fbT[:], vv[:], start=True, stop=True).then_inc(turned, 1)
            pe.wait_ge(quant, 1)
            for k, (src, _, rows, lowrank) in enumerate(jobs):
                pe.wait_ge(copied, FT + k if k < 2 else FT + k)
                if lowrank is not None:
                    f, c = lowrank
                    pe.matmul(ps[2 + k % 2][:, 0:P], fbv[:, c * P:c * P + P], uT[:, f * P:f * P + P],
                              start=True, stop=True)
                pe.transpose(ps[k % 2][0:rows, 0:P], src, o["ident"][:]).then_inc(turned, 1)


def quantise_rows(v, ch, w, scl, rsc, n, width):
    for a in range(n):
        ch.tick(v.tensor_reduce(scl[:, a:a + 1], w[:, a, :], AX.X, ALU.add, apply_absolute_value=True))
    ch.hold()
    ch.link(v.tensor_scalar(scl, scl, 1.0 / width, 1e-5, ALU.mult, ALU.max))
    ch.link(v.reciprocal(rsc, scl))
    for a in range(n):
        ch.tick(v.tensor_scalar(w[:, a, :], w[:, a, :], rsc[:, a:a + 1], MAGIC, ALU.mult, ALU.add))
    ch.hold()
    for a in range(n):
        ch.tick(v.tensor_scalar(w[:, a, :], w[:, a, :], MAGIC, 1.0, ALU.subtract, ALU.min))
    ch.hold()
    for a in range(n):
        ch.tick(v.tensor_scalar(w[:, a, :], w[:, a, :], -1.0, scl[:, a:a + 1], ALU.max, ALU.mult))
    ch.hold()


def alignment_phase(nc, io, scr):
    with ExitStack() as ctx:
        def sb(name, shape, dt=F32):
            return ctx.enter_context(nc.sbuf_tensor(name, shape, dt))

        def sem(name):
            return ctx.enter_context(nc.semaphore(name))

        dist = [sb(f"rows_d{p}", [NB, ROWS, S]) for p in range(2)]
        cost = [sb(f"rows_r{p}", [NB, ROWS, S + 1]) for p in range(2)]
        best = sb("best", [NB, S])
        d_in = [sem(f"d_in{p}") for p in range(2)]
        r_out = [sem(f"r_out{p}") for p in range(2)]
        v_out, rooted, costed, edge, rch, tick = (sem(n) for n in ("virtual_out", "rooted", "costed", "edge", "row_chain", "sp_tick2"))
        block = ctx.enter_context(nc.Block())
        dram_d = scr["d"].rearrange("i b s -> b i s")

        @block.sync
        def _(sp):
            sp.dma_start(dist[0][:], dram_d[:, 0:ROWS, :]).then_inc(d_in[0], 16)
            sp.dma_start(dist[1][:], dram_d[:, ROWS:2 * ROWS, :]).then_inc(d_in[1], 16)
            sp.wait_ge(edge, 1)
            sp.dma_start(scr["r"][:, 0:1, :], cost[1][:, ROWS - 1:ROWS, :]).then_inc(v_out, 16)
            sp.wait_ge(v_out, 16)
            sp.sem_inc(edge, 1)

            def chunk(h, p, more):
                done(sp, costed, 2 * h + p + 1, NCH, tick)
                sp.dma_start(scr["r"][:, bass.ds((2 * h + p) * ROWS + 1, ROWS), :], cost[p][:]).then_inc(r_out[p], 16)
                if more:
                    sp.dma_start(dist[p][:], dram_d[:, bass.ds((2 * h + p + 2) * ROWS, ROWS), :]).then_inc(d_in[p], 16)
            with sp.Fori(0, NCH // 2 - 1) as h:
                chunk(h, 0, True)
                chunk(h, 1, True)
            chunk(NCH // 2 - 1, 0, False)
            chunk(NCH // 2 - 1, 1, False)
            for p in range(2):
                sp.wait_ge(r_out[p], 16 * NCH // 2)

        @block.scalar
        def _(act):
            def chunk(h, p):
                act.wait_ge(d_in[p], 16 * (h + 1))
                act.activation(dist[p][:], dist[p][:], ACT.Sqrt).then_inc(rooted, 1)
            with act.Fori(0, NCH // 2) as h:
                chunk(h, 0)
                chunk(h, 1)

        @block.vector
        def _(v):
            ch = Chain(v, rch)
            ch.link(v.memset(cost[0][:, :, 0:1], BIG))
            ch.link(v.memset(cost[1][:, :, 0:1], BIG))
            ch.link(v.memset(cost[1][:, ROWS - 1, :], BIG))
            ch.link(v.memset(cost[1][:, ROWS - 1, 0:1], 0.0))
            v.sem_inc(edge, 1)
            v.wait_ge(edge, 2)

            def chunk(h, p, full):
                v.wait_ge(rooted, 2 * h + p + 1)
                if full:
                    v.wait_ge(r_out[p], 16 * h)
                for i in range(ROWS):
                    prev = cost[p][:, i - 1, :] if i else cost[1 - p][:, ROWS - 1, :]
                    ch.link(v.tensor_tensor(best[:], prev[:, 1:S + 1], prev[:, 0:S], ALU.min))
                    row = v.tensor_tensor_scan(cost[p][:, i, 1:S + 1], best[:], dist[p][:, i, :], BIG, ALU.min, ALU.add)
                    ch.link(row)
                v.sem_inc(costed, 1)

            chunk(0, 0, False)
            ch.link(v.memset(cost[1][:, ROWS - 1, 0:1], BIG))
            chunk(0, 1, False)
            start = ch.n
            with v.Fori(1, NCH // 2) as h:
                ch.base = (h - 1) * (4 * ROWS)
                chunk(h, 0, True)
                chunk(h, 1, True)
            assert ch.n - start == 4 * ROWS


def path_phase(nc, io, scr, vin, vout):
    with ExitStack() as ctx:
        def sb(name, shape, dt=F32):
            return ctx.enter_context(nc.sbuf_tensor(name, shape, dt))

        def sem(name):
            return ctx.enter_context(nc.semaphore(name))

        W = S + 1
        cur = [sb(f"cur{p}", [P, T, W]) for p in range(2)]
        prv = [sb(f"prv{p}", [P, T, W]) for p in range(2)]
        m, dg, nl = sb("m", [P, T, S]), sb("dg", [P, T, S]), sb("nl", [P, T, S])
        hh = sb("hh", [P, T, S])
        last_ = sb("last_", [P, T, W])
        step = [sb(f"step{p}", [P, T, S]) for p in range(2)]
        iota = sb("iota", [P, T, S])
        ident = sb("ident2", [NB, NB])
        rows = [sb(f"rows_g{p}", [NB, ROWS, S]) for p in range(2)]
        hop = sb("hop", [NB, S])
        cell = sb("cell", [NB, ROWS + 1])
        path = sb("path", [NB, S + 1])
        ps = [ctx.enter_context(nc.psum_tensor(f"pp{r}", [P, 512], F32)) for r in range(4)]
        r_in = [sem(f"rr_in{p}") for p in range(2)]
        g_out = [sem(f"g_out{p}") for p in range(2)]
        g_in = [sem(f"g_in{p}") for p in range(2)]
        consts, used, pch, vch, held, ran, copied, stepped, turned, tick = (sem(n) for n in (
            "consts2", "cells_used", "pool_chain2", "v_chain2", "held", "ran", "path_cp", "stepped", "turned2", "sp_tick3"))
        ptick, gdone = sem("pool_tick3"), sem("chunk_used")
        block = ctx.enter_context(nc.Block())

        @block.sync
        def _(sp):
            def load(n, h, p):
                sp.dma_start(cur[p][:], scr["r"][n, 1:S + 1, :].rearrange("(t p) s -> p t s", p=P)).then_inc(r_in[p], 16)
                sp.dma_start(prv[p][:], scr["r"][n, 0:S, :].rearrange("(t p) s -> p t s", p=P)).then_inc(r_in[p], 16)

            def store(n, h, p):
                done(sp, stepped, n + 1, NB, tick)
                sp.dma_start(scr["g"].rearrange("(t p) b s -> p t b s", p=P)[:, :, n, :], step[p][:]).then_inc(g_out[p], 16)
            load(0, 0, 0)
            load(1, 0, 1)
            with sp.Fori(0, NB // 2 - 1) as h:
                for p in range(2):
                    store(2 * h + p, h, p)
                    done(sp, used, 2 * h + p + 1, NB, tick)
                    load(2 * h + p + 2, h + 1, p)
            store(NB - 2, 0, 0)
            store(NB - 1, 0, 1)
            for p in range(2):
                sp.wait_ge(g_out[p], 16 * NB // 2)
            dram_g = scr["g"].rearrange("i b s -> b i s")

            def rows_in(k, p):
                sp.dma_start(rows[p][:], dram_g[:, bass.ds((NCH - 1 - k) * ROWS, ROWS), :]).then_inc(g_in[p], 16)
            rows_in(0, 0)
            rows_in(1, 1)
            with sp.Fori(0, NCH // 2 - 1) as h:
                for p in range(2):
                    done(sp, gdone, 2 * h + p + 1, NCH, tick)
                    rows_in(2 * h + p + 2, p)

        @block.gpsimd
        def _(pool):
            pc = Chain(pool, pch)
            pc.link(pool.iota(iota[:], pattern=[[0, T], [1, S]], base=0, channel_multiplier=0,
                              allow_small_or_imprecise_dtypes=True))
            pc.link(pool.memset(ident[:], 0.0))
            pc.link(pool.affine_select(out=ident[:], in_=ident[:], compare_op=ALU.not_equal, fill=1.0,
                                       base=0, pattern=[[-1, NB]], channel_multiplier=1))
            pc.link(pool.memset(last_[:, :, 0:1], 0.0))
            pool.sem_inc(consts, 1)

            def seq(n, h, p, full):
                done(pool, ran, n + 1, NB, ptick)
                if full:
                    done(pool, g_out[p], 16 * h, 16 * NB, ptick)
                pool.tensor_tensor(step[p][:], last_[:, :, 1:W], last_[:, :, 0:S], ALU.subtract).then_inc(stepped, 1)
            seq(0, 0, 0, False)
            seq(1, 0, 1, False)
            with pool.Fori(1, NB // 2) as h:
                seq(2 * h, h, 0, True)
                seq(2 * h + 1, h, 1, True)

        @block.vector
        def _(v):
            ch = Chain(v, vch)
            v.wait_ge(consts, 1)

            def seq(n, h, p, full):
                v.wait_ge(r_in[p], 32 * (h + 1))
                c, r = cur[p], prv[p]
                ch.tick(v.tensor_tensor(m[:], r[:, :, 1:W], r[:, :, 0:S], ALU.min))
                ch.tick(v.tensor_tensor(dg[:], r[:, :, 0:S], r[:, :, 1:W], ALU.is_le))
                ch.hold()
                ch.tick(v.tensor_tensor(nl[:], m[:], c[:, :, 0:S], ALU.is_le))
                ch.tick(v.scalar_tensor_tensor(hh[:], dg[:], -0.75, iota[:], ALU.mult, ALU.add))
                ch.hold()
                v.sem_inc(used, 1)
                ch.link(v.tensor_tensor(hh[:], hh[:], nl[:], ALU.mult))
                if full:
                    v.wait_ge(stepped, n)
                for t in range(T):
                    last = v.tensor_tensor_scan(last_[:, t, 1:W], hh[:, t, :], hh[:, t, :], 0.0, ALU.max, ALU.max)
                last.then_inc(ran, 1)
            seq(0, 0, 0, False)
            seq(1, 0, 1, True)
            start = ch.n
            with v.Fori(1, NB // 2) as h:
                ch.base = (h - 1) * 10
                seq(2 * h, h, 0, True)
                seq(2 * h + 1, h, 1, True)
            assert ch.n - start == 10
            ch.base = (NB // 2 - 2) * 10

            ch.link(v.memset(path[:], 0.0))
            ch.link(v.memset(path[:, S:S + 1], float(S - 1)))
            ch.link(v.memset(cell[:, 0:1], float(S - 1)))

            def chunk(k, h, p):
                v.wait_ge(g_in[p], 16 * (h + 1))
                ch.link(v.tensor_copy(cell[:, ROWS:ROWS + 1], cell[:, 0:1]))
                for i in range(ROWS - 1, -1, -1):
                    ch.link(v.scalar_tensor_tensor(hop[:], iota[0:NB, 0, :], cell[:, i + 1:i + 2], rows[p][:, i, :],
                                                   ALU.is_le, ALU.mult, accum_out=cell[:, i:i + 1]))
                ch.link(v.tensor_copy(path[:, bass.ds((NCH - 1 - k) * ROWS, ROWS)], cell[:, 0:ROWS]))
                v.sem_inc(gdone, 1)
            start, base = ch.n, ch.base
            with v.Fori(0, NCH // 2) as h:
                ch.base = h * (2 * (ROWS + 2)) + base
                chunk(2 * h, h, 0)
                chunk(2 * h + 1, h, 1)
            assert ch.n - start == 2 * (ROWS + 2)
            ch.base = base + (NCH // 2 - 1) * 2 * (ROWS + 2)
            ch.link(v.memset(path[:, 0:1], 0.0))
            v.sem_inc(held, 1)
            for t in range(T):
                v.wait_ge(turned, 2 * t + 2)
                v.tensor_copy(vout[:, t, :], ps[2 * t][:, 0:NB]).then_inc(copied, 1)
                v.tensor_copy(vin[:, t, :], ps[2 * t + 1][:, 0:NB]).then_inc(copied, 1)
            v.wait_ge(copied, 2 * T)

        @block.tensor
        def _(pe):
            pe.wait_ge(consts, 1)
            pe.wait_ge(held, 1)
            for t in range(T):
                pe.transpose(ps[2 * t][:, 0:NB], path[:, t * P:t * P + P], ident[:]).then_inc(turned, 1)
                pe.transpose(ps[2 * t + 1][:, 0:NB], path[:, t * P + 1:t * P + P + 1], ident[:]).then_inc(turned, 1)


def last_layer_phase(nc, io, scr, vin, vout, out):
    with ExitStack() as ctx:
        def sb(name, shape, dt=F32):
            return ctx.enter_context(nc.sbuf_tensor(name, shape, dt))

        def sem(name):
            return ctx.enter_context(nc.semaphore(name))

        w1T, w2T = sb("w1T", [P, C, F], BF16), sb("w2T", [P, FT, D], BF16)
        identb, iota = sb("identb", [P, P], BF16), sb("iota3", [P, S])
        gates, wscale = sb("gates3", [P, 4]), sb("wscale", [P, 2])
        b1, b2 = sb("b1", [P, F]), sb("b2", [P, D])
        setup_last_weights(nc, io, dict(w1T=w1T, w2T=w2T, identb=identb, iota=iota, gates=gates, wscale=wscale,
                                        b1=b1, b2=b2))

        x2 = [sb(f"x2_{p}", [P, T, D]) for p in range(2)]
        cx = [sb(f"cx_{p}", [P, T, D]) for p in range(2)]
        before_, mask = sb("before_", [P, T, S]), sb("mask", [P, T, S])
        x3 = sb("x3", [P, T, D])
        x3b = [sb(f"x3b{p}", [P, T, D]) for p in range(2)]
        xc, xr = sb("xc", [P, T, D]), sb("xr", [P, T, D])
        xq, xqT = sb("xq", [P, T, D], BF16), sb("xqT", [P, C, S], BF16)
        st, mv = sb("st3", [P, T, 6]), sb("mv3", [P, T, 2])
        var, amax, y, tmp, q = (sb(n, [P, 2 * T]) for n in ("var4", "amax4", "y4", "tmp4", "q4"))
        back_ = [sb(f"back{p}", [P, 2 * T]) for p in range(2)]
        hb = [sb(f"hb{t}", [P, F]) for t in range(T)]
        gl = [sb(f"gl{t}", [P, F]) for t in range(T)]
        sq = sb("sq", [P, F])
        ssum = sb("ssum", [P, T])
        hr_ = [sb(f"hr{t}", [P, F]) for t in range(T)]
        hq = [sb(f"hq{t}", [P, F], BF16) for t in range(T)]
        hqT = [sb(f"hqT{t}", [P, FT, P], BF16) for t in range(T)]
        xo = [sb(f"xo{p}", [P, T, D]) for p in range(2)]

        pe_x = ctx.enter_context(nc.psum_tensor("pe_x", [P, T, D], F32))
        pt_x = ctx.enter_context(nc.psum_tensor("pt_x", [P, C, S], BF16))
        ph = [ctx.enter_context(nc.psum_tensor(f"ph{t}", [P, F], F32)) for t in range(T)]
        pt_h = ctx.enter_context(nc.psum_tensor("pt_h", [P, FT, P], BF16))
        po = ctx.enter_context(nc.psum_tensor("po", [P, T, D], F32))

        names = ["expand", "xq_t", "h_mm", "hq_t", "o_mm",
                 "xqT_cp", "gelu", "squares", "hqT_cp", "x_round",
                 "masked", "x3_res", "x_scaled", "h_bias", "h_scaled", "x4_res",
                 "x3_bias", "h_round", "chain3", "tick_sp3", "tick_pool3"]
        e = {n: sem(n) for n in names}
        x_in = [sem(f"x2_in{p}") for p in range(2)]
        o_out = [sem(f"o_out{p}") for p in range(2)]
        block = ctx.enter_context(nc.Block())
        tok = "(t p) d -> p t d"

        def there(b):
            return not isinstance(b.n, int) or 0 <= b.n < NB

        def run(iteration, eng, chain=None):
            for n in range(-2, 3):
                iteration(Batch(n // 2, n % 2))
            before = chain.n if chain else 0
            iteration(Batch(1, 1))
            start = chain.n if chain else 0
            step = 2 * (start - before)
            with eng.Fori(2, NB // 2 - 2) as h:
                if chain:
                    chain.base = (h - 2) * step
                iteration(Batch(h, 0))
                iteration(Batch(h, 1))
            if chain:
                assert chain.n - start == step
                chain.base = (NB // 2 - 5) * step
            iteration(Batch(NB // 2 - 2, 0))
            iteration(Batch(NB // 2 - 2, 1))
            iteration(Batch(NB // 2 - 1, 0))
            iteration(Batch(NB // 2 - 1, 1))
            iteration(Batch(NB // 2, 0))

        @block.sync
        def _(sp):
            def w(s, count, most=NB):
                done(sp, s, count, most, e["tick_sp3"])

            def load(b):
                w(e["expand"], b.n - 1)
                w(e["x3_res"], b.n - 1)
                sp.dma_start(x2[b.p][:], scr["x2"][b.n].rearrange(tok, p=P)).then_inc(x_in[b.p], 16)
                sp.dma_start(cx[b.p][:], io["ctx_1024"][b.n].rearrange(tok, p=P)).then_inc(x_in[b.p], 16)

            def store(b):
                w(e["x4_res"], b.n + 1)
                sp.dma_start(out[b.n].rearrange(tok, p=P), xo[b.p][:]).then_inc(o_out[b.p], 16)
            load(Batch(0, 0))

            def iteration(i):
                if there(i.off(3)):
                    load(i.off(3))
                if there(i.off(-1)):
                    store(i.off(-1))
            run(iteration, sp)
            for p in range(2):
                sp.wait_ge(o_out[p], 16 * NB // 2)

        @block.tensor
        def _(pe):
            def w(s, count, most=NB):
                done(pe, e[s] if isinstance(s, str) else s, count, most)

            def expand(b):
                w("masked", b.n + 1), w("x3_res", b.n)
                w(x_in[b.p], 32 * (b.half + 1), 32 * NB)
                for j in range(T):
                    for t in range(T):
                        last = pe.matmul(pe_x[:, j, :], mask[:, t, j * P:j * P + P], cx[b.p][:, t, :],
                                         start=(t == 0), stop=(t == T - 1))
                last.then_inc(e["expand"], 1)

            def hidden(b):
                w("x_round", b.n + 1), w("xqT_cp", b.n)
                for c in range(C):
                    for t in range(T):
                        last = pe.transpose(pt_x[:, c, t * P:t * P + P], xq[:, t, c * P:c * P + P], identb[:])
                last.then_inc(e["xq_t"], 1)
                w("xqT_cp", b.n + 1)
                for t in range(T):
                    w("h_bias", 2 * b.n + t - 1, 2 * NB)
                    for j in range(2):
                        for c in range(C):
                            last = pe.matmul(ph[t][:, 512 * j:512 * j + 512], xqT[:, c, t * P:t * P + P],
                                             w1T[:, c, 512 * j:512 * j + 512], start=(c == 0), stop=(c == C - 1))
                    last.then_inc(e["h_mm"], 1)

            def output(b):
                for t in range(T):
                    w("h_round", 2 * b.n + t + 1, 2 * NB), w("hqT_cp", 2 * b.n + t, 2 * NB)
                    for f in range(FT):
                        last = pe.transpose(pt_h[:, f, :], hq[t][:, f * P:f * P + P], identb[:])
                    last.then_inc(e["hq_t"], 1)
                w("x4_res", b.n)
                for t in range(T):
                    w("hqT_cp", 2 * b.n + t + 1, 2 * NB)
                    for f in range(FT):
                        last = pe.matmul(po[:, t, :], hqT[t][:, f, :], w2T[:, f, :], start=(f == 0), stop=(f == FT - 1))
                last.then_inc(e["o_mm"], 1)

            def iteration(i):
                if there(i.off(2)):
                    expand(i.off(2))
                if there(i.off(1)):
                    hidden(i.off(1))
                if there(i):
                    output(i)
            run(iteration, pe)

        @block.scalar
        def _(act):
            def w(s, count, most=NB):
                done(act, e[s] if isinstance(s, str) else s, count, most)

            def activate(b):
                for t in range(T):
                    w("h_bias", 2 * b.n + t + 1, 2 * NB), w("h_scaled", 2 * b.n + t - 1, 2 * NB)
                    act.activation(gl[t][:], hb[t][:], ACT.Gelu).then_inc(e["gelu"], 1)
                for t in range(T):
                    w("gelu", 2 * b.n + t + 1, 2 * NB), w("squares", 2 * b.n + t, 2 * NB)
                    w("x_scaled", b.n + 1)
                    act.activation(sq[:], gl[t][:], ACT.Square, accum_out=ssum[:, t:t + 1]).then_inc(e["squares"], 1)

            def turn_x(b):
                w("x_scaled", b.n + 1), w("xq_t", b.n)
                act.activation(xq[:], xr[:], ACT.Copy, bias=-MAGIC).then_inc(e["x_round"], 1)
                w("xq_t", b.n + 1), w("h_mm", 2 * b.n, 2 * NB)
                act.activation(xqT[:], pt_x[:], ACT.Copy).then_inc(e["xqT_cp"], 1)

            def turn_h(b):
                for t in range(T):
                    w("hq_t", 2 * b.n + t + 1, 2 * NB), w("o_mm", b.n)
                    act.activation(hqT[t][:], pt_h[:], ACT.Copy).then_inc(e["hqT_cp"], 1)

            def iteration(i):
                if there(i):
                    activate(i)
                if there(i.off(1)):
                    turn_x(i.off(1))
                if there(i):
                    turn_h(i)
            run(iteration, act)

        @block.gpsimd
        def _(pool):
            def w(s, count, most=NB):
                done(pool, e[s], count, most, e["tick_pool3"])

            def iteration(i):
                a = i.off(1)
                if there(a):
                    w("x3_res", a.n + 1), w("x4_res", a.n - 1)
                    for t in range(T):
                        last = pool.tensor_tensor(x3b[a.p][:, t, :], x3[:, t, :], b2[:], ALU.add)
                    last.then_inc(e["x3_bias"], 1)
                if there(i):
                    for t in range(T):
                        w("h_scaled", 2 * i.n + t + 1, 2 * NB), w("hq_t", 2 * i.n + t - 1, 2 * NB)
                        pool.tensor_scalar(hq[t][:], hr_[t][:], -MAGIC, 1.0, ALU.add, ALU.mult).then_inc(e["h_round"], 1)
            run(iteration, pool)

        @block.vector
        def _(v):
            ch = Chain(v, e["chain3"])

            def w(s, count, most=NB):
                done(v, e[s] if isinstance(s, str) else s, count, most)

            def path_mask(b):
                w("masked", b.n)
                for t in range(T):
                    ch.tick(v.tensor_scalar(before_[:, t, :], iota[:], vin[:, t, bass.ds(b.n, 1)], None, ALU.is_le))
                ch.hold()
                w("expand", b.n)
                for t in range(T):
                    last = v.scalar_tensor_tensor(mask[:, t, :], iota[:], vout[:, t, bass.ds(b.n, 1)],
                                                  before_[:, t, :], ALU.is_ge, ALU.mult)
                last.then_inc(e["masked"], 1)

            def bias(b):
                for t in range(T):
                    w("h_mm", 2 * b.n + t + 1, 2 * NB), w("gelu", 2 * b.n + t - 1, 2 * NB)
                    v.scalar_tensor_tensor(hb[t][:], ph[t][:], back_[b.p][:, t:t + 1], b1[:], ALU.mult, ALU.add)\
                        .then_inc(e["h_bias"], 1)

            def residual(b):
                w("expand", b.n + 1), w("x3_bias", b.n)
                v.scalar_tensor_tensor(x3[:], pe_x[:], gates[:, 1:2], x2[b.p][:], ALU.mult, ALU.add)\
                    .then_inc(e["x3_res"], 1)

            def centre(b):
                w("x3_res", b.n + 1)
                for t in range(T):
                    ch.tick(v.bn_stats(st[:, t, :], x3[:, t, :]))
                ch.hold()
                ch.tick_event()
                for t in range(T):
                    ch.tick(v.bn_aggr(mv[:, t, :], st[:, t, :]))
                ch.hold()
                for t in range(T):
                    ch.tick(v.tensor_scalar(xc[:, t, :], x3[:, t, :], mv[:, t, 0:1], None, ALU.subtract))
                ch.tick(v.tensor_scalar(var[:, 0:T], mv[:, :, 1], 1.0 + EPS, EPS * EPS, ALU.mult, ALU.add))
                ch.hold()
                ch.tick(v.tensor_reduce(amax[:, 0:T], xc[:], AX.X, ALU.max, apply_absolute_value=True))

            def maxima(b):
                for t in range(T):
                    w("gelu", 2 * b.n + t + 1, 2 * NB)
                    ch.tick(v.tensor_reduce(amax[:, T + t:T + t + 1], gl[t][:], AX.X, ALU.max, apply_absolute_value=True))
                w("squares", 2 * (b.n + 1), 2 * NB)
                ch.tick(v.tensor_scalar(var[:, T:2 * T], ssum[:], 1.0 / F, EPS, ALU.mult, ALU.add))

            def factors(lo, hi, to):
                ch.hold()
                newton_rsqrt(v, ch, var[:, lo:hi], y[:, lo:hi], tmp[:, lo:hi])
                ch.link(v.tensor_tensor(tmp[:, lo:hi], amax[:, lo:hi], y[:, lo:hi], ALU.mult))
                ch.link(v.tensor_scalar(tmp[:, lo:hi], tmp[:, lo:hi], 1e-5, 1.0 / 127, ALU.max, ALU.mult))
                ch.tick(v.reciprocal(q[:, lo:hi], tmp[:, lo:hi]))
                for cols, dst, k in ((slice(0, T), to[0], 0), (slice(T, 2 * T), to[1], 1)):
                    if dst is not None:
                        ch.tick(v.tensor_scalar(dst[:, cols], tmp[:, cols], wscale[:, k:k + 1], None, ALU.mult))
                ch.hold()
                ch.link(v.tensor_tensor(q[:, lo:hi], q[:, lo:hi], y[:, lo:hi], ALU.mult))

            def scale_x(b):
                w("x_round", b.n)
                for t in range(T):
                    last = v.tensor_scalar(xr[:, t, :], xc[:, t, :], q[:, t:t + 1], MAGIC, ALU.mult, ALU.add)
                last.then_inc(e["x_scaled"], 1)

            def scale_h(b):
                for t in range(T):
                    w("h_round", 2 * b.n + t - 1, 2 * NB)
                    v.tensor_scalar(hr_[t][:], gl[t][:], q[:, T + t:T + t + 1], MAGIC, ALU.mult, ALU.add)\
                        .then_inc(e["h_scaled"], 1)

            def output(b):
                w("x3_bias", b.n + 1), w(o_out[b.p], 16 * b.half, 16 * NB), w("o_mm", b.n + 1)
                for t in range(T):
                    last = v.scalar_tensor_tensor(xo[b.p][:, t, :], po[:, t, :], back_[b.p][:, T + t:T + t + 1],
                                                  x3b[b.p][:, t, :], ALU.mult, ALU.add)
                last.then_inc(e["x4_res"], 1)

            def iteration(i):
                a, z = i.off(1), i.off(-1)
                if there(a):
                    residual(a)
                if there(i):
                    bias(i)
                if there(a):
                    centre(a)
                if there(i):
                    maxima(i)
                lo, hi = (0 if there(a) else T), (2 * T if there(i) else T)
                if lo < hi:
                    factors(lo, hi, (back_[a.p] if there(a) else None, back_[i.p] if there(i) else None))
                if there(a):
                    scale_x(a)
                if there(i):
                    scale_h(i)
                if there(z):
                    output(z)
                if there(i.off(3)):
                    path_mask(i.off(3))
            path_mask(Batch(0, 0))
            run(iteration, v, ch)


def setup_last_weights(nc, io, o):
    with ExitStack() as ctx:
        def sb(name, shape, dt=F32):
            return ctx.enter_context(nc.sbuf_tensor(name, shape, dt))

        def sem(name):
            return ctx.enter_context(nc.semaphore(name))

        w1, w2 = sb("w1", [P, FT, D]), sb("w2", [P, C, F])
        w1b, w2b = sb("w1b", [P, FT, D], BF16), sb("w2b", [P, C, F], BF16)
        gin, ones = sb("gin3", [P, 4]), sb("ones3", [P, P])
        part, scl, rsc = sb("part", [P, 2]), sb("scl3", [P, 2]), sb("rsc3", [P, 2])
        ps = [ctx.enter_context(nc.psum_tensor(f"sl{r}", [P, P], BF16)) for r in range(2)]
        tot = ctx.enter_context(nc.psum_tensor("tot", [P, 512], F32))
        loaded, consts, summed, totals, quant, turned, copied, tanhd, vch, pch = (sem(n) for n in (
            "l_loaded", "l_consts", "l_summed", "l_totals", "l_quant", "l_turned", "l_copied", "l_tanh", "l_chain",
            "l_pchain"))
        block = ctx.enter_context(nc.Block())

        @block.sync
        def _(sp):
            sp.dma_start(w1[:], io["L1_ffn_w1"].rearrange("(a p) d -> p a d", p=P)).then_inc(loaded, 16)
            sp.dma_start(w2[:], io["L1_ffn_w2"].rearrange("(a p) f -> p a f", p=P)).then_inc(loaded, 16)
            sp.dma_start(o["b1"][:], io["L1_ffn_b1"].partition_broadcast(P)).then_inc(loaded, 16)
            sp.dma_start(o["b2"][:], io["L1_ffn_b2"].partition_broadcast(P)).then_inc(loaded, 16)
            sp.dma_start(gin[:, 0:2], io["g_xattn"].partition_broadcast(P)).then_inc(loaded, 16)
            sp.dma_start(gin[:, 2:4], io["g_ffn"].partition_broadcast(P)).then_inc(loaded, 16)
            sp.wait_ge(loaded, 96)

        @block.gpsimd
        def _(pool):
            pc = Chain(pool, pch)
            pc.link(pool.memset(ones[:], 1.0))
            pc.link(pool.memset(o["identb"][:], 0.0))
            pc.link(pool.affine_select(out=o["identb"][:], in_=o["identb"][:], compare_op=ALU.not_equal, fill=1.0,
                                       base=0, pattern=[[-1, P]], channel_multiplier=1))
            pc.link(pool.iota(o["iota"][:], pattern=[[1, S]], base=0, channel_multiplier=0,
                              allow_small_or_imprecise_dtypes=True))
            pool.sem_inc(consts, 1)

        @block.scalar
        def _(act):
            act.wait_ge(loaded, 96)
            act.activation(o["gates"][:], gin[:], ACT.Tanh).then_inc(tanhd, 1)
            act.wait_ge(tanhd, 1)

        jobs = [(w1b[:, f, c * P:c * P + P], o["w1T"][:, c, f * P:f * P + P]) for f in range(FT) for c in range(C)]
        jobs += [(w2b[:, a, f * P:f * P + P], o["w2T"][:, f, a * P:a * P + P]) for a in range(C) for f in range(FT)]

        @block.vector
        def _(v):
            ch = Chain(v, vch)
            v.wait_ge(loaded, 96)
            ch.tick(v.tensor_reduce(part[:, 0:1], w1[:], AX.XY, ALU.add, apply_absolute_value=True))
            ch.link(v.tensor_reduce(part[:, 1:2], w2[:], AX.XY, ALU.add, apply_absolute_value=True))
            v.sem_inc(summed, 1)
            v.wait_ge(totals, 1)
            ch.link(v.tensor_scalar(scl[:], tot[:, 0:2], 1.0 / (D * F), 1e-5, ALU.mult, ALU.max))
            ch.link(v.reciprocal(rsc[:], scl[:]))
            for k, (w_, b_) in enumerate(((w1, w1b), (w2, w2b))):
                ch.link(v.tensor_scalar(w_[:], w_[:], rsc[:, k:k + 1], MAGIC, ALU.mult, ALU.add))
                ch.link(v.tensor_scalar(w_[:], w_[:], MAGIC, 1.0, ALU.subtract, ALU.min))
                ch.link(v.tensor_scalar(b_[:], w_[:], -1.0, None, ALU.max))
            v.sem_inc(quant, 1)
            v.wait_ge(tanhd, 1)
            ch.link(v.tensor_copy(o["wscale"][:, 0:1], scl[:, 0:1]))
            ch.link(v.tensor_tensor(o["wscale"][:, 1:2], scl[:, 1:2], o["gates"][:, 3:4], ALU.mult))
            ch.link(v.tensor_scalar(o["b2"][:], o["b2"][:], o["gates"][:, 3:4], None, ALU.mult))
            for k, (_, dst) in enumerate(jobs):
                v.wait_ge(turned, k + 1)
                v.tensor_copy(dst, ps[k % 2][:]).then_inc(copied, 1)
            v.wait_ge(copied, len(jobs))

        @block.tensor
        def _(pe):
            pe.wait_ge(consts, 1)
            pe.wait_ge(summed, 1)
            pe.matmul(tot[:, 0:2], ones[:], part[:], start=True, stop=True).then_inc(totals, 1)
            pe.wait_ge(quant, 1)
            for k, (src, _) in enumerate(jobs):
                if k >= 2:
                    pe.wait_ge(copied, k - 1)
                pe.transpose(ps[k % 2][:], src, o["identb"][:]).then_inc(turned, 1)


def build(nc, io, out):
    scr = {
        "q": nc.dram_tensor("q_parts_dram", (3, D, S), BF16).ap(),
        "k": nc.dram_tensor("k_parts_dram", (3, D, S), BF16).ap(),
        "x2": nc.dram_tensor("x2_dram", (NB, S, D), F32).ap(),
        "d": nc.dram_tensor("dist_dram", (S, NB, S), F32).ap(),
        "r": nc.dram_tensor("cost_dram", (NB, S + 1, S + 1), F32).ap(),
        "g": nc.dram_tensor("step_dram", (S, NB, S), F32).ap(),
    }
    attention_phase(nc, io, scr)
    with nc.sbuf_tensor("vin", [P, T, NB], F32) as vin, nc.sbuf_tensor("vout", [P, T, NB], F32) as vout:
        alignment_phase(nc, io, scr)
        path_phase(nc, io, scr, vin, vout)
        last_layer_phase(nc, io, scr, vin, vout, out)


_INS = ['x', 'ctx_1024', 'g_xattn', 'g_ffn', 'L0_xattn_wq', 'L0_xattn_wk', 'L0_xattn_wv', 'L0_xattn_wo',
        'L0_ffn_fast_b', 'L0_ffn_w_fc', 'L0_ffn_w_proj', 'L0_ffn_u', 'L0_ffn_v', 'L0_ffn_gate',
        'L1_ffn_w1', 'L1_ffn_b1', 'L1_ffn_w2', 'L1_ffn_b2']


def kernel(**inputs):
    import numpy as _np
    import concourse.bacc as _bacc
    from concourse import mybir as _mybir
    from concourse.bass_utils import run_bass_kernel_spmd as _run

    nc = _bacc.Bacc("TRN2", target_bir_lowering=False, num_devices=1)
    arrays, io = {}, {}
    for name in _INS:
        a = _np.ascontiguousarray(inputs[name])
        if name == 'L0_ffn_gate':
            a = a.reshape(1)
        arrays[f"in_{name}_dram"] = a
        io[name] = nc.dram_tensor(f"in_{name}_dram", a.shape, _mybir.dt.from_np(a.dtype), kind="ExternalInput").ap()
    out = nc.dram_tensor("out_0_dram", (NB, S, D), F32, kind="ExternalOutput").ap()
    build(nc, io, out)
    r = _run(nc, [arrays], core_ids=[0])
    return r.results[0]["out_0_dram"]
```
